# Optimizing a Trainium2 kernel written in Bass

```python
import numpy as np
import jax
import jax.numpy as jnp

def _softmax(x, axis=-1):
    return jax.nn.softmax(x, axis=axis)

def _gelu(x):
    return jax.nn.gelu(x, approximate=True)

def _silu(x):
    return jax.nn.silu(x)

def _sigmoid(x):
    return jax.nn.sigmoid(x)

def _layernorm(x, axis=-1, eps=1e-05):
    m = jnp.mean(x, axis=axis, keepdims=True)
    v = jnp.var(x, axis=axis, keepdims=True)
    return (x - m) / jnp.sqrt(v + eps)

def _scatter_add(tgt, idx, src, axis=0):
    return tgt.at[idx].add(src)

def _segment_sum(src, seg, n):
    return jax.ops.segment_sum(src, seg, n)
kernel_name = 'mk_flamingo_gated_d4_seqx_r4_0806eb'

def setup_inputs(seed: int=0):
    np.random.seed(seed)
    _w = jnp.asarray

    def _rec_inputs():
        import jax
        import jax.numpy as jnp
        _rk = jax.random.key(seed)
        x = 7.22e-05 + 1 * jax.random.normal(jax.random.fold_in(_rk, 1), (16, 112, 256), jnp.float32)
        _lenS = 112 - jax.random.randint(jax.random.fold_in(_rk, 7), (16,), 0, max(1, 112 // 4) + 1, jnp.int32)
        _lenS2 = 375 - jax.random.randint(jax.random.fold_in(_rk, 8), (16,), 0, max(1, 375 // 4) + 1, jnp.int32)
        _ctx_1024P = jax.random.normal(jax.random.fold_in(_rk, 11), (16, 16, 256), jnp.float32)
        _ctx_1024c = jax.random.dirichlet(jax.random.fold_in(_rk, 511), 0.3 * jnp.ones((16,), jnp.float32), (16, 375))
        _ctx_1024t = jnp.einsum('bsk,bkd->bsd', _ctx_1024c, _ctx_1024P)
        _ctx_1024t = _ctx_1024t * jax.lax.rsqrt(jnp.mean(jnp.square(_ctx_1024t)) + 1e-12) * 0.953939
        ctx_1024 = 0.00191187 + 0.999416 * (_ctx_1024t + 0.3 * jax.random.normal(jax.random.fold_in(_rk, 611), (16, 375, 256), jnp.float32))
        _validS = jnp.arange(112)[None, :] < _lenS[:, None]
        _validS2 = jnp.arange(375)[None, :] < _lenS2[:, None]
        _causal = jnp.tril(jnp.ones((112, 112), dtype=bool))
        mask_BxS2_bf1 = jnp.ones((16, 375), dtype=bool)
        mask_1x1xSxS2_ik1 = jnp.where(jnp.broadcast_to(_validS2[0:1, None, None, :], (1, 1, 112, 375)), 1, 0).astype(jnp.int32)
        _g = jax.random.normal(jax.random.fold_in(_rk, 9001), (2, 4), jnp.float32)
        _g = jnp.sign(_g) * jnp.maximum(jnp.abs(_g), 1.0) + (_g == 0) * 1.0
        g_xattn = _g[0]
        g_ffn = _g[1]
        return (x, ctx_1024, mask_BxS2_bf1, mask_1x1xSxS2_ik1, g_xattn, g_ffn)
    x, ctx_1024, mask_BxS2_bf1, mask_1x1xSxS2_ik1, g_xattn, g_ffn = _rec_inputs()

    def _L0_xattn_setup():
        import jax, jax.numpy as jnp
        import numpy as np
        D_MODEL = 256
        NUM_HEADS = 8
        GRID_SIZE = 5
        SPLINE_ORDER = 3
        LN_EPS = 1e-05

        def _grid():
            h = 2.0 / GRID_SIZE
            g = jnp.arange(-SPLINE_ORDER, GRID_SIZE + SPLINE_ORDER + 1, dtype=jnp.float32) * h - 1.0
            return jnp.broadcast_to(g, (D_MODEL, g.shape[0]))

        def _b_splines(x, grid):
            x = x[..., None]
            bases = ((x >= grid[:, :-1]) & (x < grid[:, 1:])).astype(x.dtype)
            for k in range(1, SPLINE_ORDER + 1):
                bases = (x - grid[:, :-(k + 1)]) / (grid[:, k:-1] - grid[:, :-(k + 1)]) * bases[..., :-1] + (grid[:, k + 1:] - x) / (grid[:, k + 1:] - grid[:, 1:-k]) * bases[..., 1:]
            return bases

        def _kan_linear(x, base_w, spline_w, spline_scaler, grid):
            shape = x.shape
            x2 = x.reshape(-1, D_MODEL)
            base = jax.nn.silu(x2) @ base_w.T
            scaled_sw = spline_w * spline_scaler[..., None]
            splines = _b_splines(x2, grid).reshape(x2.shape[0], -1)
            spl = splines @ scaled_sw.reshape(D_MODEL, -1).T
            return (base + spl).reshape(*shape[:-1], D_MODEL)

        def _layernorm(x, g, b):
            mu = jnp.mean(x, axis=-1, keepdims=True)
            var = jnp.mean(jnp.square(x - mu), axis=-1, keepdims=True)
            return (x - mu) * jax.lax.rsqrt(var + LN_EPS) * g + b
        key = jax.random.key(seed)
        ks = jax.random.split(key, 8)
        d = D_MODEL
        s = 0.02
        return {'visual_tokens': jax.random.normal(ks[0], (8, 256, d), jnp.float32), 'top_k_report_tokens': jax.random.normal(ks[1], (8, 32, d), jnp.float32), 'wq': jax.random.normal(ks[2], (d, d), jnp.float32) * s, 'bq': jnp.zeros((d,), jnp.float32), 'wk': jax.random.normal(ks[3], (d, d), jnp.float32) * s, 'bk': jnp.zeros((d,), jnp.float32), 'wv': jax.random.normal(ks[4], (d, d), jnp.float32) * s, 'bv': jnp.zeros((d,), jnp.float32), 'ln_g': jnp.ones((d,), jnp.float32), 'ln_b': jnp.zeros((d,), jnp.float32), 'kan_base_w': jax.random.normal(ks[5], (d, d), jnp.float32) * s, 'kan_spline_w': jax.random.normal(ks[6], (d, d, GRID_SIZE + SPLINE_ORDER), jnp.float32) * s, 'kan_spline_scaler': jax.random.normal(ks[7], (d, d), jnp.float32) * s + 1.0}
    _L0_xattn_all = _L0_xattn_setup()
    _L0_xattn_in = {k: v for k, v in _L0_xattn_all.items() if k in ('wq', 'bq', 'wk', 'bk', 'wv', 'bv', 'ln_g', 'ln_b', 'kan_base_w', 'kan_spline_w', 'kan_spline_scaler')}
    del _L0_xattn_all

    def _L0_ffn_setup():
        import jax, jax.numpy as jnp
        import numpy as np
        D_MODEL = 256
        DEPTH = 8
        M = 2 ** DEPTH
        N_INTERNAL = M - 1
        B, T = (8, 1024)

        def _leaf_probs(gate):
            BT = gate.shape[0]
            lp = jnp.ones((BT, M), dtype=gate.dtype)
            for level in range(DEPTH):
                n = 2 ** level
                half = M // (2 * n)
                g = gate[:, n - 1:2 * n - 1]
                f = jnp.stack([1.0 - g, g], axis=-1)
                f = jnp.broadcast_to(f[..., None], (BT, n, 2, half))
                lp = lp * f.reshape(BT, M)
            return lp
        key = jax.random.key(seed)
        ks = jax.random.split(key, 7)
        x = jax.random.normal(ks[0], (B, T, D_MODEL), dtype=jnp.float32)
        Wq = jax.random.normal(ks[1], (D_MODEL, D_MODEL), dtype=jnp.float32) * 0.02
        routers = jax.random.normal(ks[2], (N_INTERNAL, D_MODEL), dtype=jnp.float32) * 0.02
        leaf_keys = jax.random.normal(ks[3], (M, D_MODEL), dtype=jnp.float32) * 0.02
        leaf_values = jax.random.normal(ks[4], (M, D_MODEL), dtype=jnp.float32) * 0.02
        Wout_w = jax.random.normal(ks[5], (D_MODEL, D_MODEL), dtype=jnp.float32) * 0.02
        Wout_b = jax.random.normal(ks[6], (D_MODEL,), dtype=jnp.float32) * 0.02
        return {'x': x, 'Wq': Wq, 'routers': routers, 'leaf_keys': leaf_keys, 'leaf_values': leaf_values, 'Wout_w': Wout_w, 'Wout_b': Wout_b}
    _L0_ffn_all = _L0_ffn_setup()
    _L0_ffn_in = {k: v for k, v in _L0_ffn_all.items() if k in ('Wq', 'routers', 'leaf_keys', 'leaf_values', 'Wout_w', 'Wout_b')}
    del _L0_ffn_all

    def _L1_xattn_setup():
        import jax, jax.numpy as jnp
        import numpy as np
        HEADS = 16
        DIM_HEAD = 64
        SCALE = DIM_HEAD ** (-0.5)
        key = jax.random.key(seed)
        ks = jax.random.split(key, 6)
        B, Nq, Nkv, D = (4, 512, 256, 256)
        inner = HEADS * DIM_HEAD
        return {'x': jax.random.normal(ks[0], (B, Nq, D), dtype=jnp.float32), 'context': jax.random.normal(ks[1], (B, Nkv, D), dtype=jnp.float32), 'mask': jnp.ones((B, Nkv), dtype=bool), 'Wq': jax.random.normal(ks[2], (inner, D), dtype=jnp.float32) * D ** (-0.5), 'Wkv': jax.random.normal(ks[3], (2 * inner, D), dtype=jnp.float32) * D ** (-0.5), 'Wout': jax.random.normal(ks[4], (D, inner), dtype=jnp.float32) * inner ** (-0.5), 'b_out': jnp.zeros((D,), dtype=jnp.float32)}
    _L1_xattn_all = _L1_xattn_setup()
    _L1_xattn_in = {k: v for k, v in _L1_xattn_all.items() if k in ('Wq', 'Wkv', 'Wout', 'b_out')}
    del _L1_xattn_all

    def _L1_ffn_setup():
        import jax, jax.numpy as jnp
        import numpy as np
        D_MODEL = 256
        D_FF = 1024
        N_EXPERTS = 8
        D_EXPERT = D_FF // N_EXPERTS
        TOP_K = 2
        LB_WEIGHT = 0.01
        B, S = (4, 512)

        def _top_k_softmax(logits, k):
            vals, _ = jax.lax.top_k(logits, k)
            thresh = vals[..., -1:]
            masked = jnp.where(logits >= thresh, logits, -jnp.inf)
            return jax.nn.softmax(masked, axis=-1)
        key = jax.random.key(seed)
        ks = jax.random.split(key, 8)
        x = jax.random.normal(ks[0], (B, S, D_MODEL), dtype=jnp.float32)
        w1 = jax.random.normal(ks[1], (N_EXPERTS, D_MODEL, D_EXPERT), dtype=jnp.float32) * (1.0 / np.sqrt(D_MODEL))
        b1 = jnp.zeros((N_EXPERTS, D_EXPERT), dtype=jnp.float32)
        w2 = jax.random.normal(ks[2], (N_EXPERTS, D_EXPERT, D_MODEL), dtype=jnp.float32) * (1.0 / np.sqrt(D_EXPERT))
        b2 = jnp.zeros((N_EXPERTS, D_MODEL), dtype=jnp.float32)
        centroids = jax.random.normal(ks[3], (N_EXPERTS, D_MODEL), dtype=jnp.float32) * 0.02
        w_route = jax.random.normal(ks[4], (N_EXPERTS, D_MODEL), dtype=jnp.float32) * (1.0 / np.sqrt(D_MODEL))
        return {'x': x, 'w1': w1, 'b1': b1, 'w2': w2, 'b2': b2, 'centroids': centroids, 'w_route': w_route}
    _L1_ffn_all = _L1_ffn_setup()
    _L1_ffn_in = {k: v for k, v in _L1_ffn_all.items() if k in ('w1', 'b1', 'w2', 'b2', 'centroids', 'w_route')}
    del _L1_ffn_all

    def _L2_xattn_setup():
        import jax, jax.numpy as jnp
        import numpy as np
        D_MODEL = 256
        NUM_HEADS = 16
        HEAD_DIM = D_MODEL // NUM_HEADS
        SEQ = 1024
        BATCH = 1
        ROPE_BASE = 10000.0

        def _rope_cos_sin(seq_len, head_dim, dtype):
            inv_freq = 1.0 / ROPE_BASE ** (jnp.arange(0, head_dim, 2, dtype=jnp.float32) / head_dim)
            pos = jnp.arange(seq_len, dtype=jnp.float32)
            freqs = pos[:, None] * inv_freq[None, :]
            emb = jnp.concatenate([freqs, freqs], axis=-1)
            return (jnp.cos(emb).astype(dtype), jnp.sin(emb).astype(dtype))

        def _rotate_half(x):
            d = x.shape[-1] // 2
            return jnp.concatenate([-x[..., d:], x[..., :d]], axis=-1)
        key = jax.random.key(seed)
        ks = jax.random.split(key, 11)
        s = 1.0 / np.sqrt(D_MODEL)
        return {'query': jax.random.normal(ks[0], (BATCH, SEQ, D_MODEL), jnp.float32), 'key': jax.random.normal(ks[1], (BATCH, SEQ, D_MODEL), jnp.float32), 'value': jax.random.normal(ks[2], (BATCH, SEQ, D_MODEL), jnp.float32), 'Wq': jax.random.normal(ks[3], (D_MODEL, D_MODEL), jnp.float32) * s, 'bq': jnp.zeros((D_MODEL,), jnp.float32), 'Wk': jax.random.normal(ks[4], (D_MODEL, D_MODEL), jnp.float32) * s, 'bk': jnp.zeros((D_MODEL,), jnp.float32), 'Wv': jax.random.normal(ks[5], (D_MODEL, D_MODEL), jnp.float32) * s, 'bv': jnp.zeros((D_MODEL,), jnp.float32), 'Wo': jax.random.normal(ks[6], (D_MODEL, D_MODEL), jnp.float32) * s, 'bo': jnp.zeros((D_MODEL,), jnp.float32)}
    _L2_xattn_all = _L2_xattn_setup()
    _L2_xattn_in = {k: v for k, v in _L2_xattn_all.items() if k in ('Wq', 'bq', 'Wk', 'bk', 'Wv', 'bv', 'Wo', 'bo')}
    del _L2_xattn_all

    def _L2_ffn_setup():
        import jax, jax.numpy as jnp
        import numpy as np
        E = 8
        K = 2
        key = jax.random.key(seed)
        ks = jax.random.split(key, 6)
        B, S, D, F = (4, 512, 256, 1024)
        s_d = 1.0 / np.sqrt(D).astype(np.float32)
        s_f = 1.0 / np.sqrt(F).astype(np.float32)
        return {'x': jax.random.normal(ks[0], (B, S, D), jnp.float32), 'ln_w': jnp.ones((D,), jnp.float32), 'Wg': jax.random.normal(ks[1], (D, E), jnp.float32) * s_d, 'bg': jnp.zeros((E,), jnp.float32), 'W1a': jax.random.normal(ks[2], (E, D, F), jnp.float32) * s_d, 'b1a': jnp.zeros((E, F), jnp.float32), 'W1b': jax.random.normal(ks[3], (E, D, F), jnp.float32) * s_d, 'b1b': jnp.zeros((E, F), jnp.float32), 'W2': jax.random.normal(ks[4], (E, F, D), jnp.float32) * s_f, 'b2': jnp.zeros((E, D), jnp.float32)}
    _L2_ffn_all = _L2_ffn_setup()
    _L2_ffn_in = {k: v for k, v in _L2_ffn_all.items() if k in ('ln_w', 'Wg', 'bg', 'W1a', 'b1a', 'W1b', 'b1b', 'W2', 'b2')}
    del _L2_ffn_all

    def _L3_xattn_setup():
        import jax, jax.numpy as jnp
        import numpy as np
        B, L, D, H = (4, 512, 256, 16)
        HD = D // H

        def _split_heads(x):
            b, l, _ = x.shape
            return x.reshape(b, l, H, HD).transpose(0, 2, 1, 3)
        key = jax.random.key(seed)
        ks = jax.random.split(key, 12)
        s = 1.0 / np.sqrt(D)
        return {'q': jax.random.normal(ks[0], (B, L, D), jnp.float32), 'k': jax.random.normal(ks[1], (B, L, D), jnp.float32), 'v': jax.random.normal(ks[2], (B, L, D), jnp.float32), 'mask': jax.random.randint(ks[3], (1, 1, L, L), 0, 2, jnp.int32), 'Wq': jax.random.normal(ks[4], (D, D), jnp.float32) * s, 'bq': jnp.zeros((D,), jnp.float32), 'Wk': jax.random.normal(ks[5], (D, D), jnp.float32) * s, 'bk': jnp.zeros((D,), jnp.float32), 'Wv': jax.random.normal(ks[6], (D, D), jnp.float32) * s, 'bv': jnp.zeros((D,), jnp.float32), 'Wo': jax.random.normal(ks[7], (D, D), jnp.float32) * s, 'bo': jnp.zeros((D,), jnp.float32)}
    _L3_xattn_all = _L3_xattn_setup()
    _L3_xattn_in = {k: v for k, v in _L3_xattn_all.items() if k in ('Wq', 'bq', 'Wk', 'bk', 'Wv', 'bv', 'Wo', 'bo')}
    del _L3_xattn_all

    def _L3_ffn_setup():
        import jax, jax.numpy as jnp
        import numpy as np
        TOP_K = 2
        ROUTE_SCALE = 1.0
        EPS = 1e-20
        key = jax.random.key(seed)
        ks = jax.random.split(key, 8)
        dim, hid, E, X = (256, 704, 8, 1)
        std = 0.02
        x = jax.random.normal(ks[0], (2, 512, dim), dtype=jnp.float32)
        w1 = jax.random.normal(ks[1], (E, hid, dim), dtype=jnp.float32) * std
        w2 = jax.random.normal(ks[2], (E, dim, hid), dtype=jnp.float32) * std
        w3 = jax.random.normal(ks[3], (E, hid, dim), dtype=jnp.float32) * std
        new_w1 = jax.random.normal(ks[4], (X, hid, dim), dtype=jnp.float32) * std
        new_w2 = jnp.zeros((X, dim, hid), dtype=jnp.float32)
        new_w3 = jax.random.normal(ks[5], (X, hid, dim), dtype=jnp.float32) * std
        gate_weight = jax.random.normal(ks[6], (E, dim), dtype=jnp.float32) * std
        new_gate_weight = jax.random.normal(ks[7], (X, dim), dtype=jnp.float32) * std
        gate_bias = jnp.zeros((X,), dtype=jnp.float32)
        return dict(x=x, w1=w1, w2=w2, w3=w3, new_w1=new_w1, new_w2=new_w2, new_w3=new_w3, gate_weight=gate_weight, new_gate_weight=new_gate_weight, gate_bias=gate_bias)
    _L3_ffn_all = _L3_ffn_setup()
    _L3_ffn_in = {k: v for k, v in _L3_ffn_all.items() if k in ('w1', 'w2', 'w3', 'new_w1', 'new_w2', 'new_w3', 'gate_weight', 'new_gate_weight', 'gate_bias')}
    del _L3_ffn_all
    return {'x': x, 'ctx_1024': ctx_1024, 'mask_BxS2_bf1': mask_BxS2_bf1, 'mask_1x1xSxS2_ik1': mask_1x1xSxS2_ik1, 'g_xattn': g_xattn, 'g_ffn': g_ffn, 'L0_xattn_wq': _L0_xattn_in['wq'], 'L0_xattn_bq': _L0_xattn_in['bq'], 'L0_xattn_wk': _L0_xattn_in['wk'], 'L0_xattn_bk': _L0_xattn_in['bk'], 'L0_xattn_wv': _L0_xattn_in['wv'], 'L0_xattn_bv': _L0_xattn_in['bv'], 'L0_xattn_ln_g': _L0_xattn_in['ln_g'], 'L0_xattn_ln_b': _L0_xattn_in['ln_b'], 'L0_xattn_kan_base_w': _L0_xattn_in['kan_base_w'], 'L0_xattn_kan_spline_w': _L0_xattn_in['kan_spline_w'], 'L0_xattn_kan_spline_scaler': _L0_xattn_in['kan_spline_scaler'], 'L0_ffn_Wq': _L0_ffn_in['Wq'], 'L0_ffn_routers': _L0_ffn_in['routers'], 'L0_ffn_leaf_keys': _L0_ffn_in['leaf_keys'], 'L0_ffn_leaf_values': _L0_ffn_in['leaf_values'], 'L0_ffn_Wout_w': _L0_ffn_in['Wout_w'], 'L0_ffn_Wout_b': _L0_ffn_in['Wout_b'], 'L1_xattn_Wq': _L1_xattn_in['Wq'], 'L1_xattn_Wkv': _L1_xattn_in['Wkv'], 'L1_xattn_Wout': _L1_xattn_in['Wout'], 'L1_xattn_b_out': _L1_xattn_in['b_out'], 'L1_ffn_w1': _L1_ffn_in['w1'], 'L1_ffn_b1': _L1_ffn_in['b1'], 'L1_ffn_w2': _L1_ffn_in['w2'], 'L1_ffn_b2': _L1_ffn_in['b2'], 'L1_ffn_centroids': _L1_ffn_in['centroids'], 'L1_ffn_w_route': _L1_ffn_in['w_route'], 'L2_xattn_Wq': _L2_xattn_in['Wq'], 'L2_xattn_bq': _L2_xattn_in['bq'], 'L2_xattn_Wk': _L2_xattn_in['Wk'], 'L2_xattn_bk': _L2_xattn_in['bk'], 'L2_xattn_Wv': _L2_xattn_in['Wv'], 'L2_xattn_bv': _L2_xattn_in['bv'], 'L2_xattn_Wo': _L2_xattn_in['Wo'], 'L2_xattn_bo': _L2_xattn_in['bo'], 'L2_ffn_ln_w': _L2_ffn_in['ln_w'], 'L2_ffn_Wg': _L2_ffn_in['Wg'], 'L2_ffn_bg': _L2_ffn_in['bg'], 'L2_ffn_W1a': _L2_ffn_in['W1a'], 'L2_ffn_b1a': _L2_ffn_in['b1a'], 'L2_ffn_W1b': _L2_ffn_in['W1b'], 'L2_ffn_b1b': _L2_ffn_in['b1b'], 'L2_ffn_W2': _L2_ffn_in['W2'], 'L2_ffn_b2': _L2_ffn_in['b2'], 'L3_xattn_Wq': _L3_xattn_in['Wq'], 'L3_xattn_bq': _L3_xattn_in['bq'], 'L3_xattn_Wk': _L3_xattn_in['Wk'], 'L3_xattn_bk': _L3_xattn_in['bk'], 'L3_xattn_Wv': _L3_xattn_in['Wv'], 'L3_xattn_bv': _L3_xattn_in['bv'], 'L3_xattn_Wo': _L3_xattn_in['Wo'], 'L3_xattn_bo': _L3_xattn_in['bo'], 'L3_ffn_w1': _L3_ffn_in['w1'], 'L3_ffn_w2': _L3_ffn_in['w2'], 'L3_ffn_w3': _L3_ffn_in['w3'], 'L3_ffn_new_w1': _L3_ffn_in['new_w1'], 'L3_ffn_new_w2': _L3_ffn_in['new_w2'], 'L3_ffn_new_w3': _L3_ffn_in['new_w3'], 'L3_ffn_gate_weight': _L3_ffn_in['gate_weight'], 'L3_ffn_new_gate_weight': _L3_ffn_in['new_gate_weight'], 'L3_ffn_gate_bias': _L3_ffn_in['gate_bias']}

def reference(x, ctx_1024, mask_BxS2_bf1, mask_1x1xSxS2_ik1, g_xattn, g_ffn, L0_xattn_wq, L0_xattn_bq, L0_xattn_wk, L0_xattn_bk, L0_xattn_wv, L0_xattn_bv, L0_xattn_ln_g, L0_xattn_ln_b, L0_xattn_kan_base_w, L0_xattn_kan_spline_w, L0_xattn_kan_spline_scaler, L0_ffn_Wq, L0_ffn_routers, L0_ffn_leaf_keys, L0_ffn_leaf_values, L0_ffn_Wout_w, L0_ffn_Wout_b, L1_xattn_Wq, L1_xattn_Wkv, L1_xattn_Wout, L1_xattn_b_out, L1_ffn_w1, L1_ffn_b1, L1_ffn_w2, L1_ffn_b2, L1_ffn_centroids, L1_ffn_w_route, L2_xattn_Wq, L2_xattn_bq, L2_xattn_Wk, L2_xattn_bk, L2_xattn_Wv, L2_xattn_bv, L2_xattn_Wo, L2_xattn_bo, L2_ffn_ln_w, L2_ffn_Wg, L2_ffn_bg, L2_ffn_W1a, L2_ffn_b1a, L2_ffn_W1b, L2_ffn_b1b, L2_ffn_W2, L2_ffn_b2, L3_xattn_Wq, L3_xattn_bq, L3_xattn_Wk, L3_xattn_bk, L3_xattn_Wv, L3_xattn_bv, L3_xattn_Wo, L3_xattn_bo, L3_ffn_w1, L3_ffn_w2, L3_ffn_w3, L3_ffn_new_w1, L3_ffn_new_w2, L3_ffn_new_w3, L3_ffn_gate_weight, L3_ffn_new_gate_weight, L3_ffn_gate_bias):
    import jax
    import jax.numpy as jnp

    def _L0_xattn_ref(visual_tokens, top_k_report_tokens, wq, bq, wk, bk, wv, bv, ln_g, ln_b, kan_base_w, kan_spline_w, kan_spline_scaler):
        import jax, jax.numpy as jnp
        import numpy as np
        D_MODEL = 256
        NUM_HEADS = 8
        GRID_SIZE = 5
        SPLINE_ORDER = 3
        LN_EPS = 1e-05

        def _grid():
            h = 2.0 / GRID_SIZE
            g = jnp.arange(-SPLINE_ORDER, GRID_SIZE + SPLINE_ORDER + 1, dtype=jnp.float32) * h - 1.0
            return jnp.broadcast_to(g, (D_MODEL, g.shape[0]))

        def _b_splines(x, grid):
            x = x[..., None]
            bases = ((x >= grid[:, :-1]) & (x < grid[:, 1:])).astype(x.dtype)
            for k in range(1, SPLINE_ORDER + 1):
                bases = (x - grid[:, :-(k + 1)]) / (grid[:, k:-1] - grid[:, :-(k + 1)]) * bases[..., :-1] + (grid[:, k + 1:] - x) / (grid[:, k + 1:] - grid[:, 1:-k]) * bases[..., 1:]
            return bases

        def _kan_linear(x, base_w, spline_w, spline_scaler, grid):
            shape = x.shape
            x2 = x.reshape(-1, D_MODEL)
            base = jax.nn.silu(x2) @ base_w.T
            scaled_sw = spline_w * spline_scaler[..., None]
            splines = _b_splines(x2, grid).reshape(x2.shape[0], -1)
            spl = splines @ scaled_sw.reshape(D_MODEL, -1).T
            return (base + spl).reshape(*shape[:-1], D_MODEL)

        def _layernorm(x, g, b):
            mu = jnp.mean(x, axis=-1, keepdims=True)
            var = jnp.mean(jnp.square(x - mu), axis=-1, keepdims=True)
            return (x - mu) * jax.lax.rsqrt(var + LN_EPS) * g + b
        B, Nv, d = visual_tokens.shape
        hd = d // NUM_HEADS
        q = visual_tokens @ wq.T + bq
        res = q
        k = top_k_report_tokens @ wk.T + bk
        v = top_k_report_tokens @ wv.T + bv
        qh = q.reshape(B, Nv, NUM_HEADS, hd).transpose(0, 2, 1, 3)
        kh = k.reshape(B, -1, NUM_HEADS, hd).transpose(0, 2, 1, 3)
        vh = v.reshape(B, -1, NUM_HEADS, hd).transpose(0, 2, 1, 3)
        attn = jax.nn.softmax(jnp.einsum('bhqd,bhkd->bhqk', qh, kh) * d ** (-0.5), axis=-1)
        out = jnp.einsum('bhqk,bhkd->bhqd', attn, vh)
        out = out.transpose(0, 2, 1, 3).reshape(B, Nv, d)
        out = _layernorm(res + out, ln_g, ln_b)
        return _kan_linear(out, kan_base_w, kan_spline_w, kan_spline_scaler, _grid())

    def _L0_ffn_ref(x, Wq, routers, leaf_keys, leaf_values, Wout_w, Wout_b):
        import jax, jax.numpy as jnp
        import numpy as np
        D_MODEL = 256
        DEPTH = 8
        M = 2 ** DEPTH
        N_INTERNAL = M - 1
        B, T = (8, 1024)

        def _leaf_probs(gate):
            BT = gate.shape[0]
            lp = jnp.ones((BT, M), dtype=gate.dtype)
            for level in range(DEPTH):
                n = 2 ** level
                half = M // (2 * n)
                g = gate[:, n - 1:2 * n - 1]
                f = jnp.stack([1.0 - g, g], axis=-1)
                f = jnp.broadcast_to(f[..., None], (BT, n, 2, half))
                lp = lp * f.reshape(BT, M)
            return lp
        Bv, Tv, d = x.shape
        q = jnp.einsum('btd,ed->bte', x, Wq)
        q_flat = q.reshape(Bv * Tv, d)
        gate = jax.nn.sigmoid(q_flat @ routers.T)
        leaf_prob = _leaf_probs(gate)
        ret = (leaf_prob @ leaf_values).reshape(Bv, Tv, d)
        return jnp.einsum('btd,ed->bte', ret, Wout_w) + Wout_b

    def _L1_xattn_ref(x, context, mask, Wq, Wkv, Wout, b_out):
        import jax, jax.numpy as jnp
        import numpy as np
        HEADS = 16
        DIM_HEAD = 64
        SCALE = DIM_HEAD ** (-0.5)
        B, Nq, _ = x.shape
        Nkv = context.shape[1]
        q = x @ Wq.T
        kv = context @ Wkv.T
        k, v = jnp.split(kv, 2, axis=-1)
        q = q.reshape(B, Nq, HEADS, DIM_HEAD).transpose(0, 2, 1, 3)
        k = k.reshape(B, Nkv, HEADS, DIM_HEAD).transpose(0, 2, 1, 3)
        v = v.reshape(B, Nkv, HEADS, DIM_HEAD).transpose(0, 2, 1, 3)
        sim = jnp.einsum('bhid,bhjd->bhij', q, k) * SCALE
        max_neg = -jnp.finfo(sim.dtype).max
        sim = jnp.where(mask[:, None, None, :], sim, max_neg)
        attn = jax.nn.softmax(sim, axis=-1)
        out = jnp.einsum('bhij,bhjd->bhid', attn, v)
        out = out.transpose(0, 2, 1, 3).reshape(B, Nq, HEADS * DIM_HEAD)
        return out @ Wout.T + b_out

    def _L1_ffn_ref(x, w1, b1, w2, b2, centroids, w_route):
        import jax, jax.numpy as jnp
        import numpy as np
        D_MODEL = 256
        D_FF = 1024
        N_EXPERTS = 8
        D_EXPERT = D_FF // N_EXPERTS
        TOP_K = 2
        LB_WEIGHT = 0.01
        B, S = (4, 512)

        def _top_k_softmax(logits, k):
            vals, _ = jax.lax.top_k(logits, k)
            thresh = vals[..., -1:]
            masked = jnp.where(logits >= thresh, logits, -jnp.inf)
            return jax.nn.softmax(masked, axis=-1)
        eps = 1e-12
        x_norm = x / jnp.maximum(jnp.linalg.norm(x, axis=-1, keepdims=True), eps)
        c_norm = centroids / jnp.maximum(jnp.linalg.norm(centroids, axis=-1, keepdims=True), eps)
        cos_scores = jnp.einsum('bsd,ed->bse', x_norm, c_norm)
        route_scores = jnp.einsum('bsd,ed->bse', x, w_route)
        logits = cos_scores + route_scores
        gates = _top_k_softmax(logits, TOP_K)
        h = jax.nn.gelu(jnp.einsum('bsd,edh->bseh', x, w1) + b1, approximate=False)
        expert_out = jnp.einsum('bseh,ehd->bsed', h, w2) + b2
        out = jnp.einsum('bse,bsed->bsd', gates, expert_out)
        return out

    def _L2_xattn_ref(query, key, value, Wq, bq, Wk, bk, Wv, bv, Wo, bo):
        import jax, jax.numpy as jnp
        import numpy as np
        D_MODEL = 256
        NUM_HEADS = 16
        HEAD_DIM = D_MODEL // NUM_HEADS
        SEQ = 1024
        BATCH = 1
        ROPE_BASE = 10000.0

        def _rope_cos_sin(seq_len, head_dim, dtype):
            inv_freq = 1.0 / ROPE_BASE ** (jnp.arange(0, head_dim, 2, dtype=jnp.float32) / head_dim)
            pos = jnp.arange(seq_len, dtype=jnp.float32)
            freqs = pos[:, None] * inv_freq[None, :]
            emb = jnp.concatenate([freqs, freqs], axis=-1)
            return (jnp.cos(emb).astype(dtype), jnp.sin(emb).astype(dtype))

        def _rotate_half(x):
            d = x.shape[-1] // 2
            return jnp.concatenate([-x[..., d:], x[..., :d]], axis=-1)
        B, Sq, _ = query.shape
        Skv = key.shape[1]
        H, Dh = (NUM_HEADS, HEAD_DIM)
        q = (query @ Wq.T + bq).reshape(B, Sq, H, Dh)
        k = (key @ Wk.T + bk).reshape(B, Skv, H, Dh)
        v = (value @ Wv.T + bv).reshape(B, Skv, H, Dh)
        cos, sin = _rope_cos_sin(max(Sq, Skv), Dh, query.dtype)
        cq, sq_ = (cos[None, :Sq, None, :], sin[None, :Sq, None, :])
        ck, sk_ = (cos[None, :Skv, None, :], sin[None, :Skv, None, :])
        q = q * cq + _rotate_half(q) * sq_
        k = k * ck + _rotate_half(k) * sk_
        scale = 1.0 / np.sqrt(Dh)
        scores = jnp.einsum('bqhd,bkhd->bhqk', q, k) * scale
        probs = jax.nn.softmax(scores, axis=-1)
        ctx = jnp.einsum('bhqk,bkhd->bqhd', probs, v).reshape(B, Sq, H * Dh)
        return ctx @ Wo.T + bo

    def _L2_ffn_ref(x, ln_w, Wg, bg, W1a, b1a, W1b, b1b, W2, b2):
        import jax, jax.numpy as jnp
        import numpy as np
        E = 8
        K = 2
        B, S, D = x.shape
        eps = jnp.finfo(x.dtype).eps
        xn = x * jax.lax.rsqrt(jnp.mean(x * x, axis=-1, keepdims=True) + eps) * ln_w
        logits = xn @ Wg + bg
        vals, idx = jax.lax.top_k(logits, K)
        topk_w = jax.nn.softmax(vals, axis=-1)
        we = jnp.sum(jax.nn.one_hot(idx, E, dtype=x.dtype) * topk_w[..., None], axis=-2)
        T = B * S
        xf = xn.reshape(T, D)
        wef = we.reshape(T, E).T

        def step(acc, params):
            W1a_e, b1a_e, W1b_e, b1b_e, W2_e, b2_e, w_e = params
            a = xf @ W1a_e + b1a_e
            b = xf @ W1b_e + b1b_e
            y = jax.nn.silu(a) * b @ W2_e + b2_e
            return (acc + w_e[:, None] * y, None)
        out0 = jnp.zeros_like(xf)
        out, _ = jax.lax.scan(step, out0, (W1a, b1a, W1b, b1b, W2, b2, wef))
        return out.reshape(B, S, D)

    def _L3_xattn_ref(q, k, v, mask, Wq, bq, Wk, bk, Wv, bv, Wo, bo):
        import jax, jax.numpy as jnp
        import numpy as np
        B, L, D, H = (4, 512, 256, 16)
        HD = D // H

        def _split_heads(x):
            b, l, _ = x.shape
            return x.reshape(b, l, H, HD).transpose(0, 2, 1, 3)
        qw = q @ Wq.T + bq
        kw = k @ Wk.T + bk
        vw = v @ Wv.T + bv
        qh, kh, vh = (_split_heads(qw), _split_heads(kw), _split_heads(vw))
        scale = 1.0 / jnp.sqrt(jnp.float32(HD))
        scores = jnp.einsum('bhqd,bhkd->bhqk', qh, kh) * scale
        scores = scores + mask.astype(scores.dtype) * -1000000000000000.0
        weights = jax.nn.softmax(scores, axis=-1)
        attn = jnp.einsum('bhqk,bhkd->bhqd', weights, vh)
        attn = attn.transpose(0, 2, 1, 3).reshape(q.shape[0], q.shape[1], D)
        return attn @ Wo.T + bo

    def _L3_ffn_ref(x, w1, w2, w3, new_w1, new_w2, new_w3, gate_weight, new_gate_weight, gate_bias):
        import jax, jax.numpy as jnp
        import numpy as np
        TOP_K = 2
        ROUTE_SCALE = 1.0
        EPS = 1e-20
        bs, slen, dim = x.shape
        x_flat = x.reshape(-1, dim)
        ew1 = jnp.concatenate([w1, new_w1], axis=0)
        ew2 = jnp.concatenate([w2, new_w2], axis=0)
        ew3 = jnp.concatenate([w3, new_w3], axis=0)
        gate = jnp.concatenate([gate_weight, new_gate_weight], axis=0)
        e_orig = w1.shape[0]
        e_tot = gate.shape[0]
        bias = jnp.concatenate([jnp.zeros((e_orig,), x.dtype), gate_bias])
        scores = jax.nn.sigmoid((x_flat @ gate.T + bias).astype(jnp.float32))
        top_scores, selected = jax.lax.top_k(scores, TOP_K)
        top_scores = top_scores / (jnp.sum(top_scores, axis=-1, keepdims=True) + EPS)
        top_scores = top_scores * ROUTE_SCALE
        onehot = jax.nn.one_hot(selected, e_tot, dtype=jnp.float32)
        cw = jnp.einsum('tk,tke->te', top_scores, onehot)
        out = jnp.zeros_like(x_flat)
        for e in range(e_tot):
            h = jax.nn.silu(x_flat @ ew1[e].T) * (x_flat @ ew3[e].T)
            out = out + cw[:, e:e + 1] * (h @ ew2[e].T)
        return out.reshape(bs, slen, dim)
    x = x + jnp.tanh(g_xattn[0]) * _L0_xattn_ref(_layernorm(x, axis=-1), ctx_1024, L0_xattn_wq, L0_xattn_bq, L0_xattn_wk, L0_xattn_bk, L0_xattn_wv, L0_xattn_bv, L0_xattn_ln_g, L0_xattn_ln_b, L0_xattn_kan_base_w, L0_xattn_kan_spline_w, L0_xattn_kan_spline_scaler)
    x = x + jnp.tanh(g_ffn[0]) * _L0_ffn_ref(_layernorm(x, axis=-1), L0_ffn_Wq, L0_ffn_routers, L0_ffn_leaf_keys, L0_ffn_leaf_values, L0_ffn_Wout_w, L0_ffn_Wout_b)
    x = x + jnp.tanh(g_xattn[1]) * _L1_xattn_ref(_layernorm(x, axis=-1), ctx_1024, mask_BxS2_bf1, L1_xattn_Wq, L1_xattn_Wkv, L1_xattn_Wout, L1_xattn_b_out)
    x = x + jnp.tanh(g_ffn[1]) * _L1_ffn_ref(_layernorm(x, axis=-1), L1_ffn_w1, L1_ffn_b1, L1_ffn_w2, L1_ffn_b2, L1_ffn_centroids, L1_ffn_w_route)
    x = x + jnp.tanh(g_xattn[2]) * _L2_xattn_ref(_layernorm(x, axis=-1), ctx_1024, ctx_1024, L2_xattn_Wq, L2_xattn_bq, L2_xattn_Wk, L2_xattn_bk, L2_xattn_Wv, L2_xattn_bv, L2_xattn_Wo, L2_xattn_bo)
    x = x + jnp.tanh(g_ffn[2]) * _L2_ffn_ref(_layernorm(x, axis=-1), L2_ffn_ln_w, L2_ffn_Wg, L2_ffn_bg, L2_ffn_W1a, L2_ffn_b1a, L2_ffn_W1b, L2_ffn_b1b, L2_ffn_W2, L2_ffn_b2)
    x = x + jnp.tanh(g_xattn[3]) * _L3_xattn_ref(_layernorm(x, axis=-1), ctx_1024, ctx_1024, mask_1x1xSxS2_ik1, L3_xattn_Wq, L3_xattn_bq, L3_xattn_Wk, L3_xattn_bk, L3_xattn_Wv, L3_xattn_bv, L3_xattn_Wo, L3_xattn_bo)
    x = x + jnp.tanh(g_ffn[3]) * _L3_ffn_ref(_layernorm(x, axis=-1), L3_ffn_w1, L3_ffn_w2, L3_ffn_w3, L3_ffn_new_w1, L3_ffn_new_w2, L3_ffn_new_w3, L3_ffn_gate_weight, L3_ffn_new_gate_weight, L3_ffn_gate_bias)
    return x

_drawn_inputs = setup_inputs


def setup_inputs(seed=0):
    import zlib

    import numpy as np

    out = dict(_drawn_inputs(seed))
    spreads = {'L0_xattn_bq': (0.0, 0.1),
     'L0_xattn_bk': (0.0, 0.8),
     'L0_xattn_bv': (0.0, 0.1),
     'L0_xattn_ln_g': (1.0, 0.2),
     'L0_xattn_ln_b': (0.0, 0.1),
     'L1_xattn_b_out': (0.0, 0.1),
     'L1_ffn_b1': (0.0, 0.1),
     'L1_ffn_b2': (0.0, 0.1),
     'L2_xattn_bq': (0.0, 0.288),
     'L2_xattn_bk': (0.0, 0.546),
     'L2_xattn_bv': (0.0, 0.1),
     'L2_xattn_bo': (0.0, 0.1),
     'L2_ffn_ln_w': (1.0, 0.2),
     'L2_ffn_bg': (0.0, 0.1),
     'L2_ffn_b1a': (0.0, 0.304),
     'L2_ffn_b1b': (0.0, 0.313),
     'L2_ffn_b2': (0.0, 0.1),
     'L3_xattn_bq': (0.0, 0.525),
     'L3_xattn_bk': (0.0, 0.8),
     'L3_xattn_bv': (0.0, 0.1),
     'L3_xattn_bo': (0.0, 0.1),
     'L3_ffn_new_w2': (0.0, 0.352)}
    factors = {'L0_xattn_wk': 3.502,
     'L0_xattn_kan_spline_scaler': 4.312,
     'L0_ffn_Wq': 8.0,
     'L0_ffn_routers': 8.0,
     'L0_ffn_leaf_values': 8.0,
     'L0_ffn_Wout_w': 8.0,
     'L3_ffn_w1': 5.034,
     'L3_ffn_w2': 4.912,
     'L3_ffn_w3': 4.889,
     'L3_ffn_gate_weight': 3.602,
     'L3_ffn_new_gate_weight': 3.089}
    for name, (base, spread) in spreads.items():
        noise = np.random.default_rng([zlib.crc32(name.encode()), seed]).standard_normal(out[name].shape)
        drawn = base * np.exp(spread * noise) if base else spread * noise
        out[name] = jnp.asarray(drawn.astype(out[name].dtype))
    for name, factor in factors.items():
        out[name] = (out[name] * factor).astype(out[name].dtype)
    return out
```

```python
from contextlib import ExitStack

import numpy as np

import concourse.bass as bass
from concourse import mybir

F32 = mybir.dt.float32
U8 = mybir.dt.uint8
I32 = mybir.dt.int32
ALU = mybir.AluOpType
ACT = mybir.ActivationFunctionType
AX = mybir.AxisListType

P = 128
B, S, D, SK = 16, 112, 256, 375
DC = D // P
KC = 3
KT = SK // KC
EPS = 1e-5
FLT_MAX = float(np.finfo(np.float32).max)


class Signal:

    def __init__(self, new, name, per):
        self.sem, self.per = new(name), per

    def at(self, b, k=0):
        return b * self.per + (k + 1)


def has(b, lag):
    return not isinstance(b, int) or b - lag >= 0


def more(b):
    return not isinstance(b, int) or b < B - 1


def half(b, par):
    return (b - par) * 8 + 16


def each(eng, body):
    body(0, 0)
    body(1, 1)
    with eng.Fori(1, B // 2 - 1, 1) as j:
        body(j * 2, 0)
        body(j * 2 + 1, 1)
    body(B - 2, 0)
    body(B - 1, 1)


KAN_RES, KAN_VAR, KAN_RESN, KAN_LNT, KAN_DIST, KAN_SILU, KAN_BASES = 0, 3, 4, 6, 8, 11, 14


class Core:

    def __init__(self, nc, dram, stack):
        self.nc, self.dram, self.stack = nc, dram, stack
        sb = lambda n, s: stack.enter_context(nc.sbuf_tensor(n, s, F32))
        self.x_all = sb("x_all", [S, B, D])
        self.ident = sb("ident", [P, P])
        self.ones = sb("ones", [1, P])
        self.minus_half = sb("minus_half", [S, 1])
        self.gates = sb("gates", [S, 8])
        self.spent, self.current = ExitStack(), ExitStack()
        self.spent_sems, self.current_sems = [], []

    def new_signals(self, tag):
        self.spent.close()
        self.spent, self.spent_sems = self.current, self.current_sems
        self.current, self.current_sems = ExitStack(), []

        def new(name):
            sem = self.current.enter_context(self.nc.semaphore(f"{tag}_{name}"))
            self.current_sems.append(sem)
            return sem

        return lambda name, per: Signal(new, name, per)

    def clear_spent(self, pool):
        for sem in self.spent_sems:
            pool.sem_clear(sem)


def sub_names(ctx, nc, stage):
    sb = lambda n, s, d=F32: ctx.enter_context(nc.sbuf_tensor(f"{stage}_{n}", s, d))
    ps = lambda n, s, d=F32: ctx.enter_context(nc.psum_tensor(f"{stage}_{n}", s, d))
    return sb, ps


def attention_stage(core, layer, heads, hd, scale, rope=False, mask=None, kan=False):
    nc, dram = core.nc, core.dram
    x_all, ident, gate, ones = core.x_all, core.ident, core.gates[:, layer:layer + 1], core.ones
    tag = f"a{layer}"
    DQ = heads * hd
    QC = DQ // P
    name = lambda n: f"L{layer}x_{n}"

    k_jobs = [("k", c) for c in range(QC)]
    if rope:
        k_jobs = [(kind, c) for c in range(QC) for kind in ("k", "kr")]
    v_width = min(DQ, 512)
    v_jobs = [("v", t, part) for t in range(KC) for part in range(DQ // v_width)]
    q_jobs = [("q", c) for c in range(0, QC, min(QC, 4))] + ([("qr", 0)] if rope else [])
    if kan:
        q_jobs.append(("qtok", 0))
    qn = min(QC, 4)
    jobs = k_jobs + v_jobs + [("xT", 0)] + q_jobs
    job_slot = {}
    kv = k_jobs + v_jobs
    per_slot = -(-len(kv) // (heads - 4))
    for i, j in enumerate(kv):
        job_slot[j] = 1 + i // per_slot
    job_slot[("xT", 0)] = heads - 3
    for j in q_jobs:
        job_slot[j] = heads - 2
    bank_of = {j: i % 2 for i, j in enumerate(jobs)}
    index_of = {j: sum(bank_of[o] == i % 2 for o in jobs[:i]) for i, j in enumerate(jobs)}
    in_bank = [sum(bank_of[j] == n for j in jobs) for n in range(2)]
    jobs_at = lambda n: [j for j in jobs if job_slot[j] == n]
    on_scalar = lambda j: j[0] == "xT" or (j[0] == "v" and layer != 1) or (j[0] in ("k", "q") and not rope)

    o_groups = max(1, DQ // 512)
    og_heads = heads // o_groups
    og_width = DQ // o_groups
    ot_chunks = og_width // P
    fin_jobs = o_groups + 1

    with ExitStack() as ctx:
        sb, ps = sub_names(ctx, nc, tag)
        sig = core.new_signals(tag)

        wq = sb("wq", [P, DC, DQ])
        wk = sb("wk", [P, DC, DQ])
        wv = sb("wv", [P, DC, DQ])
        weights = [(wq, "wqT"), (wk, "wkT"), (wv, "wvT")]
        if rope:
            wqr, wkr = sb("wqr", [P, DC, DQ]), sb("wkr", [P, DC, DQ])
            weights += [(wqr, "wqrT"), (wkr, "wkrT")]
        small = []
        if layer != 1:
            bq, bk, bv = sb("bq", [P, QC]), sb("bk", [P, QC]), sb("bv", [P, QC])
            small += [(bq, "bq"), (bk, "bk"), (bv, "bv")]
        if rope:
            bqr, bkr = sb("bqr", [P, QC]), sb("bkr", [P, QC])
            cos, sin = sb("cos", [P, SK]), sb("sin", [P, SK])
            small += [(bqr, "bqr"), (bkr, "bkr"), (cos, "cos"), (sin, "sin")]
        if hd == 16:
            halves = sb("halves", [P, 2])
            small += [(halves, "halves")]
        if kan:
            lng, lnb = sb("lng", [P, DC]), sb("lnb", [P, DC])
            base_w = sb("base_w", [P, DC, D])
            spline_w = sb("spline_w", [P, DC, 8, D])
            scaler = sb("scaler", [P, DC, D])
            centers = sb("centers", [P, 8])
            bqrow, bvrow = sb("bqrow", [1, D]), sb("bvrow", [1, D])
            bqs = sb("bqs", [P, QC])
            small += [(lng, "ln_g"), (lnb, "ln_b"), (centers, "centers"), (bqrow, "bqrow"), (bvrow, "bvrow")]
            weights += [(base_w, "base_wT"), (spline_w, "spline_wT"), (scaler, "scalerT")]
        else:
            wo = sb("wo", [P, QC, D])
            borow = sb("borow", [1, D])
            weights += [(wo, "woT")]
            small += [(borow, "bo")]

        ctxT = sb("ctxT", [P, 2, DC, SK])
        stats, mv = sb("stats", [S, 6]), sb("mv", [S, 2])
        rstd = sb("rstd", [S, 1])
        xn = sb("xn", [S, D])
        xT = sb("xT", [P, DC, S])
        qT = sb("qT", [P, 2, 2 if hd == 16 else 1, QC, S])
        kT = sb("kT", [P, 2, QC, SK])
        v = sb("v", [KT, 2, KC, DQ])
        probs = sb("probs", [S, 2, SK])
        pT = sb("pT", [KT, 2, KC, S])
        negmax = sb("negmax", [S, heads])
        rowsum = sb("rowsum", [S, 2, heads])
        rinv = sb("rinv", [S, heads])
        o = sb("o", [S, og_width])
        oT = sb("oT", [P, QC, S])
        if rope:
            rot_a, rot_b = sb("rot_a", [P, 2, SK]), sb("rot_b", [P, 2, SK])
            qrot_a, qrot_b = sb("qrot_a", [P, DC, S]), sb("qrot_b", [P, DC, S])
        if hd == 16:
            qfull = sb("qfull", [P, DC, S])
        if mask:
            masked = sb("masked", [S, 2, SK])
            if mask == "keys":
                mask_in = sb("mask_in", [S, 2, SK], U8)
                mask_add = sb("mask_add", [S, 2, SK])
            else:
                mask_in = sb("mask_in", [S, 1, SK], I32)
                mask_add = sb("mask_add", [S, 1, SK])
        if kan:
            qtok = sb("qtok", [S, 2, D])
            res = sb("res", [S, D])
            stats2, mv2, rstd2 = sb("stats2", [S, 6]), sb("mv2", [S, 2]), sb("rstd2", [S, 1])
            resn = sb("resn", [S, D])
            lnT = sb("lnT", [P, DC, S])
            silu = sb("silu", [P, DC, S])
            sexp = sb("sexp", [P, DC, S])
            dist = sb("dist", [P, DC, 8, S])
            near2, near1 = sb("near2", [P, DC, 8, S]), sb("near1", [P, DC, 8, S])
            sq2, sq1 = sb("sq2", [P, DC, 8, S]), sb("sq1", [P, DC, 8, S])

        sc_ps = ps("sc_ps", [S, 2, 512])
        pT_ps = ps("pT_ps", [P, 2, 512])
        o_ps = ps("o_ps", [S, 512])
        job_ps = ps("job_ps", [P, 2, 512])
        fin_ps = ps("fin_ps", [P, 512])

        s_w = sig("weights_in", 1)
        s_small = sig("small_in", 1)
        s_ctx = [sig(f"ctx_in{i}", 1) for i in range(2)]
        s_job = [sig(f"job{i}_ready", in_bank[i]) for i in range(2)]
        s_jobfree = [sig(f"job{i}_free", in_bank[i]) for i in range(2)]
        s_ln = sig("ln_steps", 3)
        s_pow = sig("rstd_ready", 1)
        s_xn = sig("xn_ready", 1)
        s_scores = sig("scores_ready", heads)
        s_max = sig("max_ready", heads)
        s_probs = sig("probs_ready", heads)
        s_pT = sig("pT_in_psum", heads)
        s_pTc = [sig(f"pT_copied{i}", heads // 2) for i in range(2)]
        s_pv = sig("pv_done", heads)
        s_o = sig("o_normalised", o_groups)
        s_rinv = sig("rinv_ready", o_groups)
        s_fin = sig("fin_ready", fin_jobs)
        s_finfree = sig("fin_free", fin_jobs)
        s_oTc = sig("oT_chunks", QC)
        s_tick = [sig(f"tick{i}", 0) for i in range(3)]
        if rope:
            s_ropek = sig("rope_k_ready", QC)
            s_rope_q = sig("rope_q_parts", 2 * DC)
            s_qsum = sig("q_summed", 1)
        s_qf = sig("q_chunks", QC)
        if hd == 16:
            s_q2 = sig("q_halves_ready", 2)
        if mask:
            s_mask = sig("mask_ready", 1)
            s_maskin = [sig(f"mask_in{i}", 1) for i in range(2)]
        if kan:
            s_setup = sig("setup", 1)
            s_k = sig("kan_dve", KAN_BASES + 1)
            s_ka = sig("kan_act", 6)
            s_pow2 = sig("rstd2_ready", 1)

        def job(j, b):
            return bank_of[j], s_job[bank_of[j]].at(b, index_of[j])

        def q_of(par, n):
            if hd == 16:
                r = 32 * ((n % 8) // 2)
                return qT[r:r + 32, par, n % 2, n // 8, :], r, 32, n // 8
            at = n * hd
            return qT[at % P:at % P + hd, par, 0, at // P, :], at % P, hd, at // P

        with nc.Block() as block:

            @block.sync
            def _(sp):
                for dst, what in small:
                    sp.dma_start(dst[:], dram[name(what)]).then_inc(s_small.sem, 16)
                if mask == "scores":
                    sp.dma_start(mask_in[:, 0, :], dram["mask_scores"]).then_inc(s_maskin[0].sem, 16)
                for dst, what in weights:
                    src = dram[name(what)]
                    sp.dma_start(dst[:], src).then_inc(s_w.sem, 16)

                def load(b, par, known):
                    if known:
                        n, value = job(kv[-1], b - 2)
                        sp.wait_ge(s_job[n].sem, value)
                        sp.sem_inc(s_tick[2].sem, 1)
                    sp.dma_start(ctxT[:, par], dram["ctxT"][b]).then_inc(s_ctx[par].sem, 16)
                    if mask == "keys":
                        if known:
                            sp.wait_ge(s_mask.sem, s_mask.at(b - 2))
                            sp.sem_inc(s_tick[2].sem, 1)
                        sp.dma_start(mask_in[:, par, :], dram["mask_keys"][b].to_broadcast([S, SK])).then_inc(s_maskin[par].sem, 16)

                load(0, 0, False)
                load(1, 1, False)
                with sp.Fori(1, B // 2, 1) as j:
                    load(j * 2, 0, True)
                    load(j * 2 + 1, 1, True)

            def in_ctx(eng, b, par, sem=s_ctx):
                eng.wait_ge(sem[par].sem, half(b, par))

            @block.gpsimd
            def _(pool):
                core.clear_spent(pool)

                def power(b):
                    pool.wait_ge(s_ln.sem, s_ln.at(b, 2))
                    pool.tensor_tensor(rstd[:], rstd[:], core.minus_half[:], ALU.pow).then_inc(s_pow.sem, 1)

                def kan_power(b):
                    pool.wait_ge(s_k.sem, s_k.at(b, KAN_VAR))
                    pool.tensor_tensor(rstd2[:], rstd2[:], core.minus_half[:], ALU.pow).then_inc(s_pow2.sem, 1)

                def body(b, par):
                    if kan and has(b, 1):
                        kan_power(b - 1)
                    if more(b):
                        power(b + 1)
                        if rope:
                            for c in range(QC):
                                rope_add(b + 1, 1 - par, c)

                def rope_add(b, par, c):
                    if has(b, 2):
                        pool.wait_ge(s_pv.sem, s_pv.at(b - 2, heads - 1))
                    for kind in ("k", "kr"):
                        n, value = job((kind, c), b)
                        pool.wait_ge(s_jobfree[n].sem, value)
                    pool.tensor_tensor(kT[:, par, c, :], rot_a[:, c, :], rot_b[:, c, :], ALU.add)\
                        .then_inc(s_ropek.sem, 1)

                power(0)
                if rope:
                    for c in range(QC):
                        rope_add(0, 0, c)
                each(pool, body)
                if kan:
                    kan_power(B - 1)

            @block.tensor
            def _(pe):
                pe.wait_ge(s_w.sem, 16 * len(weights))
                pe.wait_ge(s_small.sem, 16 * len(small))
                if kan:
                    pe.wait_ge(s_setup.sem, 2 + DC)

                def run_job(j, b, par):
                    kind, n = j[0], bank_of[j]
                    value = job(j, b)[1]
                    if has(b, 1) or index_of[j] > 0:
                        pe.wait_ge(s_jobfree[n].sem, value - 1)
                    if j == jobs[0]:
                        in_ctx(pe, b, par)
                    if kind in ("k", "kr"):
                        w = wk if kind == "k" else wkr
                        for c in range(DC):
                            mm = pe.matmul(job_ps[:, n, 0:SK], w[:, c, j[1] * P:(j[1] + 1) * P],
                                           ctxT[:, par, c, :], start=(c == 0), stop=(c == DC - 1))
                    elif kind == "v":
                        _, t, part = j
                        for c in range(DC):
                            mm = pe.matmul(job_ps[0:KT, n, 0:v_width], ctxT[:, par, c, t * KT:(t + 1) * KT],
                                           wv[:, c, part * v_width:(part + 1) * v_width],
                                           start=(c == 0), stop=(c == DC - 1))
                    elif kind == "xT":
                        pe.wait_ge(s_xn.sem, s_xn.at(b))
                        for c in range(DC):
                            mm = pe.transpose(job_ps[:, n, c * S:(c + 1) * S], xn[:, c * P:(c + 1) * P],
                                              ident[0:S, 0:S])
                    elif kind in ("q", "qr"):
                        m, v2 = job(("xT", 0), b)
                        pe.wait_ge(s_jobfree[m].sem, v2)
                        w = wq if kind == "q" else wqr
                        for i in range(qn):
                            f = j[1] + i
                            for c in range(DC):
                                mm = pe.matmul(job_ps[:, n, i * S:(i + 1) * S], w[:, c, f * P:(f + 1) * P],
                                               xT[:, c, :], start=(c == 0), stop=(c == DC - 1))
                    else:
                        for c in range(DC):
                            pe.matmul(job_ps[0:S, n, 0:D], xT[:, c, :], wq[:, c, :], start=(c == 0), stop=False)
                        pe.matmul(job_ps[0:S, n, 0:D], ones[0:1, 0:S], bqrow[:], start=False, stop=False)
                        mm = pe.matmul(job_ps[0:S, n, 0:D], ones[0:1, 0:S], bvrow[:], start=False, stop=True)
                    mm.then_inc(s_job[n].sem, 1)

                def scores(b, par, n):
                    if n == 0:
                        for i in range(2):
                            pe.wait_ge(s_jobfree[i].sem, s_jobfree[i].at(b, in_bank[i] - 1))
                        if rope:
                            pe.wait_ge(s_ropek.sem, s_ropek.at(b, QC - 1))
                        if hd == 16:
                            pe.wait_ge(s_q2.sem, s_q2.at(b, 1))
                    free = s_max if mask else s_probs
                    if has(b, 1) or n >= 2:
                        pe.wait_ge(free.sem, free.at(b, n) - 2)
                    lhs, r, k, c = q_of(par, n)
                    pe.matmul(sc_ps[:, n % 2, 0:SK], lhs, kT[r:r + k, par, c, :], start=True, stop=True)\
                        .then_inc(s_scores.sem, 1)

                def transposes(b, n):
                    pe.wait_ge(s_probs.sem, s_probs.at(b, n))
                    if has(b, 1) or n >= 2:
                        pe.wait_ge(s_pTc[n % 2].sem, s_pTc[n % 2].at(b, n // 2) - 1)
                    for t in range(KC):
                        mm = pe.transpose(pT_ps[0:KT, n % 2, t * S:(t + 1) * S],
                                          probs[:, n % 2, t * KT:(t + 1) * KT], ident[0:S, 0:S])
                    mm.then_inc(s_pT.sem, 1)

                def pv(b, par, n):
                    pe.wait_ge(s_pTc[n % 2].sem, s_pTc[n % 2].at(b, n // 2))
                    if n % og_heads == 0 and (has(b, 1) or n > 0):
                        pe.wait_ge(s_o.sem, s_o.at(b, n // og_heads) - 1)
                    w = (n % og_heads) * hd
                    for t in range(KC):
                        mm = pe.matmul(o_ps[:, w:w + hd], pT[:, n % 2, t, :], v[:, par, t, n * hd:(n + 1) * hd],
                                       start=(t == 0), stop=(t == KC - 1))
                    mm.then_inc(s_pv.sem, 1)

                def turn_o(b, g):
                    pe.wait_ge(s_o.sem, s_o.at(b, g))
                    if has(b, 1) or g > 0:
                        pe.wait_ge(s_finfree.sem, s_finfree.at(b, g) - 1)
                    for c in range(ot_chunks):
                        mm = pe.transpose(fin_ps[:, c * S:(c + 1) * S], (resn if kan else o)[:, c * P:(c + 1) * P],
                                          ident[0:S, 0:S])
                    mm.then_inc(s_fin.sem, 1)

                def output(b):
                    pe.wait_ge(s_finfree.sem, s_finfree.at(b, o_groups - 1))
                    for c in range(QC):
                        pe.matmul(fin_ps[0:S, 0:D], oT[:, c, :], wo[:, c, :], start=(c == 0), stop=False)
                    pe.matmul(fin_ps[0:S, 0:D], ones[0:1, 0:S], borow[:], start=False, stop=True)\
                        .then_inc(s_fin.sem, 1)

                def kan_turn(b):
                    pe.wait_ge(s_k.sem, s_k.at(b, KAN_RESN))
                    if has(b, 1):
                        pe.wait_ge(s_finfree.sem, s_finfree.at(b, 0) - 1)
                    for c in range(DC):
                        mm = pe.transpose(fin_ps[:, c * S:(c + 1) * S], resn[:, c * P:(c + 1) * P], ident[0:S, 0:S])
                    mm.then_inc(s_fin.sem, 1)

                def kan_output(b):
                    pe.wait_ge(s_finfree.sem, s_finfree.at(b, 0))
                    pe.wait_ge(s_k.sem, s_k.at(b, KAN_SILU))
                    for c in range(DC):
                        pe.matmul(fin_ps[0:S, 0:D], silu[:, c, :], base_w[:, c, :], start=(c == 0), stop=False)
                    pe.wait_ge(s_k.sem, s_k.at(b, KAN_BASES))
                    for c in range(DC):
                        for i in range(8):
                            mm = pe.matmul(fin_ps[0:S, 0:D], dist[:, c, i, :], spline_w[:, c, i, :],
                                           start=False, stop=(c == DC - 1 and i == 7))
                    mm.then_inc(s_fin.sem, 1)

                def body(b, par):
                    for n in range(heads):
                        if n + 1 < heads:
                            scores(b, par, n + 1)
                        elif more(b):
                            scores(b + 1, 1 - par, 0)
                        transposes(b, n)
                        if n > 0:
                            pv(b, par, n - 1)
                        elif has(b, 1):
                            pv(b - 1, 1 - par, heads - 1)
                        if has(b, 1):
                            finish(b - 1, n)
                        if o_groups == 2 and n == og_heads + 2:
                            turn_o(b, 0)
                        if more(b):
                            for j in jobs_at(n):
                                run_job(j, b + 1, 1 - par)

                def finish(b, n):
                    if kan:
                        if n == 3:
                            kan_turn(b)
                        if n == heads - 1:
                            kan_output(b)
                        return
                    if n == 2:
                        turn_o(b, o_groups - 1)
                    if n == 4:
                        output(b)

                for j in jobs:
                    run_job(j, 0, 0)
                scores(0, 0, 0)
                each(pe, body)
                pv(B - 1, 1, heads - 1)
                for n in range(heads):
                    finish(B - 1, n)

            @block.scalar
            def _(act):
                act.wait_ge(s_small.sem, 16 * len(small))

                def copy_job(j, b, par):
                    kind, n = j[0], bank_of[j]
                    if not on_scalar(j):
                        return
                    if kind in ("v", "k", "q") and has(b, 2):
                        act.wait_ge(s_pv.sem, s_pv.at(b - 2, heads - 1))
                    act.wait_ge(s_job[n].sem, job(j, b)[1])
                    free = s_jobfree[n].sem
                    if kind == "k":
                        f = j[1]
                        act.activation(kT[:, par, f, :], job_ps[:, n, 0:SK], ACT.Identity,
                                       bias=bk[:, f:f + 1] if layer != 1 else 0.0).then_inc(free, 1)
                    elif kind == "v":
                        _, t, part = j
                        act.activation(v[:, par, t, part * v_width:(part + 1) * v_width],
                                       job_ps[0:KT, n, 0:v_width], ACT.Copy).then_inc(free, 1)
                    elif kind == "xT":
                        for i in range(2):
                            if has(b, 1):
                                act.wait_ge(s_job[i].sem, s_job[i].at(b - 1, in_bank[i] - 1))
                        act.activation(xT[:, :, :], job_ps[:, n, 0:DC * S].rearrange("p (c s) -> p c s", c=DC),
                                       ACT.Copy).then_inc(free, 1)
                    elif kind == "q" and layer == 1:
                        act.activation(qT[:, par, 0, j[1]:j[1] + qn, :],
                                       job_ps[:, n, 0:qn * S].rearrange("p (c s) -> p c s", c=qn),
                                       ACT.Copy, scale=scale).then_inc(free, 1)
                    elif kind == "q" and hd == 16:
                        if has(b, 1):
                            act.wait_ge(s_q2.sem, s_q2.at(b - 1, 1))
                        for c in range(QC):
                            ins = act.activation(qfull[:, c, :], job_ps[:, n, c * S:(c + 1) * S], ACT.Identity,
                                                 bias=bq[:, c:c + 1])
                            ins.then_inc(s_qf.sem, 1)
                        act.wait_ge(s_qf.sem, s_qf.at(b, QC - 1))
                        act.sem_inc(free, 1)
                    elif kind == "q":
                        for c in range(QC):
                            act.activation(qT[:, par, 0, c, :], job_ps[:, n, c * S:(c + 1) * S], ACT.Identity,
                                           scale=scale, bias=bqs[:, c:c + 1]).then_inc(s_qf.sem, 1)
                        act.wait_ge(s_qf.sem, s_qf.at(b, QC - 1))
                        act.sem_inc(free, 1)

                def exps(b, par, n):
                    act.wait_ge(s_max.sem, s_max.at(b, n))
                    if has(b, 1) or n >= 2:
                        act.wait_ge(s_pT.sem, s_pT.at(b, n) - 2)
                    if n == 0 and has(b, 2):
                        act.wait_ge(s_rinv.sem, s_rinv.at(b - 2, o_groups - 1))
                    src = masked[:, n % 2, :] if mask else sc_ps[:, n % 2, 0:SK]
                    act.activation(probs[:, n % 2, :], src, ACT.Exp, bias=negmax[:, n:n + 1],
                                   scale=-1.0 if mask else 1.0,
                                   accum_out=rowsum[:, par, n:n + 1]).then_inc(s_probs.sem, 1)

                def copy_pT(b, n):
                    act.wait_ge(s_pT.sem, s_pT.at(b, n))
                    if has(b, 1) or n >= 2:
                        act.wait_ge(s_pv.sem, s_pv.at(b, n) - 2)
                    act.activation(pT[:, n % 2, :, :], pT_ps[0:KT, n % 2, 0:KC * S].rearrange("p (c s) -> p c s", c=KC),
                                   ACT.Copy).then_inc(s_pTc[n % 2].sem, 1)

                def copy_oT(b, g):
                    act.wait_ge(s_fin.sem, s_fin.at(b, g))
                    if has(b, 1):
                        act.wait_ge(s_fin.sem, s_fin.at(b - 1, fin_jobs - 1))
                    if layer == 1:
                        act.activation(oT[:, g * ot_chunks:(g + 1) * ot_chunks, :],
                                       fin_ps[:, 0:ot_chunks * S].rearrange("p (c s) -> p c s", c=ot_chunks),
                                       ACT.Copy).then_inc(s_finfree.sem, 1)
                    else:
                        for c in range(ot_chunks):
                            act.activation(oT[:, c, :], fin_ps[:, c * S:(c + 1) * S], ACT.Identity,
                                           bias=bv[:, c:c + 1]).then_inc(s_oTc.sem, 1)
                        act.wait_ge(s_oTc.sem, s_oTc.at(b, ot_chunks - 1))
                        act.sem_inc(s_finfree.sem, 1)

                def kan_step(b, n):
                    flat = lambda t: t[:].rearrange("p c i s -> p (c i s)")
                    if n == 4:
                        act.wait_ge(s_k.sem, s_k.at(b, KAN_LNT))
                        act.activation(sexp[:], lnT[:], ACT.Exp, scale=-1.0).then_inc(s_ka.sem, 1)
                        act.wait_ge(s_k.sem, s_k.at(b, KAN_DIST))
                        act.activation(flat(dist), flat(dist), ACT.Abs).then_inc(s_ka.sem, 1)
                    if n == 5:
                        act.wait_ge(s_ka.sem, s_ka.at(b, 1))
                        act.activation(flat(near2), flat(dist), ACT.Relu, scale=-1.0, bias=2.0).then_inc(s_ka.sem, 1)
                        act.activation(flat(near1), flat(dist), ACT.Relu, scale=-1.0, bias=1.0).then_inc(s_ka.sem, 1)
                    if n == 6:
                        act.wait_ge(s_ka.sem, s_ka.at(b, 2))
                        act.activation(flat(sq2), flat(near2), ACT.Square).then_inc(s_ka.sem, 1)
                        act.wait_ge(s_ka.sem, s_ka.at(b, 3))
                        act.activation(flat(sq1), flat(near1), ACT.Square).then_inc(s_ka.sem, 1)

                def body(b, par):
                    for n in range(heads):
                        if n + 1 < heads:
                            exps(b, par, n + 1)
                        elif more(b):
                            exps(b + 1, 1 - par, 0)
                        if n % 2 == 0:
                            copy_pT(b, n)
                        if has(b, 1):
                            if kan:
                                kan_step(b - 1, n)
                            elif n == 3:
                                copy_oT(b - 1, o_groups - 1)
                        if o_groups == 2 and n == og_heads + 3:
                            copy_oT(b, 0)
                        if more(b):
                            for j in jobs_at(n):
                                copy_job(j, b + 1, 1 - par)

                if kan:
                    act.wait_ge(s_setup.sem, 2 + DC)
                for j in jobs:
                    copy_job(j, 0, 0)
                exps(0, 0, 0)
                each(act, body)
                for n in range(heads):
                    if kan:
                        kan_step(B - 1, n)
                    elif n == 3:
                        copy_oT(B - 1, o_groups - 1)

            @block.vector
            def _(dve):
                dve.wait_ge(s_small.sem, 16 * len(small))

                def hold(sem, value):
                    dve.wait_ge(sem, value)
                    dve.sem_inc(s_tick[1].sem, 1)

                if mask == "scores":
                    dve.wait_ge(s_maskin[0].sem, 16)
                    dve.tensor_scalar(mask_add[:, 0, :], mask_in[:, 0, :], -1e15, None, ALU.mult)\
                        .then_inc(s_mask.sem, 1)
                    dve.wait_ge(s_mask.sem, 1)
                if kan:
                    dve.wait_ge(s_w.sem, 16 * len(weights))
                    dve.tensor_scalar(bqs[:], bq[:], scale, None, ALU.mult).then_inc(s_setup.sem, 1)
                    dve.tensor_scalar(scaler[:], scaler[:], 1.0 / 6.0, None, ALU.mult).then_inc(s_setup.sem, 1)
                    dve.wait_ge(s_setup.sem, 2)
                    for c in range(DC):
                        dve.tensor_tensor(spline_w[:, c], spline_w[:, c],
                                          scaler[:, c, :].unsqueeze(1).to_broadcast([P, 8, D]),
                                          ALU.mult).then_inc(s_setup.sem, 1)

                def norm_stats(b):
                    dve.bn_stats(stats[:], x_all[:, b, :]).then_inc(s_ln.sem, 1)
                    hold(s_ln.sem, s_ln.at(b, 0))
                    dve.bn_aggr(mv[:], stats[:]).then_inc(s_ln.sem, 1)
                    dve.wait_ge(s_ln.sem, s_ln.at(b, 1))
                    dve.tensor_scalar(rstd[:], mv[:, 1:2], EPS, None, ALU.add).then_inc(s_ln.sem, 1)

                def norm_apply(b):
                    dve.wait_ge(s_pow.sem, s_pow.at(b))
                    if has(b, 1):
                        n, value = job(("xT", 0), b - 1)
                        dve.wait_ge(s_job[n].sem, value)
                    dve.tensor_scalar(xn[:], x_all[:, b, :], mv[:, 0:1], rstd[:, 0:1], ALU.subtract, ALU.mult)\
                        .then_inc(s_xn.sem, 1)

                def make_mask(b, par):
                    in_ctx(dve, b, par, s_maskin)
                    if has(b, 2):
                        dve.wait_ge(s_max.sem, s_max.at(b - 2, heads - 1))
                    dve.tensor_scalar(mask_add[:, par, :], mask_in[:, par, :], 1.0, FLT_MAX, ALU.subtract, ALU.mult)\
                        .then_inc(s_mask.sem, 1)

                def copy_job(j, b, par):
                    kind, n = j[0], bank_of[j]
                    if on_scalar(j):
                        return
                    dve.wait_ge(s_job[n].sem, job(j, b)[1])
                    free = s_jobfree[n].sem
                    if kind in ("k", "kr"):
                        f = j[1]
                        if has(b, 1):
                            dve.wait_ge(s_ropek.sem, s_ropek.at(b - 1, f))
                        dst, bias, table = (rot_a, bk, cos) if kind == "k" else (rot_b, bkr, sin)
                        dve.scalar_tensor_tensor(out=dst[:, f, :], in0=job_ps[:, n, 0:SK], scalar=bias[:, f:f + 1],
                                                 in1=table[:], op0=ALU.add, op1=ALU.mult).then_inc(free, 1)
                    elif kind in ("q", "qr"):
                        if has(b, 1):
                            dve.wait_ge(s_qsum.sem, s_qsum.at(b - 1))
                        dst, bias, table = (qrot_a, bq, cos) if kind == "q" else (qrot_b, bqr, sin)
                        for c in range(DC):
                            dve.scalar_tensor_tensor(out=dst[:, c, :], in0=job_ps[:, n, c * S:(c + 1) * S],
                                                     scalar=bias[:, c:c + 1], in1=table[:, 0:S], op0=ALU.add,
                                                     op1=ALU.mult).then_inc(s_rope_q.sem, 1)
                        dve.wait_ge(s_rope_q.sem, s_rope_q.at(b, (kind == "qr") * DC + DC - 1))
                        dve.sem_inc(free, 1)
                    elif kind == "v":
                        if has(b, 2):
                            dve.wait_ge(s_pv.sem, s_pv.at(b - 2, heads - 1))
                        _, t, part = j
                        dve.tensor_copy(v[:, par, t, part * v_width:(part + 1) * v_width],
                                        job_ps[0:KT, n, 0:v_width]).then_inc(free, 1)
                    elif kind == "qtok":
                        if has(b, 2):
                            dve.wait_ge(s_k.sem, s_k.at(b - 2, KAN_RES))
                        dve.tensor_copy(qtok[:, par, :], job_ps[0:S, n, 0:D]).then_inc(free, 1)

                def halve_q(b, par):
                    if rope:
                        dve.wait_ge(s_rope_q.sem, s_rope_q.at(b, 2 * DC - 1))
                        if has(b, 1):
                            dve.wait_ge(s_q2.sem, s_q2.at(b - 1, 1))
                        dve.tensor_tensor(qfull[:], qrot_a[:], qrot_b[:], ALU.add).then_inc(s_qsum.sem, 1)
                        dve.wait_ge(s_qsum.sem, s_qsum.at(b))
                    else:
                        dve.wait_ge(s_qf.sem, s_qf.at(b, QC - 1))
                    if has(b, 2):
                        dve.wait_ge(s_pv.sem, s_pv.at(b - 2, heads - 1))
                    for i in range(2):
                        dve.tensor_scalar(qT[:, par, i], qfull[:], halves[:, i:i + 1], None, ALU.mult)\
                            .then_inc(s_q2.sem, 1)

                def row_max(b, par, n):
                    dve.wait_ge(s_scores.sem, s_scores.at(b, n))
                    if has(b, 1) and not mask:
                        dve.wait_ge(s_probs.sem, s_probs.at(b - 1, n))
                    if mask:
                        if n == 0 and mask == "keys":
                            dve.wait_ge(s_mask.sem, s_mask.at(b))
                        if has(b, 1) or n >= 2:
                            dve.wait_ge(s_probs.sem, s_probs.at(b, n) - 2)
                        dve.sem_inc(s_tick[1].sem, 1)
                        m = mask_add[:, par if mask == "keys" else 0, :]
                        dve.tensor_tensor_reduce(out=masked[:, n % 2, :], in0=sc_ps[:, n % 2, 0:SK], in1=m,
                                                 scale=-1.0, scalar=FLT_MAX, op0=ALU.add, op1=ALU.min,
                                                 accum_out=negmax[:, n:n + 1]).then_inc(s_max.sem, 1)
                    else:
                        dve.tensor_reduce(negmax[:, n:n + 1], sc_ps[:, n % 2, 0:SK], AX.X, ALU.max, negate=True)\
                            .then_inc(s_max.sem, 1)

                def copy_pT(b, n):
                    dve.wait_ge(s_pT.sem, s_pT.at(b, n))
                    if has(b, 1) or n >= 2:
                        dve.wait_ge(s_pv.sem, s_pv.at(b, n) - 2)
                    dve.tensor_copy(pT[:, n % 2, :, :], pT_ps[0:KT, n % 2, 0:KC * S].rearrange("p (c s) -> p c s", c=KC))\
                        .then_inc(s_pTc[n % 2].sem, 1)

                def normalise(b, par, g):
                    h0 = g * og_heads
                    dve.wait_ge(s_probs.sem, s_probs.at(b, h0 + og_heads - 1))
                    dve.reciprocal(rinv[:, h0:h0 + og_heads], rowsum[:, par, h0:h0 + og_heads]).then_inc(s_rinv.sem, 1)
                    dve.wait_ge(s_rinv.sem, s_rinv.at(b, g))
                    dve.wait_ge(s_pv.sem, s_pv.at(b, h0 + og_heads - 1))
                    if not kan and (has(b, 1) or g > 0):
                        prev = s_fin.at(b, g - 1) if g > 0 else s_fin.at(b - 1, o_groups - 1)
                        dve.wait_ge(s_fin.sem, prev)
                    dve.tensor_tensor(o[:].rearrange("s (h d) -> s h d", h=og_heads),
                                      o_ps[:, 0:og_width].rearrange("s (h d) -> s h d", h=og_heads),
                                      rinv[:, h0:h0 + og_heads].unsqueeze(2).to_broadcast([S, og_heads, hd]),
                                      ALU.mult).then_inc(s_o.sem, 1)

                def update(b):
                    dve.wait_ge(s_fin.sem, s_fin.at(b, fin_jobs - 1))
                    dve.scalar_tensor_tensor(out=x_all[:, b, :], in0=fin_ps[0:S, 0:D], scalar=gate,
                                             in1=x_all[:, b, :], op0=ALU.mult, op1=ALU.add).then_inc(s_finfree.sem, 1)

                def kan_step(b, par, n):
                    def done(ins, k):
                        ins.then_inc(s_k.sem, 1)
                        hold(s_k.sem, s_k.at(b, k))
                    flat = lambda t: t[:].rearrange("p c i s -> p (c i s)")
                    if n == 1:
                        dve.wait_ge(s_o.sem, s_o.at(b))
                        done(dve.tensor_tensor(res[:], o[:], qtok[:, par, :], ALU.add), KAN_RES)
                        done(dve.bn_stats(stats2[:], res[:]), KAN_RES + 1)
                        done(dve.bn_aggr(mv2[:], stats2[:]), KAN_RES + 2)
                        done(dve.tensor_scalar(rstd2[:], mv2[:, 1:2], EPS, None, ALU.add), KAN_VAR)
                    if n == 2:
                        dve.wait_ge(s_pow2.sem, s_pow2.at(b))
                        done(dve.tensor_scalar(resn[:], res[:], mv2[:, 0:1], rstd2[:, 0:1], ALU.subtract, ALU.mult),
                             KAN_RESN)
                    if n == 3:
                        dve.wait_ge(s_fin.sem, s_fin.at(b, 0))
                        for c in range(DC):
                            done(dve.tensor_scalar(lnT[:, c, :], fin_ps[:, c * S:(c + 1) * S], lng[:, c:c + 1],
                                                   lnb[:, c:c + 1], ALU.mult, ALU.add), KAN_RESN + 1 + c)
                        dve.sem_inc(s_finfree.sem, 1)
                        for c in range(DC):
                            done(dve.scalar_tensor_tensor(
                                out=dist[:, c], in0=lnT[:, c, :].unsqueeze(1).to_broadcast([P, 8, S]), scalar=2.5,
                                in1=centers[:].unsqueeze(2).to_broadcast([P, 8, S]),
                                op0=ALU.mult, op1=ALU.subtract), KAN_LNT + 1 + c)
                    if n == 5:
                        dve.wait_ge(s_ka.sem, s_ka.at(b, 0))
                        done(dve.tensor_scalar(sexp[:], sexp[:], 1.0, None, ALU.add), KAN_DIST + 1)
                        done(dve.reciprocal(sexp[:], sexp[:]), KAN_DIST + 2)
                        done(dve.tensor_tensor(silu[:], lnT[:], sexp[:], ALU.mult), KAN_SILU)
                    if n == 6:
                        dve.wait_ge(s_ka.sem, s_ka.at(b, 4))
                        done(dve.tensor_tensor(flat(near2), flat(sq2), flat(near2), ALU.mult), KAN_SILU + 1)
                        dve.wait_ge(s_ka.sem, s_ka.at(b, 5))
                        done(dve.scalar_tensor_tensor(out=flat(near1), in0=flat(sq1), scalar=-4.0, in1=flat(near1),
                                                      op0=ALU.mult, op1=ALU.mult), KAN_SILU + 2)
                        done(dve.tensor_tensor(flat(dist), flat(near2), flat(near1), ALU.add), KAN_BASES)
                    if n == heads - 1:
                        update(b)

                def body(b, par):
                    for n in range(heads):
                        if n + 1 < heads:
                            row_max(b, par, n + 1)
                        elif more(b):
                            row_max(b + 1, 1 - par, 0)
                        if n % 2 == 1:
                            copy_pT(b, n)
                        if has(b, 1):
                            if n == 0:
                                normalise(b - 1, 1 - par, o_groups - 1)
                            if kan:
                                kan_step(b - 1, 1 - par, n)
                            elif n == 5:
                                update(b - 1)
                        if o_groups == 2 and n == og_heads:
                            normalise(b, par, 0)
                        if more(b):
                            if n == 0:
                                norm_stats(b + 1)
                            if n == heads - 4:
                                norm_apply(b + 1)
                                if mask == "keys":
                                    make_mask(b + 1, 1 - par)
                            for j in jobs_at(n):
                                copy_job(j, b + 1, 1 - par)
                            if n == heads - 2 and hd == 16:
                                halve_q(b + 1, 1 - par)

                norm_stats(0)
                norm_apply(0)
                if mask == "keys":
                    make_mask(0, 0)
                for j in jobs:
                    copy_job(j, 0, 0)
                if hd == 16:
                    halve_q(0, 0)
                row_max(0, 0, 0)
                each(dve, body)
                normalise(B - 1, 1, o_groups - 1)
                if kan:
                    for n in range(heads):
                        kan_step(B - 1, 1, n)
                else:
                    update(B - 1)


def setup_stage(core):
    nc = core.nc
    s_in = core.stack.enter_context(nc.semaphore("x_in"))
    s_g = core.stack.enter_context(nc.semaphore("gates_in"))
    s_one = core.stack.enter_context(nc.semaphore("ones_ready"))
    with nc.Block() as block:
        @block.sync
        def _(sp):
            sp.dma_start(core.gates[:], core.dram["gates"].to_broadcast([S, 8])).then_inc(s_g, 16)
            sp.dma_start(core.ident[:], core.dram["ident"]).then_inc(s_in, 16)
            sp.dma_start(core.x_all[:], core.dram["x"].rearrange("b s d -> s b d")).then_inc(s_in, 16)
            sp.wait_ge(s_in, 32)

        @block.scalar
        def _(act):
            act.wait_ge(s_g, 16)
            act.activation(core.gates[:], core.gates[:], ACT.Tanh).then_inc(s_g, 1)
            act.wait_ge(s_g, 17)

        @block.vector
        def _(dve):
            dve.memset(core.ones[:], 1.0).then_inc(s_one, 1)
            dve.memset(core.minus_half[:], -0.5).then_inc(s_one, 1)
            dve.wait_ge(s_one, 2)


def tree_stage(core):
    nc, dram, x_all, ident, ones = core.nc, core.dram, core.x_all, core.ident, core.ones
    gate = core.gates[:, 4:5]
    LEVELS = 8
    M = 2 ** LEVELS
    with ExitStack() as ctx:
        sb, ps = sub_names(ctx, nc, "f0")
        sig = core.new_signals("f0")
        wq, routers = sb("wq", [P, DC, D]), sb("routers", [P, DC, M - 1])
        leaves, wout, bout = sb("leaves", [P, DC, D]), sb("wout", [P, DC, D]), sb("bout", [1, D])
        loads = [(wq, "L0f_wqT"), (routers, "L0f_routersT"), (leaves, "L0f_leaves"), (wout, "L0f_woutT"),
                 (bout, "L0f_bout")]
        stats, mv, rstd, xn = sb("stats", [S, 6]), sb("mv", [S, 2]), sb("rstd", [S, 1]), sb("xn", [S, D])
        xT, qT = sb("xT", [P, DC, S]), sb("qT", [P, DC, S])
        right, left = sb("right", [S, M - 1]), sb("left", [S, M - 1])
        paths = [sb(f"paths{l}", [S, 2 ** (l + 1)]) for l in range(LEVELS)]
        leafT, retT = sb("leafT", [P, DC, S]), sb("retT", [P, DC, S])
        x_ps, q_ps, r_ps = ps("x_ps", [P, 512]), ps("q_ps", [P, 512]), ps("r_ps", [S, 512])
        l_ps, v_ps, y_ps = ps("l_ps", [P, 512]), ps("v_ps", [P, 512]), ps("y_ps", [S, 512])
        s_w = sig("weights_in", 1)
        s_ln, s_pow, s_xn = sig("ln_steps", 3), sig("rstd_ready", 1), sig("xn_ready", 1)
        s_xps, s_xT, s_qps, s_qT = sig("x_turned", 1), sig("xT_ready", 1), sig("q_ready", 1), sig("qT_ready", 1)
        s_rps, s_right, s_tree = sig("routers_done", 1), sig("right_ready", 1), sig("tree_steps", 1 + 2 * LEVELS)
        s_lps, s_leafT = sig("leaves_turned", 1), sig("leafT_ready", 1)
        s_vps, s_retT, s_yps, s_y = sig("values_done", 1), sig("retT_ready", 1), sig("out_done", 1), sig("x_updated", 1)
        s_tick = sig("tick", 0)

        def turns(eng, front, middle, back):
            front(0)
            middle(0)
            front(1)

            def turn(b):
                back(b - 2)
                middle(b - 1)
                front(b)

            with eng.Fori(2, B, 1) as b:
                turn(b)
            back(B - 2)
            middle(B - 1)
            back(B - 1)

        with nc.Block() as block:
            @block.sync
            def _(sp):
                for dst, what in loads:
                    sp.dma_start(dst[:], dram[what]).then_inc(s_w.sem, 16)

            @block.gpsimd
            def _(pool):
                core.clear_spent(pool)
                with pool.Fori(0, B, 1) as b:
                    pool.wait_ge(s_ln.sem, s_ln.at(b, 2))
                    pool.tensor_tensor(rstd[:], rstd[:], core.minus_half[:], ALU.pow).then_inc(s_pow.sem, 1)

            @block.tensor
            def _(pe):
                pe.wait_ge(s_w.sem, 16 * len(loads))

                def front(b):
                    pe.wait_ge(s_xn.sem, s_xn.at(b))
                    if has(b, 1):
                        pe.wait_ge(s_xT.sem, s_xT.at(b - 1))
                    for c in range(DC):
                        mm = pe.transpose(x_ps[:, c * S:(c + 1) * S], xn[:, c * P:(c + 1) * P], ident[0:S, 0:S])
                    mm.then_inc(s_xps.sem, 1)
                    pe.wait_ge(s_xT.sem, s_xT.at(b))
                    if has(b, 1):
                        pe.wait_ge(s_qT.sem, s_qT.at(b - 1))
                    for f in range(DC):
                        for c in range(DC):
                            mm = pe.matmul(q_ps[:, f * S:(f + 1) * S], wq[:, c, f * P:(f + 1) * P], xT[:, c, :],
                                           start=(c == 0), stop=(c == DC - 1))
                    mm.then_inc(s_qps.sem, 1)

                def middle(b):
                    pe.wait_ge(s_qT.sem, s_qT.at(b))
                    if has(b, 1):
                        pe.wait_ge(s_right.sem, s_right.at(b - 1))
                    for c in range(DC):
                        mm = pe.matmul(r_ps[:, 0:M - 1], qT[:, c, :], routers[:, c, :], start=(c == 0),
                                       stop=(c == DC - 1))
                    mm.then_inc(s_rps.sem, 1)

                def back(b):
                    pe.wait_ge(s_tree.sem, s_tree.at(b, 2 * LEVELS))
                    if has(b, 1):
                        pe.wait_ge(s_leafT.sem, s_leafT.at(b - 1))
                    for c in range(DC):
                        mm = pe.transpose(l_ps[:, c * S:(c + 1) * S], paths[-1][:, c * P:(c + 1) * P],
                                          ident[0:S, 0:S])
                    mm.then_inc(s_lps.sem, 1)
                    pe.wait_ge(s_leafT.sem, s_leafT.at(b))
                    if has(b, 1):
                        pe.wait_ge(s_retT.sem, s_retT.at(b - 1))
                    for f in range(DC):
                        for c in range(DC):
                            mm = pe.matmul(v_ps[:, f * S:(f + 1) * S], leaves[:, c, f * P:(f + 1) * P],
                                           leafT[:, c, :], start=(c == 0), stop=(c == DC - 1))
                    mm.then_inc(s_vps.sem, 1)
                    pe.wait_ge(s_retT.sem, s_retT.at(b))
                    if has(b, 1):
                        pe.wait_ge(s_y.sem, s_y.at(b - 1))
                    for c in range(DC):
                        pe.matmul(y_ps[:, 0:D], retT[:, c, :], wout[:, c, :], start=(c == 0), stop=False)
                    pe.matmul(y_ps[:, 0:D], ones[0:1, 0:S], bout[:], start=False, stop=True).then_inc(s_yps.sem, 1)

                turns(pe, front, middle, back)

            @block.scalar
            def _(act):
                turned = lambda t: t[:, 0:DC * S].rearrange("p (c s) -> p c s", c=DC)

                def front(b):
                    act.wait_ge(s_xps.sem, s_xps.at(b))
                    if has(b, 1):
                        act.wait_ge(s_qps.sem, s_qps.at(b - 1))
                    act.activation(xT[:], turned(x_ps), ACT.Copy).then_inc(s_xT.sem, 1)
                    act.wait_ge(s_qps.sem, s_qps.at(b))
                    if has(b, 1):
                        act.wait_ge(s_rps.sem, s_rps.at(b - 1))
                    act.activation(qT[:], turned(q_ps), ACT.Copy).then_inc(s_qT.sem, 1)

                def middle(b):
                    act.wait_ge(s_rps.sem, s_rps.at(b))
                    if has(b, 1):
                        act.wait_ge(s_tree.sem, s_tree.at(b - 1, 2 * LEVELS))
                    act.activation(right[:], r_ps[:, 0:M - 1], ACT.Sigmoid).then_inc(s_right.sem, 1)

                def back(b):
                    act.wait_ge(s_lps.sem, s_lps.at(b))
                    if has(b, 1):
                        act.wait_ge(s_vps.sem, s_vps.at(b - 1))
                    act.activation(leafT[:], turned(l_ps), ACT.Copy).then_inc(s_leafT.sem, 1)
                    act.wait_ge(s_vps.sem, s_vps.at(b))
                    if has(b, 1):
                        act.wait_ge(s_yps.sem, s_yps.at(b - 1))
                    act.activation(retT[:], turned(v_ps), ACT.Copy).then_inc(s_retT.sem, 1)

                turns(act, front, middle, back)

            @block.vector
            def _(dve):
                def hold(sem, value):
                    dve.wait_ge(sem, value)
                    dve.sem_inc(s_tick.sem, 1)

                def front(b):
                    dve.bn_stats(stats[:], x_all[:, b, :]).then_inc(s_ln.sem, 1)
                    hold(s_ln.sem, s_ln.at(b, 0))
                    dve.bn_aggr(mv[:], stats[:]).then_inc(s_ln.sem, 1)
                    dve.wait_ge(s_ln.sem, s_ln.at(b, 1))
                    dve.tensor_scalar(rstd[:], mv[:, 1:2], EPS, None, ALU.add).then_inc(s_ln.sem, 1)
                    dve.wait_ge(s_pow.sem, s_pow.at(b))
                    if has(b, 1):
                        dve.wait_ge(s_xps.sem, s_xps.at(b - 1))
                    dve.tensor_scalar(xn[:], x_all[:, b, :], mv[:, 0:1], rstd[:, 0:1], ALU.subtract, ALU.mult)\
                        .then_inc(s_xn.sem, 1)

                def middle(b):
                    dve.wait_ge(s_right.sem, s_right.at(b))
                    dve.tensor_scalar(left[:], right[:], -1.0, 1.0, ALU.mult, ALU.add).then_inc(s_tree.sem, 1)
                    for level in range(LEVELS):
                        n = 2 ** level
                        pair = paths[level][:].rearrange("s (n two) -> s n two", two=2)
                        dve.wait_ge(s_tree.sem, s_tree.at(b, 2 * level))
                        if level == LEVELS - 1 and has(b, 1):
                            dve.wait_ge(s_lps.sem, s_lps.at(b - 1))
                        for side, prob in enumerate((left, right)):
                            g = prob[:, n - 1:2 * n - 1]
                            if level == 0:
                                dve.tensor_copy(paths[0][:, side:side + 1], g).then_inc(s_tree.sem, 1)
                            else:
                                dve.tensor_tensor(pair[:, :, side], paths[level - 1][:], g, ALU.mult)\
                                    .then_inc(s_tree.sem, 1)

                def back(b):
                    dve.wait_ge(s_yps.sem, s_yps.at(b))
                    dve.scalar_tensor_tensor(out=x_all[:, b, :], in0=y_ps[:, 0:D], scalar=gate, in1=x_all[:, b, :],
                                             op0=ALU.mult, op1=ALU.add).then_inc(s_y.sem, 1)

                turns(dve, front, middle, back)


def route_stage(core, layer, E, xT_all, mix):
    nc, dram, x_all, ident, ones = core.nc, core.dram, core.x_all, core.ident, core.ones
    tag = f"r{layer}"
    name = lambda n: f"L{layer}f_{n}"
    gate = core.gates[:, 4 + layer:5 + layer]
    has_b2 = layer != 3
    RMS_EPS = float(np.finfo(np.float32).eps)
    with ExitStack() as ctx:
        sb, ps = sub_names(ctx, nc, tag)
        sig = core.new_signals(tag)
        wg = sb("wg", [P, DC, E])
        loads = [(wg[:], dram[name("gateT")])]
        if layer == 1:
            cents = sb("cents", [8, D])
            loads.append((cents[:], dram[name("centroids")]))
        else:
            bg = sb("bg", [1, E])
            loads.append((bg[:], dram[name("gate_bias")]))
        if layer == 2:
            ln_w = sb("ln_w", [P, DC])
            loads.append((ln_w[:], dram[name("ln_w")]))
        if has_b2:
            b2 = sb("b2", [E, D])
            loads.append((b2[:], dram[name("b2")]))
        number = sb("number", [S, E])
        loads.append((number[:], dram[f"numbers{E}"].to_broadcast([S, E])))
        stats, mv, rstd = sb("stats", [S, 2, 6]), sb("mv", [S, 2, 2]), sb("rstd", [S, 2, 1])
        rms = sb("rms", [S, 2, 1])
        sq, norm, cn = sb("sq", [S, D]), sb("norm", [S, 2, 1]), sb("cn", [8, D])
        cnT = sb("cnT", [P, DC, 8])
        xn, xT = sb("xn", [S, 2, D]), sb("xT", [P, 2, DC, S])
        logits = sb("logits", [S, B, E])
        best, at = sb("best", [S, B, 8]), sb("at", [S, B, 8], mybir.dt.uint32)
        place = sb("place", [S, B, 8])
        share, total = sb("share", [S, B, 2]), sb("total", [S, B])
        pick = sb("pick", [S, B, E])
        mixT, gscale = sb("mixT", [E, 2, S]), sb("gscale", [S, 1])
        x_ps, l_ps = ps("x_ps", [P, 2, 512]), ps("l_ps", [S, 2, 512])
        m_ps, y_ps = ps("m_ps", [P, 2, 512]), ps("y_ps", [S, 2, 512])
        s_w = sig("weights_in", 1)
        twice = layer in (1, 2)
        s_ln, s_pow, s_xn = sig("ln_steps", 5 if twice else 3), sig("rstd_ready", 2 if twice else 1), sig("xn_ready", 1)
        s_rms, s_l1 = sig("scale_ready", 1), sig("route_part", 1)
        s_xps, s_xT, s_all = sig("x_turned", 1), sig("xT_ready", DC), sig("xT_all_ready", 1)
        s_lps, s_l, s_tick = sig("logits_done", 1), sig("logits_copied", 1), sig("tick", 0)
        s_cos = sig("cosine_part", 1)
        s_rt, s_to_act, s_act = sig("route_steps", 1), sig("for_scalar", 1), sig("scalar_done", 1)
        s_mps, s_m, s_yps, s_y = sig("mix_turned", 1), sig("mixT_ready", 1), sig("bias_done", 1), sig("bias_added", 1)
        s_mix = sig("mix_ready", 1)
        cosine = layer == 1

        with nc.Block() as block:
            @block.sync
            def _(sp):
                for dst, src in loads:
                    sp.dma_start(dst, src).then_inc(s_w.sem, 16)

            @block.gpsimd
            def _(pool):
                core.clear_spent(pool)
                if cosine:
                    pool.wait_ge(s_cos.sem, 2)
                    pool.tensor_tensor(norm[0:8, 0, :], norm[0:8, 0, :], core.minus_half[0:8, :], ALU.pow)\
                        .then_inc(s_cos.sem, 1)

                def body(b, par):
                    pool.wait_ge(s_ln.sem, s_ln.at(b, 2))
                    pool.tensor_tensor(rstd[:, par, :], rstd[:, par, :], core.minus_half[:], ALU.pow)\
                        .then_inc(s_pow.sem, 1)
                    if twice:
                        pool.wait_ge(s_ln.sem, s_ln.at(b, 4))
                        pool.tensor_tensor(rms[:, par, :], rms[:, par, :], core.minus_half[:], ALU.pow)\
                            .then_inc(s_pow.sem, 1)
                each(pool, body)

            @block.tensor
            def _(pe):
                pe.wait_ge(s_w.sem, 16 * len(loads))
                if cosine:
                    pe.wait_ge(s_cos.sem, 4)
                    for c in range(DC):
                        mm = pe.transpose(x_ps[:, 0, c * 8:(c + 1) * 8], cn[:, c * P:(c + 1) * P], ident[0:8, 0:8])
                    mm.then_inc(s_cos.sem, 1)
                    pe.wait_ge(s_cos.sem, 6)

                def turn(b, par):
                    pe.wait_ge(s_xn.sem, s_xn.at(b))
                    if has(b, 2):
                        pe.wait_ge(s_xT.sem, s_xT.at(b - 2, DC - 1))
                    for c in range(DC):
                        mm = pe.transpose(x_ps[:, par, c * S:(c + 1) * S], xn[:, par, c * P:(c + 1) * P],
                                          ident[0:S, 0:S])
                    mm.then_inc(s_xps.sem, 1)

                def score(b, par):
                    pe.wait_ge(s_xT.sem, s_xT.at(b, DC - 1))
                    if has(b, 2):
                        pe.wait_ge(s_l.sem, s_l.at(b - 2))
                    for c in range(DC):
                        mm = pe.matmul(l_ps[:, par, 0:E], xT[:, par, c, :], wg[:, c, :], start=(c == 0),
                                       stop=(cosine and c == DC - 1))
                    if cosine:
                        for c in range(DC):
                            mm = pe.matmul(l_ps[:, par, 8:16], xT[:, par, c, :], cnT[:, c, :], start=(c == 0),
                                           stop=(c == DC - 1))
                    else:
                        mm = pe.matmul(l_ps[:, par, 0:E], ones[0:1, 0:S], bg[:], start=False, stop=True)
                    mm.then_inc(s_lps.sem, 1)

                def body(b, par):
                    turn(b, par)
                    if has(b, 1):
                        score(b - 1, 1 - par)
                each(pe, body)
                score(B - 1, 1)
                if has_b2:
                    pe.wait_ge(s_mix.sem, 1)
                    for b in range(B):
                        if b >= 2:
                            pe.wait_ge(s_m.sem, b - 1)
                        pe.transpose(m_ps[0:E, b % 2, 0:S], mix[:, b, :], ident[0:S, 0:S]).then_inc(s_mps.sem, 1)
                        pe.wait_ge(s_m.sem, b + 1)
                        if b >= 2:
                            pe.wait_ge(s_y.sem, b - 1)
                        pe.matmul(y_ps[:, b % 2, 0:D], mixT[:, b % 2, :], b2[:], start=True, stop=True)\
                            .then_inc(s_yps.sem, 1)

            @block.scalar
            def _(act):
                act.wait_ge(s_w.sem, 16 * len(loads))
                if cosine:
                    act.wait_ge(s_cos.sem, 5)
                    act.activation(cnT[:], x_ps[:, 0, 0:DC * 8].rearrange("p (c e) -> p c e", c=DC), ACT.Copy)\
                        .then_inc(s_cos.sem, 1)

                def body(b, par):
                    act.wait_ge(s_xps.sem, s_xps.at(b))
                    if has(b, 2):
                        act.wait_ge(s_lps.sem, s_lps.at(b - 2))
                        act.wait_ge(s_all.sem, s_all.at(b - 2))
                    for c in range(DC):
                        act.activation(xT[:, par, c, :], x_ps[:, par, c * S:(c + 1) * S], ACT.Copy,
                                       scale=ln_w[:, c:c + 1] if layer == 2 else 1.0).then_inc(s_xT.sem, 1)
                    act.wait_ge(s_xT.sem, s_xT.at(b, DC - 1))
                    act.sem_inc(s_tick.sem, 1)
                    act.activation(xT_all[:, :, b, :], xT[:, par, :, :], ACT.Copy).then_inc(s_all.sem, 1)
                each(act, body)
                what = {1: pick[:], 2: share[:, :, 1], 3: logits[:]}[layer]
                act.wait_ge(s_to_act.sem, 1)
                act.activation(what, what, ACT.Sigmoid if layer == 3 else ACT.Exp).then_inc(s_act.sem, 1)
                if has_b2:
                    for b in range(B):
                        act.wait_ge(s_mps.sem, b + 1)
                        if b >= 2:
                            act.wait_ge(s_yps.sem, b - 1)
                        act.activation(mixT[:, b % 2, :], m_ps[0:E, b % 2, 0:S], ACT.Copy).then_inc(s_m.sem, 1)

            @block.vector
            def _(dve):
                dve.wait_ge(s_w.sem, 16 * len(loads))
                if cosine:
                    dve.tensor_tensor_reduce(out=cn[:], in0=cents[:], in1=cents[:], scale=1.0, scalar=0.0,
                                             op0=ALU.mult, op1=ALU.add, accum_out=norm[0:8, 0, :])\
                        .then_inc(s_cos.sem, 1)
                    dve.wait_ge(s_cos.sem, 1)
                    dve.tensor_scalar(norm[0:8, 0, :], norm[0:8, 0, :], 1e-24, None, ALU.max).then_inc(s_cos.sem, 1)
                    dve.wait_ge(s_cos.sem, 3)
                    dve.tensor_scalar(cn[:], cents[:], norm[0:8, 0, :], None, ALU.mult).then_inc(s_cos.sem, 1)

                def hold(sem, value):
                    dve.wait_ge(sem, value)
                    dve.sem_inc(s_tick.sem, 1)

                def front(b, par):
                    dve.bn_stats(stats[:, par, :], x_all[:, b, :]).then_inc(s_ln.sem, 1)
                    hold(s_ln.sem, s_ln.at(b, 0))
                    dve.bn_aggr(mv[:, par, :], stats[:, par, :]).then_inc(s_ln.sem, 1)
                    dve.wait_ge(s_ln.sem, s_ln.at(b, 1))
                    dve.tensor_scalar(rstd[:, par, :], mv[:, par, 1:2], EPS, None, ALU.add).then_inc(s_ln.sem, 1)
                    if twice:
                        dve.wait_ge(s_pow.sem, s_pow.at(b, 0))
                        dve.scalar_tensor_tensor(out=rms[:, par, :], in0=rstd[:, par, :], scalar=mv[:, par, 1:2],
                                                 in1=rstd[:, par, :], op0=ALU.mult, op1=ALU.mult)\
                            .then_inc(s_ln.sem, 1)
                        dve.wait_ge(s_ln.sem, s_ln.at(b, 3))
                        if layer == 2:
                            dve.tensor_scalar(rms[:, par, :], rms[:, par, :], RMS_EPS, None, ALU.add)\
                                .then_inc(s_ln.sem, 1)
                        else:
                            dve.tensor_scalar(rms[:, par, :], rms[:, par, :], float(D), 1e-24, ALU.mult, ALU.max)\
                                .then_inc(s_ln.sem, 1)

                def apply(b, par):
                    dve.wait_ge(s_pow.sem, s_pow.at(b, s_pow.per - 1))
                    by = rstd
                    if layer == 2:
                        dve.tensor_tensor(rms[:, par, :], rms[:, par, :], rstd[:, par, :], ALU.mult)\
                            .then_inc(s_rms.sem, 1)
                        dve.wait_ge(s_rms.sem, s_rms.at(b))
                        by = rms
                    if has(b, 2):
                        dve.wait_ge(s_xps.sem, s_xps.at(b - 2))
                    dve.tensor_scalar(xn[:, par, :], x_all[:, b, :], mv[:, par, 0:1], by[:, par, :],
                                      ALU.subtract, ALU.mult).then_inc(s_xn.sem, 1)

                def take(b, par):
                    dve.wait_ge(s_lps.sem, s_lps.at(b))
                    if cosine:
                        dve.tensor_scalar(logits[:, b, :], l_ps[:, par, 0:E], 1.0, None, ALU.mult)\
                            .then_inc(s_l1.sem, 1)
                        dve.wait_ge(s_l1.sem, s_l1.at(b))
                        dve.scalar_tensor_tensor(out=logits[:, b, :], in0=l_ps[:, par, 8:16],
                                                 scalar=rms[:, par, :], in1=logits[:, b, :],
                                                 op0=ALU.mult, op1=ALU.add).then_inc(s_l.sem, 1)
                    else:
                        dve.tensor_scalar(logits[:, b, :], l_ps[:, par, 0:E], 1.0, None, ALU.mult)\
                            .then_inc(s_l.sem, 1)

                def body(b, par):
                    front(b, par)
                    apply(b, par)
                    if has(b, 1):
                        take(b - 1, 1 - par)
                each(dve, body)
                take(B - 1, 1)

                steps = [0]

                def done(ins):
                    steps[0] += 1
                    ins.then_inc(s_rt.sem, 1)
                    dve.wait_ge(s_rt.sem, steps[0])

                over_experts = lambda t: t.unsqueeze(2).to_broadcast([S, B, E])
                dve.wait_ge(s_l.sem, B)
                if layer == 3:
                    dve.sem_inc(s_to_act.sem, 1)
                    dve.wait_ge(s_act.sem, 1)
                for b in range(B):
                    last = dve.max(best[:, b, :], logits[:, b, :])
                done(last)
                if layer == 1:
                    done(dve.tensor_tensor(pick[:], logits[:], over_experts(best[:, :, 0]), ALU.subtract))
                    dve.sem_inc(s_to_act.sem, 1)
                    done(dve.tensor_tensor(logits[:], logits[:], over_experts(best[:, :, 1]), ALU.is_ge))
                    dve.wait_ge(s_act.sem, 1)
                    done(dve.tensor_tensor(pick[:], pick[:], logits[:], ALU.mult))
                    done(dve.tensor_reduce(total[:], pick[:], AX.X, ALU.add))
                    done(dve.reciprocal(total[:], total[:]))
                    done(dve.tensor_tensor(mix[:], pick[:], over_experts(total[:]), ALU.mult))
                else:
                    for b in range(B):
                        last = dve.max_index(at[:, b, :], best[:, b, :], logits[:, b, :])
                    done(last)
                    done(dve.tensor_copy(place[:], at[:]))
                    if layer == 2:
                        done(dve.tensor_tensor(share[:, :, 1], best[:, :, 1], best[:, :, 0], ALU.subtract))
                        dve.sem_inc(s_to_act.sem, 1)
                        dve.wait_ge(s_act.sem, 1)
                        done(dve.tensor_scalar(total[:], share[:, :, 1], 1.0, None, ALU.add))
                        done(dve.reciprocal(share[:, :, 0], total[:]))
                        done(dve.tensor_tensor(share[:, :, 1], share[:, :, 1], share[:, :, 0], ALU.mult))
                    else:
                        done(dve.tensor_tensor(total[:], best[:, :, 0], best[:, :, 1], ALU.add))
                        done(dve.tensor_scalar(total[:], total[:], 1e-20, None, ALU.add))
                        done(dve.reciprocal(total[:], total[:]))
                        for k in range(2):
                            done(dve.tensor_tensor(share[:, :, k], best[:, :, k], total[:], ALU.mult))
                    every = number[:].unsqueeze(1).to_broadcast([S, B, E])
                    for k, dst in enumerate((mix, pick)):
                        done(dve.tensor_tensor(dst[:], every, over_experts(place[:, :, k]), ALU.is_equal))
                        done(dve.tensor_tensor(dst[:], dst[:], over_experts(share[:, :, k]), ALU.mult))
                    done(dve.tensor_tensor(mix[:], mix[:], pick[:], ALU.add))
                done(dve.tensor_scalar(mix[:], mix[:], gate, None, ALU.mult))
                dve.sem_inc(s_mix.sem, 1)
                if has_b2:
                    for b in range(B):
                        dve.wait_ge(s_yps.sem, b + 1)
                        dve.tensor_tensor(x_all[:, b, :], x_all[:, b, :], y_ps[:, b % 2, 0:D], ALU.add)\
                            .then_inc(s_y.sem, 1)


G = 4
GB = B // G
GN = GB * S


def small_experts_stage(core, xT_all, mix):
    nc, dram, x_all = core.nc, core.dram, core.x_all
    E = 8
    with ExitStack() as ctx:
        sb, ps = sub_names(ctx, nc, "e1")
        sig = core.new_signals("e1")
        w1, b1, w2 = sb("w1", [P, DC, E * P]), sb("b1", [P, E]), sb("w2", [P, E, D])
        loads = [(w1, "L1f_w1"), (b1, "L1f_b1"), (w2, "L1f_w2")]
        hid = sb("hid", [P, 2, GN])
        u_ps = ps("u_ps", [P, 2, 512])
        y_ps = ps("y_ps", [S, 2, GB, D])
        s_w = sig("weights_in", 1)
        s_up, s_gelu, s_down, s_y = sig("up_done", E), sig("gelu_done", E), sig("down_done", E), sig("added", E * GB)
        s_tick = sig("tick", 0)
        x_of = xT_all[:].rearrange("p c b s -> p c (b s)")
        with nc.Block() as block:
            @block.sync
            def _(sp):
                for dst, what in loads:
                    sp.dma_start(dst[:], dram[what]).then_inc(s_w.sem, 16)

            @block.gpsimd
            def _(pool):
                core.clear_spent(pool)

            def groups(eng, body):
                body(0)
                with eng.Fori(1, G, 1) as g:
                    body(g)

            @block.tensor
            def _(pe):
                pe.wait_ge(s_w.sem, 16 * len(loads))

                def down(g, e):
                    pe.wait_ge(s_gelu.sem, s_gelu.at(g, e))
                    if has(g, 1) or e >= 2:
                        pe.wait_ge(s_y.sem, s_y.at(g, GB * e + GB - 1) - 2 * GB)
                    for t in range(GB):
                        mm = pe.matmul(y_ps[:, e % 2, t, :], hid[:, e % 2, t * S:(t + 1) * S], w2[:, e, :],
                                       start=True, stop=True)
                    mm.then_inc(s_down.sem, 1)

                def body(g):
                    for e in range(E):
                        if has(g, 1) or e >= 2:
                            pe.wait_ge(s_gelu.sem, s_gelu.at(g, e) - 2)
                        for c in range(DC):
                            mm = pe.matmul(u_ps[:, e % 2, 0:GN], w1[:, c, e * P:(e + 1) * P],
                                           x_of[:, c, bass.ds(g * GN, GN)], start=(c == 0), stop=(c == DC - 1))
                        mm.then_inc(s_up.sem, 1)
                        if e > 0:
                            down(g, e - 1)
                    down(g, E - 1)
                groups(pe, body)

            @block.scalar
            def _(act):
                act.wait_ge(s_w.sem, 16 * len(loads))

                def body(g):
                    for e in range(E):
                        act.wait_ge(s_up.sem, s_up.at(g, e))
                        if has(g, 1) or e >= 2:
                            act.wait_ge(s_down.sem, s_down.at(g, e) - 2)
                        act.activation(hid[:, e % 2, :], u_ps[:, e % 2, 0:GN], ACT.Gelu, bias=b1[:, e:e + 1])\
                            .then_inc(s_gelu.sem, 1)
                groups(act, body)

            @block.vector
            def _(dve):
                def body(g):
                    for e in range(E):
                        dve.wait_ge(s_down.sem, s_down.at(g, e))
                        for t in range(GB):
                            b = g * GB + t
                            if e > 0:
                                dve.wait_ge(s_y.sem, s_y.at(g, (e - 1) * GB + t))
                            dve.scalar_tensor_tensor(out=x_all[:, b, :], in0=y_ps[:, e % 2, t, :],
                                                     scalar=mix[:, b, e:e + 1], in1=x_all[:, b, :],
                                                     op0=ALU.mult, op1=ALU.add).then_inc(s_y.sem, 1)
                groups(dve, body)


def experts_stage(core, layer, E, F, xT_all, mix):
    nc, dram, x_all = core.nc, core.dram, core.x_all
    name = lambda n: f"L{layer}f_{n}"
    FC = -(-F // P)
    rows = [min(P, F - f * P) for f in range(FC)]
    biased = layer == 2
    assert FC % 2 == 0
    with ExitStack() as ctx:
        sb, ps = sub_names(ctx, nc, f"e{layer}")
        sig = core.new_signals(f"e{layer}")
        w1, w3, w2 = sb("w1", [P, 2, DC, F]), sb("w3", [P, 2, DC, F]), sb("w2", [P, 2, FC, D])
        loads = [(w1, "w1"), (w3, "w3"), (w2, "w2")]
        if biased:
            b1, b3 = sb("b1", [P, 2, FC]), sb("b3", [P, 2, FC])
            loads += [(b1, "b1"), (b3, "b3")]
        hid = sb("hid", [P, 2, FC, GN])
        silu = sb("silu", [P, 2, GN])
        col = sb("col", [S, 2, B])
        a_ps, b_ps, y_ps = ps("a_ps", [P, 2, 512]), ps("b_ps", [P, 2, 512]), ps("y_ps", [S, 2, 512])
        s_w = [sig(f"weights_in{i}", 1) for i in range(2)]
        s_up, s_silu, s_hid = sig("up_done", G * FC), sig("silu_done", G * FC), sig("hid_ready", G * FC)
        s_down, s_y, s_col = sig("down_done", B), sig("added", B), sig("column_ready", 1)
        s_tick = sig("tick", 0)
        x_of = xT_all[:].rearrange("p c b s -> p c (b s)")

        def experts(eng, body):
            body(0, 0)
            body(1, 1)
            with eng.Fori(1, E // 2, 1) as j:
                body(j * 2, 0)
                body(j * 2 + 1, 1)
            if E % 2:
                body(E - 1, 0)

        def weights_in(eng, e, par):
            eng.wait_ge(s_w[par].sem, half(e, par) * len(loads))

        with nc.Block() as block:
            @block.gpsimd
            def _(pool):
                core.clear_spent(pool)

            @block.sync
            def _(sp):
                def body(e, par):
                    if has(e, 2):
                        sp.wait_ge(s_down.sem, s_down.at(e - 2, B - 1))
                        sp.sem_inc(s_tick.sem, 1)
                    for dst, what in loads:
                        sp.dma_start(dst[:, par], dram[name(what)][e]).then_inc(s_w[par].sem, 16)
                experts(sp, body)

            @block.tensor
            def _(pe):
                def body(e, par):
                    weights_in(pe, e, par)
                    for g in range(G):
                        for f in range(FC):
                            n = g * FC + f
                            if has(e, 1) or n >= 2:
                                pe.wait_ge(s_hid.sem, s_hid.at(e, n) - 2)
                            for w, out in ((w1, a_ps), (w3, b_ps)):
                                for c in range(DC):
                                    mm = pe.matmul(out[0:rows[f], f % 2, 0:GN], w[:, par, c, f * P:f * P + rows[f]],
                                                   x_of[:, c, g * GN:(g + 1) * GN], start=(c == 0),
                                                   stop=(c == DC - 1))
                            mm.then_inc(s_up.sem, 1)
                        for t in range(GB):
                            b = g * GB + t
                            if has(e, 1) or b >= 2:
                                pe.wait_ge(s_y.sem, s_y.at(e, b) - 2)
                            for f in range(FC):
                                if t == 0:
                                    pe.wait_ge(s_hid.sem, s_hid.at(e, g * FC + f))
                                mm = pe.matmul(y_ps[:, b % 2, 0:D], hid[0:rows[f], g % 2, f, t * S:(t + 1) * S],
                                               w2[0:rows[f], par, f, :], start=(f == 0), stop=(f == FC - 1))
                            mm.then_inc(s_down.sem, 1)
                experts(pe, body)

            @block.scalar
            def _(act):
                def body(e, par):
                    if biased:
                        weights_in(act, e, par)
                    for g in range(G):
                        for f in range(FC):
                            n, r = g * FC + f, rows[f]
                            act.wait_ge(s_up.sem, s_up.at(e, n))
                            if has(e, 1) or n >= 2:
                                act.wait_ge(s_hid.sem, s_hid.at(e, n) - 2)
                            act.activation(silu[0:r, f % 2, :], a_ps[0:r, f % 2, 0:GN], ACT.Silu,
                                           bias=b1[0:r, par, f:f + 1] if biased else 0.0).then_inc(s_silu.sem, 1)
                experts(act, body)

            @block.vector
            def _(dve):
                def body(e, par):
                    if biased:
                        weights_in(dve, e, par)
                    dve.tensor_scalar(col[:, par, :], mix[:, :, e], 1.0, None, ALU.mult).then_inc(s_col.sem, 1)
                    dve.wait_ge(s_col.sem, s_col.at(e))
                    for g in range(G):
                        for f in range(FC):
                            n, r = g * FC + f, rows[f]
                            dve.wait_ge(s_silu.sem, s_silu.at(e, n))
                            if f == 0 and (has(e, 1) or g >= 2):
                                dve.wait_ge(s_down.sem, s_down.at(e, g * GB) - 1 - GB)
                            dst = hid[0:r, g % 2, f, :]
                            if biased:
                                dve.scalar_tensor_tensor(out=dst, in0=b_ps[0:r, f % 2, 0:GN],
                                                         scalar=b3[0:r, par, f:f + 1], in1=silu[0:r, f % 2, :],
                                                         op0=ALU.add, op1=ALU.mult).then_inc(s_hid.sem, 1)
                            else:
                                dve.tensor_tensor(dst, b_ps[0:r, f % 2, 0:GN], silu[0:r, f % 2, :], ALU.mult)\
                                    .then_inc(s_hid.sem, 1)
                        for t in range(GB):
                            b = g * GB + t
                            dve.wait_ge(s_down.sem, s_down.at(e, b))
                            dve.scalar_tensor_tensor(out=x_all[:, b, :], in0=y_ps[:, b % 2, 0:D],
                                                     scalar=col[:, par, b:b + 1], in1=x_all[:, b, :],
                                                     op0=ALU.mult, op1=ALU.add).then_inc(s_y.sem, 1)
                experts(dve, body)


def moe(core, layer, E, F):
    with ExitStack() as ctx:
        xT_all = ctx.enter_context(core.nc.sbuf_tensor(f"xT_all{layer}", [P, DC, B, S], F32))
        mix = ctx.enter_context(core.nc.sbuf_tensor(f"mix{layer}", [S, B, E], F32))
        route_stage(core, layer, E, xT_all, mix)
        if layer == 1:
            small_experts_stage(core, xT_all, mix)
        else:
            experts_stage(core, layer, E, F, xT_all, mix)


def store_stage(core, out):
    nc = core.nc
    s_out = core.stack.enter_context(nc.semaphore("x_stored"))
    with nc.Block() as block:
        @block.sync
        def _(sp):
            sp.dma_start(out.rearrange("b s d -> s b d"), core.x_all[:]).then_inc(s_out, 16)
            sp.wait_ge(s_out, 16)


def flamingo(nc, dram, out, stages=8):
    with ExitStack() as stack:
        core = Core(nc, dram, stack)
        setup_stage(core)
        todo = [
            lambda: attention_stage(core, 0, heads=8, hd=32, scale=D ** -0.5, kan=True),
            lambda: tree_stage(core),
            lambda: attention_stage(core, 1, heads=16, hd=64, scale=64 ** -0.5, mask="keys"),
            lambda: moe(core, 1, 8, 128),
            lambda: attention_stage(core, 2, heads=16, hd=16, scale=0.25, rope=True),
            lambda: moe(core, 2, 8, 1024),
            lambda: attention_stage(core, 3, heads=16, hd=16, scale=0.25, mask="scores"),
            lambda: moe(core, 3, 9, 704),
        ]
        for stage in todo[:stages]:
            stage()
        store_stage(core, out)


def host_layout(inputs):
    get = lambda n: np.asarray(inputs[n])

    def chunks(a):
        return np.ascontiguousarray(a.reshape(a.shape[0] // P, P, *a.shape[1:]).swapaxes(0, 1))

    turned = lambda a: chunks(np.ascontiguousarray(a.T))
    row = lambda a: np.ascontiguousarray(a.reshape(1, -1))
    col = lambda a: np.ascontiguousarray(a.reshape(-1, P).T)
    o = {
        "x": get("x"),
        "gates": np.concatenate([get("g_xattn"), get("g_ffn")]).reshape(1, 8),
        "ident": np.eye(P, dtype=np.float32),
        "ctxT": np.ascontiguousarray(get("ctx_1024").transpose(0, 2, 1).reshape(B, DC, P, SK).transpose(0, 2, 1, 3)),
        "mask_keys": np.ascontiguousarray(get("mask_BxS2_bf1")).view(np.uint8).reshape(B, 1, SK),
        "mask_scores": get("mask_1x1xSxS2_ik1")[0, 0],
        "numbers8": np.arange(8, dtype=np.float32).reshape(1, 8),
        "numbers9": np.arange(9, dtype=np.float32).reshape(1, 9),
    }
    for n in "qkv":
        o[f"L0x_w{n}T"] = turned(get(f"L0_xattn_w{n}"))
        o[f"L0x_b{n}"] = col(get(f"L0_xattn_b{n}"))
    o["L0x_bqrow"], o["L0x_bvrow"] = row(get("L0_xattn_bq")), row(get("L0_xattn_bv"))
    o["L0x_ln_g"], o["L0x_ln_b"] = col(get("L0_xattn_ln_g")), col(get("L0_xattn_ln_b"))
    o["L0x_base_wT"] = turned(get("L0_xattn_kan_base_w"))
    o["L0x_spline_wT"] = chunks(get("L0_xattn_kan_spline_w").transpose(1, 2, 0))
    o["L0x_scalerT"] = turned(get("L0_xattn_kan_spline_scaler"))
    o["L0x_centers"] = np.ascontiguousarray(np.broadcast_to(np.arange(8, dtype=np.float32) - 3.5, (P, 8)))
    o["L0f_wqT"], o["L0f_routersT"] = turned(get("L0_ffn_Wq")), turned(get("L0_ffn_routers"))
    o["L0f_leaves"], o["L0f_woutT"] = chunks(get("L0_ffn_leaf_values")), turned(get("L0_ffn_Wout_w"))
    o["L0f_bout"] = row(get("L0_ffn_Wout_b"))
    o["L1x_wqT"] = turned(get("L1_xattn_Wq"))
    o["L1x_wkT"], o["L1x_wvT"] = turned(get("L1_xattn_Wkv")[:1024]), turned(get("L1_xattn_Wkv")[1024:])
    o["L1x_woT"], o["L1x_bo"] = turned(get("L1_xattn_Wout")), row(get("L1_xattn_b_out"))
    o["L1f_gateT"], o["L1f_centroids"] = turned(get("L1_ffn_w_route")), get("L1_ffn_centroids")
    o["L1f_b2"] = get("L1_ffn_b2")
    o["L1f_w1"] = chunks(get("L1_ffn_w1").transpose(1, 0, 2).reshape(D, 8 * P))
    o["L1f_b1"] = np.ascontiguousarray(get("L1_ffn_b1").T)
    o["L1f_w2"] = np.ascontiguousarray(get("L1_ffn_w2").transpose(1, 0, 2))
    for layer in (2, 3):
        for n in "qkvo":
            o[f"L{layer}x_w{n}T"] = turned(get(f"L{layer}_xattn_W{n}"))
            o[f"L{layer}x_b{n}"] = (row if n == "o" else col)(get(f"L{layer}_xattn_b{n}"))
        odd = np.arange(P) // 16 % 2
        o[f"L{layer}x_halves"] = np.stack([(1 - odd) * 0.25, odd * 0.25], axis=1).astype(np.float32)
    swap = np.arange(D) // 16 * 16 + (np.arange(D) % 16 + 8) % 16
    for n in "qk":
        o[f"L2x_w{n}rT"] = turned(get(f"L2_xattn_W{n}")[swap])
        o[f"L2x_b{n}r"] = col(get(f"L2_xattn_b{n}")[swap])
    inv_freq = np.float32(1.0) / np.float32(10000.0) ** (np.arange(0, 16, 2, dtype=np.float32) / np.float32(16))
    freqs = np.arange(SK, dtype=np.float32)[None, :] * inv_freq[np.arange(P) % 8][:, None]
    sign = np.where(np.arange(P) % 16 < 8, -1.0, 1.0).astype(np.float32)
    o["L2x_cos"] = np.cos(freqs)
    o["L2x_sin"] = np.sin(freqs) * sign[:, None]
    o["L2f_gateT"], o["L2f_gate_bias"] = chunks(get("L2_ffn_Wg")), row(get("L2_ffn_bg"))
    o["L2f_ln_w"], o["L2f_b2"] = col(get("L2_ffn_ln_w")), get("L2_ffn_b2")
    per_expert = lambda a: np.ascontiguousarray(a.reshape(a.shape[0], a.shape[1] // P, P, a.shape[2]).transpose(0, 2, 1, 3))
    o["L2f_w1"], o["L2f_w3"] = per_expert(get("L2_ffn_W1a")), per_expert(get("L2_ffn_W1b"))
    o["L2f_w2"] = per_expert(get("L2_ffn_W2"))
    for n, what in (("b1", "b1a"), ("b3", "b1b")):
        o[f"L2f_{n}"] = np.ascontiguousarray(get(f"L2_ffn_{what}").reshape(8, 8, P).transpose(0, 2, 1))
    both = lambda a, b: np.concatenate([get(a), get(b)], axis=0)
    o["L3f_gateT"] = turned(both("L3_ffn_gate_weight", "L3_ffn_new_gate_weight"))
    o["L3f_gate_bias"] = row(np.concatenate([np.zeros(8, np.float32), get("L3_ffn_gate_bias")]))
    for n in ("w1", "w3"):
        o[f"L3f_{n}"] = per_expert(both(f"L3_ffn_{n}", f"L3_ffn_new_{n}").transpose(0, 2, 1))
    w2 = both("L3_ffn_w2", "L3_ffn_new_w2").transpose(0, 2, 1)
    padded = np.zeros((w2.shape[0], 6 * P, D), np.float32)
    padded[:, :w2.shape[1]] = w2
    o["L3f_w2"] = per_expert(padded)
    return {k: np.ascontiguousarray(a) for k, a in o.items()}


def kernel(**inputs):
    import concourse.bacc as bacc
    from concourse.bass_utils import run_bass_kernel_spmd

    nc = bacc.Bacc("TRN2", target_bir_lowering=False, num_devices=1)
    arrays = {f"in_{k}": a for k, a in host_layout(inputs).items()}
    dram = {k[3:]: nc.dram_tensor(k, a.shape, mybir.dt.from_np(a.dtype), kind="ExternalInput").ap()
            for k, a in arrays.items()}
    out = nc.dram_tensor("out_0", (B, S, D), F32, kind="ExternalOutput").ap()
    flamingo(nc, dram, out)
    result = run_bass_kernel_spmd(nc, [arrays], core_ids=[0])
    return result.results[0]["out_0"]
```

```python
from contextlib import ExitStack

import numpy as np

import concourse.bass as bass
from concourse import mybir

F32 = mybir.dt.float32
U8 = mybir.dt.uint8
I32 = mybir.dt.int32
ALU = mybir.AluOpType
ACT = mybir.ActivationFunctionType
AX = mybir.AxisListType

P = 128
B, S, D, SK = 16, 112, 256, 375
DC = D // P
KC = 3
KT = SK // KC
EPS = 1e-5
FLT_MAX = float(np.finfo(np.float32).max)


class Signal:

    def __init__(self, new, name, per):
        self.sem, self.per = new(name), per

    def at(self, b, k=0):
        return b * self.per + (k + 1)


def has(b, lag):
    return not isinstance(b, int) or b - lag >= 0


def more(b):
    return not isinstance(b, int) or b < B - 1


def exists(b):
    return not isinstance(b, int) or 0 <= b < B


def half(b, par):
    return (b - par) * 8 + 16


def each(eng, body):
    body(0, 0)
    body(1, 1)
    with eng.Fori(1, B // 2 - 1, 1) as j:
        body(j * 2, 0)
        body(j * 2 + 1, 1)
    body(B - 2, 0)
    body(B - 1, 1)


LEAD = 3
KAN_RES, KAN_VAR, KAN_RESN, KAN_LNT, KAN_DIST, KAN_SILU, KAN_BASES = 0, 3, 4, 6, 8, 11, 14


class Core:

    def __init__(self, nc, dram, stack):
        self.nc, self.dram, self.stack = nc, dram, stack
        sb = lambda n, s: stack.enter_context(nc.sbuf_tensor(n, s, F32))
        self.x_all = sb("x_all", [S, B, D])
        self.ident = sb("ident", [P, P])
        self.ones = sb("ones", [1, P])
        self.minus_half = sb("minus_half", [S, 1])
        self.zeros = sb("zeros", [P, D])
        self.gates = sb("gates", [S, 8])
        self.spent, self.current = ExitStack(), ExitStack()
        self.spent_sems, self.current_sems = [], []

    def new_signals(self, tag):
        self.spent.close()
        self.spent, self.spent_sems = self.current, self.current_sems
        self.current, self.current_sems = ExitStack(), []

        def new(name):
            sem = self.current.enter_context(self.nc.semaphore(f"{tag}_{name}"))
            self.current_sems.append(sem)
            return sem

        return lambda name, per: Signal(new, name, per)

    def clear_spent(self, pool):
        for sem in self.spent_sems:
            pool.sem_clear(sem)


def sub_names(ctx, nc, stage):
    sb = lambda n, s, d=F32: ctx.enter_context(nc.sbuf_tensor(f"{stage}_{n}", s, d))
    ps = lambda n, s, d=F32: ctx.enter_context(nc.psum_tensor(f"{stage}_{n}", s, d))
    return sb, ps


def attention_stage(core, layer, heads, hd, scale, rope=False, mask=None, kan=False):
    nc, dram = core.nc, core.dram
    x_all, ident, gate, ones = core.x_all, core.ident, core.gates[:, layer:layer + 1], core.ones
    tag = f"a{layer}"
    DQ = heads * hd
    QC = DQ // P
    name = lambda n: f"L{layer}x_{n}"

    k_jobs = [("k", c) for c in range(QC)]
    if rope:
        k_jobs = [(kind, c) for c in range(QC) for kind in ("k", "kr")]
    v_width = min(DQ, 512)
    v_jobs = [("v", t, part) for t in range(KC) for part in range(DQ // v_width)]
    q_jobs = [("q", c) for c in range(0, QC, min(QC, 4))] + ([("qr", 0)] if rope else [])
    if kan:
        q_jobs.append(("qtok", 0))
    qn = min(QC, 4)
    jobs = k_jobs + v_jobs + [("xT", 0)] + q_jobs
    kv = k_jobs + v_jobs
    job_slot = {j: i * (heads - LEAD) // len(jobs) for i, j in enumerate(jobs)}
    index_of = {j: i for i, j in enumerate(jobs)}
    jobs_at = lambda n: [j for j in jobs if job_slot[j] == n]
    norm_slot = min(2, job_slot[("xT", 0)] - 1)
    on_scalar = lambda j: j[0] == "xT" or (j[0] == "v" and layer != 1) or (j[0] in ("k", "q") and not rope)

    VW = max(hd, 32)
    OC = heads * VW // P
    o_groups = -(-OC // 4)
    og_heads = heads // o_groups
    og_blocks = OC // o_groups

    with ExitStack() as ctx:
        sb, ps = sub_names(ctx, nc, tag)
        sig = core.new_signals(tag)

        wq = sb("wq", [P, DC, DQ])
        wk = sb("wk", [P, DC, DQ])
        wv = sb("wv", [P, DC, DQ])
        weights = [(wq, "wqT"), (wk, "wkT"), (wv, "wvT")]
        if rope:
            wqr, wkr = sb("wqr", [P, DC, DQ]), sb("wkr", [P, DC, DQ])
            weights += [(wqr, "wqrT"), (wkr, "wkrT")]
        small = []
        if layer != 1:
            bq, bk, bv = sb("bq", [P, QC]), sb("bk", [P, QC]), sb("bv", [P, OC])
            small += [(bq, "bq"), (bk, "bk"), (bv, "bv")]
        if rope:
            bqr, bkr = sb("bqr", [P, QC]), sb("bkr", [P, QC])
            cos, sin = sb("cos", [P, SK]), sb("sin", [P, SK])
            small += [(bqr, "bqr"), (bkr, "bkr"), (cos, "cos"), (sin, "sin")]
        if hd == 16:
            halves = sb("halves", [P, 2])
            small += [(halves, "halves")]
        if kan:
            lng, lnb = sb("lng", [P, DC]), sb("lnb", [P, DC])
            base_w = sb("base_w", [P, DC, D])
            spline_w = sb("spline_w", [P, DC, 8, D])
            scaler = sb("scaler", [P, DC, D])
            centers = sb("centers", [P, 8])
            bqrow, bvrow = sb("bqrow", [1, D]), sb("bvrow", [1, D])
            bqs = sb("bqs", [P, QC])
            small += [(lng, "ln_g"), (lnb, "ln_b"), (centers, "centers"), (bqrow, "bqrow"), (bvrow, "bvrow")]
            weights += [(base_w, "base_wT"), (spline_w, "spline_wT"), (scaler, "scalerT")]
        else:
            wo = sb("wo", [P, OC, D])
            borow = sb("borow", [1, D])
            weights += [(wo, "woT")]
            small += [(borow, "bo")]

        ctxT = sb("ctxT", [P, 2, DC, SK])
        stats, mv = sb("stats", [S, 6]), sb("mv", [S, 2])
        rstd = sb("rstd", [S, 1])
        xn = sb("xn", [S, D])
        xT = sb("xT", [P, DC, S])
        qT = sb("qT", [P, 2, 2 if hd == 16 else 1, QC, S])
        kT = sb("kT", [P, 2, QC, SK])
        v = sb("v", [KT, 2, KC, heads, VW])
        probs = sb("probs", [S, 4, SK])
        pT = sb("pT", [KT, 2, KC, S])
        negmax = sb("negmax", [S, heads])
        rowsum = sb("rowsum", [S, heads])
        rinv = sb("rinv", [S, heads])
        oT = sb("oT", [P, OC, S])
        if rope:
            rot_a, rot_b = sb("rot_a", [P, 2, SK]), sb("rot_b", [P, 2, SK])
            qrot_a, qrot_b = sb("qrot_a", [P, DC, S]), sb("qrot_b", [P, DC, S])
        if hd == 16:
            qfull = sb("qfull", [P, DC, S])
        if mask:
            masked = sb("masked", [S, 2, SK])
            if mask == "keys":
                mask_in = sb("mask_in", [S, 2, SK], U8)
                mask_add = sb("mask_add", [S, 2, SK])
            else:
                mask_in = sb("mask_in", [S, 1, SK], I32)
                mask_add = sb("mask_add", [S, 1, SK])
        if kan:
            qtok = sb("qtok", [S, 2, D])
            res = sb("res", [S, D])
            stats2, mv2, rstd2 = sb("stats2", [S, 6]), sb("mv2", [S, 2]), sb("rstd2", [S, 1])
            resn = sb("resn", [S, D])
            lnT = sb("lnT", [P, DC, S])
            silu = sb("silu", [P, DC, S])
            sexp = sb("sexp", [P, DC, S])
            dist = sb("dist", [P, DC, 8, S])
            near2, near1 = sb("near2", [P, DC, 8, S]), sb("near1", [P, DC, 8, S])
            sq2, sq1 = sb("sq2", [P, DC, 8, S]), sb("sq1", [P, DC, 8, S])

        sc_ps = ps("sc_ps", [S, 4, 512])
        pT_ps = ps("pT_ps", [P, 512])
        o_ps = ps("o_ps", [P, 512])
        job_ps = ps("job_ps", [P, 512])
        fin_ps = ps("fin_ps", [P, 512])

        s_w = sig("weights_in", 1)
        s_small = sig("small_in", 1)
        s_ctx = [sig(f"ctx_in{i}", 1) for i in range(2)]
        s_job = sig("job_ready", len(jobs))
        s_jobfree = sig("job_free", len(jobs))
        s_ln = sig("ln_steps", 3)
        s_pow = sig("rstd_ready", 1)
        s_xn = sig("xn_ready", 1)
        s_scores = sig("scores_ready", heads)
        s_max = sig("max_ready", heads)
        s_probs = sig("probs_ready", heads)
        s_pT = sig("pT_in_psum", heads)
        s_pTc = [sig(f"pT_copied{i}", heads // 2) for i in range(2)]
        s_pv = sig("pv_done", heads)
        s_rinv = sig("rinv_ready", heads)
        s_scaled = sig("probs_scaled", heads)
        s_o = sig("o_copied", o_groups)
        s_out = sig("output_done", 1)
        s_x = sig("x_updated", 1)
        s_zero = sig("v_zeroed", 1)
        s_tick = [sig(f"tick{i}", 0) for i in range(4)]
        if rope:
            s_ropek = sig("rope_k_ready", QC)
            s_rope_q = sig("rope_q_parts", 2 * DC)
            s_qsum = sig("q_summed", 1)
        s_qf = sig("q_chunks", QC)
        if hd == 16:
            s_q2 = sig("q_halves_ready", 2)
        if mask:
            s_mask = sig("mask_ready", 1)
            s_maskin = [sig(f"mask_in{i}", 1) for i in range(2)]
        if kan:
            s_setup = sig("setup", 1)
            s_k = sig("kan_dve", KAN_BASES + 1)
            s_ka = sig("kan_act", 6)
            s_pow2 = sig("rstd2_ready", 1)
            s_oback = sig("o_turned", 1)
            s_lnt = sig("ln_turned", 1)

        def job(j, b):
            return s_job.at(b, index_of[j])

        def ahead(b, par, n, lead):
            if n + lead < heads:
                return [(b, par, n + lead)]
            return [(b + 1, 1 - par, n + lead - heads)] if more(b) else []

        def v_of(par, t, part):
            h = v_width // hd
            return v[:, par, t, part * h:(part + 1) * h, 0:hd]

        def q_of(par, n):
            if hd == 16:
                r = 32 * ((n % 8) // 2)
                return qT[r:r + 32, par, n % 2, n // 8, :], r, 32, n // 8
            at = n * hd
            return qT[at % P:at % P + hd, par, 0, at // P, :], at % P, hd, at // P

        with nc.Block() as block:

            @block.sync
            def _(sp):
                for dst, what in small:
                    sp.dma_start(dst[:], dram[name(what)]).then_inc(s_small.sem, 16)
                if mask == "scores":
                    sp.dma_start(mask_in[:, 0, :], dram["mask_scores"]).then_inc(s_maskin[0].sem, 16)
                for dst, what in weights:
                    src = dram[name(what)]
                    sp.dma_start(dst[:], src).then_inc(s_w.sem, 16)

                def load(b, par, known):
                    if known:
                        sp.wait_ge(s_job.sem, job(kv[-1], b - 2))
                        sp.sem_inc(s_tick[2].sem, 1)
                    sp.dma_start(ctxT[:, par], dram["ctxT"][b]).then_inc(s_ctx[par].sem, 16)
                    if mask == "keys":
                        if known:
                            sp.wait_ge(s_mask.sem, s_mask.at(b - 2))
                            sp.sem_inc(s_tick[2].sem, 1)
                        sp.dma_start(mask_in[:, par, :], dram["mask_keys"][b].to_broadcast([S, SK])).then_inc(s_maskin[par].sem, 16)

                load(0, 0, False)
                load(1, 1, False)
                with sp.Fori(1, B // 2, 1) as j:
                    load(j * 2, 0, True)
                    load(j * 2 + 1, 1, True)

            def in_ctx(eng, b, par, sem=s_ctx):
                eng.wait_ge(sem[par].sem, half(b, par))

            @block.gpsimd
            def _(pool):
                core.clear_spent(pool)

                def power(b):
                    pool.wait_ge(s_ln.sem, s_ln.at(b, 2))
                    pool.tensor_tensor(rstd[:], rstd[:], core.minus_half[:], ALU.pow).then_inc(s_pow.sem, 1)

                def scale_probs(b, par, n):
                    pool.wait_ge(s_rinv.sem, s_rinv.at(b, n))
                    pool.sem_inc(s_tick[3].sem, 1)
                    pool.tensor_scalar(probs[:, n % 4, :], probs[:, n % 4, :], rinv[:, n:n + 1], None, ALU.mult)\
                        .then_inc(s_scaled.sem, 1)

                def kan_power(b):
                    pool.wait_ge(s_k.sem, s_k.at(b, KAN_VAR))
                    pool.tensor_tensor(rstd2[:], rstd2[:], core.minus_half[:], ALU.pow).then_inc(s_pow2.sem, 1)

                def body(b, par):
                    for n in range(heads):
                        for at in ahead(b, par, n, 1):
                            scale_probs(*at)
                        if n == 0 and more(b):
                            power(b + 1)
                        if kan and n == 1 and has(b, 1):
                            kan_power(b - 1)
                        for c in range(QC):
                            if rope and more(b) and job_slot[("kr", c)] == n:
                                rope_add(b + 1, 1 - par, c)

                def rope_add(b, par, c):
                    if has(b, 2):
                        pool.wait_ge(s_pv.sem, s_pv.at(b - 2, heads - 1))
                    for kind in ("k", "kr"):
                        pool.wait_ge(s_jobfree.sem, job((kind, c), b))
                    pool.tensor_tensor(kT[:, par, c, :], rot_a[:, c, :], rot_b[:, c, :], ALU.add)\
                        .then_inc(s_ropek.sem, 1)

                power(0)
                if rope:
                    for c in range(QC):
                        rope_add(0, 0, c)
                scale_probs(0, 0, 0)
                each(pool, body)
                if kan:
                    kan_power(B - 1)

            @block.tensor
            def _(pe):
                pe.wait_ge(s_w.sem, 16 * len(weights))
                pe.wait_ge(s_small.sem, 16 * len(small))
                if kan:
                    pe.wait_ge(s_setup.sem, 2 + DC)

                def run_job(j, b, par):
                    kind = j[0]
                    if has(b, 1) or index_of[j] > 0:
                        pe.wait_ge(s_jobfree.sem, job(j, b) - 1)
                    if j == jobs[0]:
                        in_ctx(pe, b, par)
                    if kind in ("k", "kr"):
                        w = wk if kind == "k" else wkr
                        for c in range(DC):
                            mm = pe.matmul(job_ps[:, 0:SK], w[:, c, j[1] * P:(j[1] + 1) * P],
                                           ctxT[:, par, c, :], start=(c == 0), stop=(c == DC - 1))
                    elif kind == "v":
                        _, t, part = j
                        for c in range(DC):
                            mm = pe.matmul(job_ps[0:KT, 0:v_width], ctxT[:, par, c, t * KT:(t + 1) * KT],
                                           wv[:, c, part * v_width:(part + 1) * v_width],
                                           start=(c == 0), stop=(c == DC - 1))
                    elif kind == "xT":
                        pe.wait_ge(s_xn.sem, s_xn.at(b))
                        for c in range(DC):
                            mm = pe.transpose(job_ps[:, c * S:(c + 1) * S], xn[:, c * P:(c + 1) * P],
                                              ident[0:S, 0:S])
                    elif kind in ("q", "qr"):
                        w = wq if kind == "q" else wqr
                        for i in range(qn):
                            f = j[1] + i
                            for c in range(DC):
                                mm = pe.matmul(job_ps[:, i * S:(i + 1) * S], w[:, c, f * P:(f + 1) * P],
                                               xT[:, c, :], start=(c == 0), stop=(c == DC - 1))
                    else:
                        for c in range(DC):
                            pe.matmul(job_ps[0:S, 0:D], xT[:, c, :], wq[:, c, :], start=(c == 0), stop=False)
                        pe.matmul(job_ps[0:S, 0:D], ones[0:1, 0:S], bqrow[:], start=False, stop=False)
                        mm = pe.matmul(job_ps[0:S, 0:D], ones[0:1, 0:S], bvrow[:], start=False, stop=True)
                    mm.then_inc(s_job.sem, 1)

                def scores(b, par, n):
                    if n == 0:
                        pe.wait_ge(s_jobfree.sem, s_jobfree.at(b, len(jobs) - 1))
                        if rope:
                            pe.wait_ge(s_ropek.sem, s_ropek.at(b, QC - 1))
                        if hd == 16:
                            pe.wait_ge(s_q2.sem, s_q2.at(b, 1))
                    free = s_max if mask else s_probs
                    if has(b, 1) or n >= 4:
                        pe.wait_ge(free.sem, free.at(b, n) - 4)
                    lhs, r, k, c = q_of(par, n)
                    pe.matmul(sc_ps[:, n % 4, 0:SK], lhs, kT[r:r + k, par, c, :], start=True, stop=True)\
                        .then_inc(s_scores.sem, 1)

                def transposes(b, n):
                    pe.wait_ge(s_scaled.sem, s_scaled.at(b, n))
                    if n > 0:
                        pe.wait_ge(s_pTc[(n - 1) % 2].sem, s_pTc[(n - 1) % 2].at(b, (n - 1) // 2))
                    elif has(b, 1):
                        pe.wait_ge(s_pTc[1].sem, s_pTc[1].at(b - 1, heads // 2 - 1))
                    for t in range(KC):
                        mm = pe.transpose(pT_ps[0:KT, t * S:(t + 1) * S],
                                          probs[:, n % 4, t * KT:(t + 1) * KT], ident[0:S, 0:S])
                    mm.then_inc(s_pT.sem, 1)

                def pv(b, par, n):
                    pe.wait_ge(s_pTc[n % 2].sem, s_pTc[n % 2].at(b, n // 2))
                    if n % og_heads == 0 and (has(b, 1) or n > 0):
                        pe.wait_ge(s_o.sem, s_o.at(b, n // og_heads) - 1)
                    r, w = n * VW % P, n * VW // P % 4 * S
                    for t in range(KC):
                        mm = pe.matmul(o_ps[r:r + VW, w:w + S], v[:, par, t, n, :], pT[:, n % 2, t, :],
                                       start=(t == 0), stop=(t == KC - 1))
                    mm.then_inc(s_pv.sem, 1)

                def output(b):
                    pe.wait_ge(s_o.sem, s_o.at(b, o_groups - 1))
                    if has(b, 1):
                        pe.wait_ge(s_x.sem, s_x.at(b - 1))
                    for c in range(OC):
                        pe.matmul(fin_ps[0:S, 0:D], oT[:, c, :], wo[:, c, :], start=(c == 0), stop=False)
                    pe.matmul(fin_ps[0:S, 0:D], ones[0:1, 0:S], borow[:], start=False, stop=True)\
                        .then_inc(s_out.sem, 1)

                def turn(src, b, signal):
                    for c in range(DC):
                        if signal is s_oback:
                            mm = pe.transpose(fin_ps[0:S, c * P:(c + 1) * P], src[:, c, :], ident[:, :])
                        else:
                            mm = pe.transpose(fin_ps[:, c * S:(c + 1) * S], src[:, c * P:(c + 1) * P], ident[0:S, 0:S])
                    mm.then_inc(signal.sem, 1)

                def kan_output(b):
                    pe.wait_ge(s_k.sem, s_k.at(b, KAN_BASES))
                    if more(b):
                        pe.wait_ge(s_k.sem, s_k.at(b + 1, KAN_RES))
                    for c in range(DC):
                        pe.matmul(fin_ps[0:S, 0:D], silu[:, c, :], base_w[:, c, :], start=(c == 0), stop=False)
                    for c in range(DC):
                        for i in range(8):
                            mm = pe.matmul(fin_ps[0:S, 0:D], dist[:, c, i, :], spline_w[:, c, i, :],
                                           start=False, stop=(c == DC - 1 and i == 7))
                    mm.then_inc(s_out.sem, 1)

                def finish(t, n):
                    if not kan:
                        if n == 1 and exists(t - 1):
                            output(t - 1)
                        return
                    if n == 1 and exists(t - 1):
                        pe.wait_ge(s_o.sem, s_o.at(t - 1))
                        if has(t, 2):
                            pe.wait_ge(s_k.sem, s_k.at(t - 2, KAN_LNT))
                        turn(oT, t - 1, s_oback)
                    if n == 2 and exists(t - 2):
                        kan_output(t - 2)
                    if n == 3 and exists(t - 1):
                        pe.wait_ge(s_k.sem, s_k.at(t - 1, KAN_RESN))
                        if has(t, 2):
                            pe.wait_ge(s_x.sem, s_x.at(t - 2))
                        turn(resn, t - 1, s_lnt)

                def body(b, par):
                    for n in range(heads):
                        for at in ahead(b, par, n, LEAD):
                            scores(*at)
                        todo = jobs_at(n) if more(b) else []
                        for j in todo[:1]:
                            run_job(j, b + 1, 1 - par)
                        transposes(b, n)
                        if n > 0:
                            pv(b, par, n - 1)
                        elif has(b, 1):
                            pv(b - 1, 1 - par, heads - 1)
                        for j in todo[1:]:
                            run_job(j, b + 1, 1 - par)
                        finish(b, n)

                if hd == 16:
                    pe.wait_ge(s_zero.sem, 1)
                for j in jobs:
                    run_job(j, 0, 0)
                for n in range(LEAD):
                    scores(0, 0, n)
                each(pe, body)
                pv(B - 1, 1, heads - 1)
                for t in range(B, B + 2):
                    for n in range(heads):
                        finish(t, n)

            @block.scalar
            def _(act):
                act.wait_ge(s_small.sem, 16 * len(small))

                def copy_job(j, b, par):
                    kind = j[0]
                    if not on_scalar(j):
                        return
                    if kind in ("v", "k", "q") and has(b, 2):
                        act.wait_ge(s_pv.sem, s_pv.at(b - 2, heads - 1))
                    act.wait_ge(s_job.sem, job(j, b))
                    free = s_jobfree.sem
                    if kind == "k":
                        f = j[1]
                        act.activation(kT[:, par, f, :], job_ps[:, 0:SK], ACT.Identity,
                                       bias=bk[:, f:f + 1] if layer != 1 else 0.0).then_inc(free, 1)
                    elif kind == "v":
                        _, t, part = j
                        if hd == 16 and isinstance(b, int) and b < 2:
                            act.wait_ge(s_zero.sem, 1)
                        act.activation(v_of(par, t, part), job_ps[0:KT, 0:v_width].rearrange("p (h d) -> p h d", d=hd),
                                       ACT.Copy).then_inc(free, 1)
                    elif kind == "xT":
                        act.activation(xT[:, :, :], job_ps[:, 0:DC * S].rearrange("p (c s) -> p c s", c=DC),
                                       ACT.Copy).then_inc(free, 1)
                    elif kind == "q" and layer == 1:
                        act.activation(qT[:, par, 0, j[1]:j[1] + qn, :],
                                       job_ps[:, 0:qn * S].rearrange("p (c s) -> p c s", c=qn),
                                       ACT.Copy, scale=scale).then_inc(free, 1)
                    elif kind == "q" and hd == 16:
                        if has(b, 1):
                            act.wait_ge(s_q2.sem, s_q2.at(b - 1, 1))
                        for c in range(QC):
                            ins = act.activation(qfull[:, c, :], job_ps[:, c * S:(c + 1) * S], ACT.Identity,
                                                 bias=bq[:, c:c + 1])
                            ins.then_inc(s_qf.sem, 1)
                        act.wait_ge(s_qf.sem, s_qf.at(b, QC - 1))
                        act.sem_inc(free, 1)
                    elif kind == "q":
                        for c in range(QC):
                            act.activation(qT[:, par, 0, c, :], job_ps[:, c * S:(c + 1) * S], ACT.Identity,
                                           scale=scale, bias=bqs[:, c:c + 1]).then_inc(s_qf.sem, 1)
                        act.wait_ge(s_qf.sem, s_qf.at(b, QC - 1))
                        act.sem_inc(free, 1)

                def exps(b, par, n):
                    act.wait_ge(s_max.sem, s_max.at(b, n))
                    if has(b, 1) or n >= 4:
                        act.wait_ge(s_pT.sem, s_pT.at(b, n) - 4)
                    src = masked[:, n % 2, :] if mask else sc_ps[:, n % 4, 0:SK]
                    act.activation(probs[:, n % 4, :], src, ACT.Exp, bias=negmax[:, n:n + 1],
                                   scale=-1.0 if mask else 1.0,
                                   accum_out=rowsum[:, n:n + 1]).then_inc(s_probs.sem, 1)

                def copy_pT(b, n):
                    act.wait_ge(s_pT.sem, s_pT.at(b, n))
                    if has(b, 1) or n >= 2:
                        act.wait_ge(s_pv.sem, s_pv.at(b, n) - 2)
                    act.activation(pT[:, n % 2, :, :], pT_ps[0:KT, 0:KC * S].rearrange("p (c s) -> p c s", c=KC),
                                   ACT.Copy).then_inc(s_pTc[n % 2].sem, 1)

                def copy_oT(b, g):
                    act.wait_ge(s_pv.sem, s_pv.at(b, (g + 1) * og_heads - 1))
                    if has(b, 1):
                        used = s_oback if kan else s_out
                        act.wait_ge(used.sem, used.at(b - 1))
                    act.activation(oT[:, g * og_blocks:(g + 1) * og_blocks, :],
                                   o_ps[:, 0:og_blocks * S].rearrange("p (c s) -> p c s", c=og_blocks),
                                   ACT.Copy).then_inc(s_o.sem, 1)

                def kan_step(b, n):
                    flat = lambda t: t[:].rearrange("p c i s -> p (c i s)")
                    if n == 4:
                        act.wait_ge(s_k.sem, s_k.at(b, KAN_LNT))
                        act.activation(sexp[:], lnT[:], ACT.Exp, scale=-1.0).then_inc(s_ka.sem, 1)
                        act.wait_ge(s_k.sem, s_k.at(b, KAN_DIST))
                        act.activation(flat(dist), flat(dist), ACT.Abs).then_inc(s_ka.sem, 1)
                    if n == 5:
                        act.wait_ge(s_ka.sem, s_ka.at(b, 1))
                        act.activation(flat(near2), flat(dist), ACT.Relu, scale=-1.0, bias=2.0).then_inc(s_ka.sem, 1)
                        act.activation(flat(near1), flat(dist), ACT.Relu, scale=-1.0, bias=1.0).then_inc(s_ka.sem, 1)
                    if n == 6:
                        act.wait_ge(s_ka.sem, s_ka.at(b, 2))
                        act.activation(flat(sq2), flat(near2), ACT.Square).then_inc(s_ka.sem, 1)
                        act.wait_ge(s_ka.sem, s_ka.at(b, 3))
                        act.activation(flat(sq1), flat(near1), ACT.Square).then_inc(s_ka.sem, 1)

                def body(b, par):
                    for n in range(heads):
                        for at in ahead(b, par, n, 2):
                            exps(*at)
                        todo = jobs_at(n) if more(b) else []
                        for j in todo[:1]:
                            copy_job(j, b + 1, 1 - par)
                        if n % 2 == 0:
                            copy_pT(b, n)
                        if n == 0 and has(b, 1) and hd != 16:
                            copy_oT(b - 1, o_groups - 1)
                        if kan and has(b, 1):
                            kan_step(b - 1, n)
                        if o_groups == 2 and n == og_heads:
                            copy_oT(b, 0)
                        for j in todo[1:]:
                            copy_job(j, b + 1, 1 - par)

                if kan:
                    act.wait_ge(s_setup.sem, 2 + DC)
                for j in jobs:
                    copy_job(j, 0, 0)
                exps(0, 0, 0)
                exps(0, 0, 1)
                each(act, body)
                if hd != 16:
                    copy_oT(B - 1, o_groups - 1)
                if kan:
                    for n in range(heads):
                        kan_step(B - 1, n)

            @block.vector
            def _(dve):
                dve.wait_ge(s_small.sem, 16 * len(small))

                def hold(sem, value):
                    dve.wait_ge(sem, value)
                    dve.sem_inc(s_tick[1].sem, 1)

                if hd == 16:
                    dve.memset(v[:], 0.0).then_inc(s_zero.sem, 1)
                if mask == "scores":
                    dve.wait_ge(s_maskin[0].sem, 16)
                    dve.tensor_scalar(mask_add[:, 0, :], mask_in[:, 0, :], -1e15, None, ALU.mult)\
                        .then_inc(s_mask.sem, 1)
                    dve.wait_ge(s_mask.sem, 1)
                if kan:
                    dve.wait_ge(s_w.sem, 16 * len(weights))
                    dve.tensor_scalar(bqs[:], bq[:], scale, None, ALU.mult).then_inc(s_setup.sem, 1)
                    dve.tensor_scalar(scaler[:], scaler[:], 1.0 / 6.0, None, ALU.mult).then_inc(s_setup.sem, 1)
                    dve.wait_ge(s_setup.sem, 2)
                    for c in range(DC):
                        dve.tensor_tensor(spline_w[:, c], spline_w[:, c],
                                          scaler[:, c, :].unsqueeze(1).to_broadcast([P, 8, D]),
                                          ALU.mult).then_inc(s_setup.sem, 1)

                def norm_stats(b):
                    dve.bn_stats(stats[:], x_all[:, b, :]).then_inc(s_ln.sem, 1)
                    hold(s_ln.sem, s_ln.at(b, 0))
                    dve.bn_aggr(mv[:], stats[:]).then_inc(s_ln.sem, 1)
                    dve.wait_ge(s_ln.sem, s_ln.at(b, 1))
                    dve.tensor_scalar(rstd[:], mv[:, 1:2], EPS, None, ALU.add).then_inc(s_ln.sem, 1)

                def norm_apply(b):
                    dve.wait_ge(s_pow.sem, s_pow.at(b))
                    if has(b, 1):
                        dve.wait_ge(s_job.sem, job(("xT", 0), b - 1))
                    dve.tensor_scalar(xn[:], x_all[:, b, :], mv[:, 0:1], rstd[:, 0:1], ALU.subtract, ALU.mult)\
                        .then_inc(s_xn.sem, 1)

                def make_mask(b, par):
                    in_ctx(dve, b, par, s_maskin)
                    if has(b, 2):
                        dve.wait_ge(s_max.sem, s_max.at(b - 2, heads - 1))
                    dve.tensor_scalar(mask_add[:, par, :], mask_in[:, par, :], 1.0, FLT_MAX, ALU.subtract, ALU.mult)\
                        .then_inc(s_mask.sem, 1)

                def copy_job(j, b, par):
                    kind = j[0]
                    if on_scalar(j):
                        return
                    dve.wait_ge(s_job.sem, job(j, b))
                    free = s_jobfree.sem
                    if kind in ("k", "kr"):
                        f = j[1]
                        if has(b, 1):
                            dve.wait_ge(s_ropek.sem, s_ropek.at(b - 1, f))
                        dst, bias, table = (rot_a, bk, cos) if kind == "k" else (rot_b, bkr, sin)
                        dve.scalar_tensor_tensor(out=dst[:, f, :], in0=job_ps[:, 0:SK], scalar=bias[:, f:f + 1],
                                                 in1=table[:], op0=ALU.add, op1=ALU.mult).then_inc(free, 1)
                    elif kind in ("q", "qr"):
                        if has(b, 1):
                            dve.wait_ge(s_qsum.sem, s_qsum.at(b - 1))
                        dst, bias, table = (qrot_a, bq, cos) if kind == "q" else (qrot_b, bqr, sin)
                        for c in range(DC):
                            dve.scalar_tensor_tensor(out=dst[:, c, :], in0=job_ps[:, c * S:(c + 1) * S],
                                                     scalar=bias[:, c:c + 1], in1=table[:, 0:S], op0=ALU.add,
                                                     op1=ALU.mult).then_inc(s_rope_q.sem, 1)
                        dve.wait_ge(s_rope_q.sem, s_rope_q.at(b, (kind == "qr") * DC + DC - 1))
                        dve.sem_inc(free, 1)
                    elif kind == "v":
                        if has(b, 2):
                            dve.wait_ge(s_pv.sem, s_pv.at(b - 2, heads - 1))
                        _, t, part = j
                        dve.tensor_copy(v_of(par, t, part), job_ps[0:KT, 0:v_width].rearrange("p (h d) -> p h d", d=hd))\
                            .then_inc(free, 1)
                    elif kind == "qtok":
                        if has(b, 2):
                            dve.wait_ge(s_k.sem, s_k.at(b - 2, KAN_RES))
                        dve.tensor_copy(qtok[:, par, :], job_ps[0:S, 0:D]).then_inc(free, 1)

                def halve_q(b, par):
                    if rope:
                        dve.wait_ge(s_rope_q.sem, s_rope_q.at(b, 2 * DC - 1))
                        if has(b, 1):
                            dve.wait_ge(s_q2.sem, s_q2.at(b - 1, 1))
                        dve.tensor_tensor(qfull[:], qrot_a[:], qrot_b[:], ALU.add).then_inc(s_qsum.sem, 1)
                        dve.wait_ge(s_qsum.sem, s_qsum.at(b))
                    else:
                        dve.wait_ge(s_qf.sem, s_qf.at(b, QC - 1))
                    if has(b, 2):
                        dve.wait_ge(s_pv.sem, s_pv.at(b - 2, heads - 1))
                    for i in range(2):
                        dve.tensor_scalar(qT[:, par, i], qfull[:], halves[:, i:i + 1], None, ALU.mult)\
                            .then_inc(s_q2.sem, 1)

                def row_max(b, par, n):
                    dve.wait_ge(s_scores.sem, s_scores.at(b, n))
                    if has(b, 1) and not mask:
                        dve.wait_ge(s_probs.sem, s_probs.at(b - 1, n))
                    if mask:
                        if n == 0 and mask == "keys":
                            dve.wait_ge(s_mask.sem, s_mask.at(b))
                        if has(b, 1) or n >= 2:
                            dve.wait_ge(s_probs.sem, s_probs.at(b, n) - 2)
                        dve.sem_inc(s_tick[1].sem, 1)
                        m = mask_add[:, par if mask == "keys" else 0, :]
                        dve.tensor_tensor_reduce(out=masked[:, n % 2, :], in0=sc_ps[:, n % 4, 0:SK], in1=m,
                                                 scale=-1.0, scalar=FLT_MAX, op0=ALU.add, op1=ALU.min,
                                                 accum_out=negmax[:, n:n + 1]).then_inc(s_max.sem, 1)
                    else:
                        dve.tensor_reduce(negmax[:, n:n + 1], sc_ps[:, n % 4, 0:SK], AX.X, ALU.max, negate=True)\
                            .then_inc(s_max.sem, 1)

                def copy_pT(b, n):
                    dve.wait_ge(s_pT.sem, s_pT.at(b, n))
                    if has(b, 1) or n >= 2:
                        dve.wait_ge(s_pv.sem, s_pv.at(b, n) - 2)
                    dve.tensor_copy(pT[:, n % 2, :, :], pT_ps[0:KT, 0:KC * S].rearrange("p (c s) -> p c s", c=KC))\
                        .then_inc(s_pTc[n % 2].sem, 1)

                def invert(b, par, n):
                    dve.wait_ge(s_probs.sem, s_probs.at(b, n))
                    dve.reciprocal(rinv[:, n:n + 1], rowsum[:, n:n + 1]).then_inc(s_rinv.sem, 1)

                def copy_oT(b):
                    dve.wait_ge(s_pv.sem, s_pv.at(b, heads - 1))
                    if has(b, 1):
                        dve.wait_ge(s_out.sem, s_out.at(b - 1))
                    dve.tensor_tensor(oT[:], o_ps[:, 0:OC * S].rearrange("p (c s) -> p c s", c=OC),
                                      bv[:].unsqueeze(2).to_broadcast([P, OC, S]), ALU.add).then_inc(s_o.sem, 1)

                def update(b):
                    dve.wait_ge(s_out.sem, s_out.at(b))
                    dve.scalar_tensor_tensor(out=x_all[:, b, :], in0=fin_ps[0:S, 0:D], scalar=gate,
                                             in1=x_all[:, b, :], op0=ALU.mult, op1=ALU.add).then_inc(s_x.sem, 1)

                def kan_step(b, par, n):
                    def done(ins, k):
                        ins.then_inc(s_k.sem, 1)
                        hold(s_k.sem, s_k.at(b, k))
                    flat = lambda t: t[:].rearrange("p c i s -> p (c i s)")
                    if n == 1:
                        dve.wait_ge(s_oback.sem, s_oback.at(b))
                        done(dve.tensor_tensor(res[:], fin_ps[0:S, 0:D], qtok[:, par, :], ALU.add), KAN_RES)
                        done(dve.bn_stats(stats2[:], res[:]), KAN_RES + 1)
                        done(dve.bn_aggr(mv2[:], stats2[:]), KAN_RES + 2)
                        done(dve.tensor_scalar(rstd2[:], mv2[:, 1:2], EPS, None, ALU.add), KAN_VAR)
                    if n == 2:
                        dve.wait_ge(s_pow2.sem, s_pow2.at(b))
                        done(dve.tensor_scalar(resn[:], res[:], mv2[:, 0:1], rstd2[:, 0:1], ALU.subtract, ALU.mult),
                             KAN_RESN)
                    if n == 3:
                        dve.wait_ge(s_lnt.sem, s_lnt.at(b))
                        for c in range(DC):
                            done(dve.tensor_scalar(lnT[:, c, :], fin_ps[:, c * S:(c + 1) * S], lng[:, c:c + 1],
                                                   lnb[:, c:c + 1], ALU.mult, ALU.add), KAN_RESN + 1 + c)
                        for c in range(DC):
                            done(dve.scalar_tensor_tensor(
                                out=dist[:, c], in0=lnT[:, c, :].unsqueeze(1).to_broadcast([P, 8, S]), scalar=2.5,
                                in1=centers[:].unsqueeze(2).to_broadcast([P, 8, S]),
                                op0=ALU.mult, op1=ALU.subtract), KAN_LNT + 1 + c)
                    if n == 5:
                        dve.wait_ge(s_ka.sem, s_ka.at(b, 0))
                        done(dve.tensor_scalar(sexp[:], sexp[:], 1.0, None, ALU.add), KAN_DIST + 1)
                        done(dve.reciprocal(sexp[:], sexp[:]), KAN_DIST + 2)
                        done(dve.tensor_tensor(silu[:], lnT[:], sexp[:], ALU.mult), KAN_SILU)
                    if n == 6:
                        dve.wait_ge(s_ka.sem, s_ka.at(b, 4))
                        done(dve.tensor_tensor(flat(near2), flat(sq2), flat(near2), ALU.mult), KAN_SILU + 1)
                        dve.wait_ge(s_ka.sem, s_ka.at(b, 5))
                        done(dve.scalar_tensor_tensor(out=flat(near1), in0=flat(sq1), scalar=-4.0, in1=flat(near1),
                                                      op0=ALU.mult, op1=ALU.mult), KAN_SILU + 2)
                        done(dve.tensor_tensor(flat(dist), flat(near2), flat(near1), ALU.add), KAN_BASES)

                def finish(t, n, par):
                    if hd == 16 and n == 0 and exists(t - 1):
                        copy_oT(t - 1)
                    if not kan and n == 2 and exists(t - 1):
                        update(t - 1)
                    if kan and n == 3 and exists(t - 2):
                        update(t - 2)
                    if kan and exists(t - 1):
                        kan_step(t - 1, 1 - par, n)

                def body(b, par):
                    for n in range(heads):
                        for at in ahead(b, par, n, 1):
                            invert(*at)
                        for at in ahead(b, par, n, LEAD):
                            row_max(*at)
                        todo = jobs_at(n) if more(b) else []
                        for j in todo[:1]:
                            copy_job(j, b + 1, 1 - par)
                        if n % 2 == 1:
                            copy_pT(b, n)
                        finish(b, n, par)
                        if more(b):
                            if n == 0:
                                norm_stats(b + 1)
                            if n == norm_slot:
                                norm_apply(b + 1)
                                if mask == "keys":
                                    make_mask(b + 1, 1 - par)
                            for j in todo[1:]:
                                copy_job(j, b + 1, 1 - par)
                            if n == job_slot[jobs[-1]] and hd == 16:
                                halve_q(b + 1, 1 - par)

                norm_stats(0)
                norm_apply(0)
                if mask == "keys":
                    make_mask(0, 0)
                for j in jobs:
                    copy_job(j, 0, 0)
                if hd == 16:
                    halve_q(0, 0)
                for n in range(LEAD):
                    row_max(0, 0, n)
                    if n == 0:
                        invert(0, 0, 0)
                each(dve, body)
                for t in range(B, B + 2):
                    for n in range(heads):
                        finish(t, n, t % 2)


def setup_stage(core):
    nc = core.nc
    s_in = core.stack.enter_context(nc.semaphore("x_in"))
    s_g = core.stack.enter_context(nc.semaphore("gates_in"))
    s_one = core.stack.enter_context(nc.semaphore("ones_ready"))
    with nc.Block() as block:
        @block.sync
        def _(sp):
            sp.dma_start(core.gates[:], core.dram["gates"].to_broadcast([S, 8])).then_inc(s_g, 16)
            sp.dma_start(core.ident[:], core.dram["ident"]).then_inc(s_in, 16)
            sp.dma_start(core.x_all[:], core.dram["x"].rearrange("b s d -> s b d")).then_inc(s_in, 16)
            sp.wait_ge(s_in, 32)

        @block.scalar
        def _(act):
            act.wait_ge(s_g, 16)
            act.activation(core.gates[:], core.gates[:], ACT.Tanh).then_inc(s_g, 1)
            act.wait_ge(s_g, 17)

        @block.vector
        def _(dve):
            dve.memset(core.ones[:], 1.0).then_inc(s_one, 1)
            dve.memset(core.minus_half[:], -0.5).then_inc(s_one, 1)
            dve.wait_ge(s_one, 2)


def tree_stage(core):
    nc, dram, x_all, ident, ones = core.nc, core.dram, core.x_all, core.ident, core.ones
    gate = core.gates[:, 4:5]
    LEVELS = 8
    M = 2 ** LEVELS
    with ExitStack() as ctx:
        sb, ps = sub_names(ctx, nc, "f0")
        sig = core.new_signals("f0")
        wq, routers = sb("wq", [P, DC, D]), sb("routers", [P, DC, M - 1])
        leaves, wout, bout = sb("leaves", [P, DC, D]), sb("wout", [P, DC, D]), sb("bout", [1, D])
        loads = [(wq, "L0f_wqT"), (routers, "L0f_routersT"), (leaves, "L0f_leaves"), (wout, "L0f_woutT"),
                 (bout, "L0f_bout")]
        stats, mv, rstd, xn = sb("stats", [S, 6]), sb("mv", [S, 2]), sb("rstd", [S, 1]), sb("xn", [S, D])
        xT, qT = sb("xT", [P, DC, S]), sb("qT", [P, DC, S])
        right, left = sb("right", [S, M - 1]), sb("left", [S, M - 1])
        paths = [sb(f"paths{l}", [S, 2 ** (l + 1)]) for l in range(LEVELS)]
        leafT, retT = sb("leafT", [P, DC, S]), sb("retT", [P, DC, S])
        x_ps, q_ps, r_ps = ps("x_ps", [P, 512]), ps("q_ps", [P, 512]), ps("r_ps", [S, 512])
        l_ps, v_ps, y_ps = ps("l_ps", [P, 512]), ps("v_ps", [P, 512]), ps("y_ps", [S, 512])
        s_w = sig("weights_in", 1)
        s_ln, s_pow, s_xn = sig("ln_steps", 3), sig("rstd_ready", 1), sig("xn_ready", 1)
        s_xps, s_xT, s_qps, s_qT = sig("x_turned", 1), sig("xT_ready", 1), sig("q_ready", 1), sig("qT_ready", 1)
        s_rps, s_right, s_tree = sig("routers_done", 1), sig("right_ready", 1), sig("tree_steps", 1 + 2 * LEVELS)
        s_lps, s_leafT = sig("leaves_turned", 1), sig("leafT_ready", 1)
        s_vps, s_retT, s_yps, s_y = sig("values_done", 1), sig("retT_ready", 1), sig("out_done", 1), sig("x_updated", 1)
        s_tick = sig("tick", 0)

        def turns(eng, front, middle, back):
            front(0)
            middle(0)
            front(1)

            def turn(b):
                back(b - 2)
                middle(b - 1)
                front(b)

            with eng.Fori(2, B, 1) as b:
                turn(b)
            back(B - 2)
            middle(B - 1)
            back(B - 1)

        with nc.Block() as block:
            @block.sync
            def _(sp):
                for dst, what in loads:
                    sp.dma_start(dst[:], dram[what]).then_inc(s_w.sem, 16)

            @block.gpsimd
            def _(pool):
                core.clear_spent(pool)
                with pool.Fori(0, B, 1) as b:
                    pool.wait_ge(s_ln.sem, s_ln.at(b, 2))
                    pool.tensor_tensor(rstd[:], rstd[:], core.minus_half[:], ALU.pow).then_inc(s_pow.sem, 1)

            @block.tensor
            def _(pe):
                pe.wait_ge(s_w.sem, 16 * len(loads))

                def front(b):
                    pe.wait_ge(s_xn.sem, s_xn.at(b))
                    if has(b, 1):
                        pe.wait_ge(s_xT.sem, s_xT.at(b - 1))
                    for c in range(DC):
                        mm = pe.transpose(x_ps[:, c * S:(c + 1) * S], xn[:, c * P:(c + 1) * P], ident[0:S, 0:S])
                    mm.then_inc(s_xps.sem, 1)
                    pe.wait_ge(s_xT.sem, s_xT.at(b))
                    if has(b, 1):
                        pe.wait_ge(s_qT.sem, s_qT.at(b - 1))
                    for f in range(DC):
                        for c in range(DC):
                            mm = pe.matmul(q_ps[:, f * S:(f + 1) * S], wq[:, c, f * P:(f + 1) * P], xT[:, c, :],
                                           start=(c == 0), stop=(c == DC - 1))
                    mm.then_inc(s_qps.sem, 1)

                def middle(b):
                    pe.wait_ge(s_qT.sem, s_qT.at(b))
                    if has(b, 1):
                        pe.wait_ge(s_right.sem, s_right.at(b - 1))
                    for c in range(DC):
                        mm = pe.matmul(r_ps[:, 0:M - 1], qT[:, c, :], routers[:, c, :], start=(c == 0),
                                       stop=(c == DC - 1))
                    mm.then_inc(s_rps.sem, 1)

                def back(b):
                    pe.wait_ge(s_tree.sem, s_tree.at(b, 2 * LEVELS))
                    if has(b, 1):
                        pe.wait_ge(s_leafT.sem, s_leafT.at(b - 1))
                    for c in range(DC):
                        mm = pe.transpose(l_ps[:, c * S:(c + 1) * S], paths[-1][:, c * P:(c + 1) * P],
                                          ident[0:S, 0:S])
                    mm.then_inc(s_lps.sem, 1)
                    pe.wait_ge(s_leafT.sem, s_leafT.at(b))
                    if has(b, 1):
                        pe.wait_ge(s_retT.sem, s_retT.at(b - 1))
                    for f in range(DC):
                        for c in range(DC):
                            mm = pe.matmul(v_ps[:, f * S:(f + 1) * S], leaves[:, c, f * P:(f + 1) * P],
                                           leafT[:, c, :], start=(c == 0), stop=(c == DC - 1))
                    mm.then_inc(s_vps.sem, 1)
                    pe.wait_ge(s_retT.sem, s_retT.at(b))
                    if has(b, 1):
                        pe.wait_ge(s_y.sem, s_y.at(b - 1))
                    for c in range(DC):
                        pe.matmul(y_ps[:, 0:D], retT[:, c, :], wout[:, c, :], start=(c == 0), stop=False)
                    pe.matmul(y_ps[:, 0:D], ones[0:1, 0:S], bout[:], start=False, stop=True).then_inc(s_yps.sem, 1)

                turns(pe, front, middle, back)

            @block.scalar
            def _(act):
                turned = lambda t: t[:, 0:DC * S].rearrange("p (c s) -> p c s", c=DC)

                def front(b):
                    act.wait_ge(s_xps.sem, s_xps.at(b))
                    if has(b, 1):
                        act.wait_ge(s_qps.sem, s_qps.at(b - 1))
                    act.activation(xT[:], turned(x_ps), ACT.Copy).then_inc(s_xT.sem, 1)
                    act.wait_ge(s_qps.sem, s_qps.at(b))
                    if has(b, 1):
                        act.wait_ge(s_rps.sem, s_rps.at(b - 1))
                    act.activation(qT[:], turned(q_ps), ACT.Copy).then_inc(s_qT.sem, 1)

                def middle(b):
                    act.wait_ge(s_rps.sem, s_rps.at(b))
                    if has(b, 1):
                        act.wait_ge(s_tree.sem, s_tree.at(b - 1, 2 * LEVELS))
                    act.activation(right[:], r_ps[:, 0:M - 1], ACT.Sigmoid).then_inc(s_right.sem, 1)

                def back(b):
                    act.wait_ge(s_lps.sem, s_lps.at(b))
                    if has(b, 1):
                        act.wait_ge(s_vps.sem, s_vps.at(b - 1))
                    act.activation(leafT[:], turned(l_ps), ACT.Copy).then_inc(s_leafT.sem, 1)
                    act.wait_ge(s_vps.sem, s_vps.at(b))
                    if has(b, 1):
                        act.wait_ge(s_yps.sem, s_yps.at(b - 1))
                    act.activation(retT[:], turned(v_ps), ACT.Copy).then_inc(s_retT.sem, 1)

                turns(act, front, middle, back)

            @block.vector
            def _(dve):
                def hold(sem, value):
                    dve.wait_ge(sem, value)
                    dve.sem_inc(s_tick.sem, 1)

                def front(b):
                    dve.bn_stats(stats[:], x_all[:, b, :]).then_inc(s_ln.sem, 1)
                    hold(s_ln.sem, s_ln.at(b, 0))
                    dve.bn_aggr(mv[:], stats[:]).then_inc(s_ln.sem, 1)
                    dve.wait_ge(s_ln.sem, s_ln.at(b, 1))
                    dve.tensor_scalar(rstd[:], mv[:, 1:2], EPS, None, ALU.add).then_inc(s_ln.sem, 1)
                    dve.wait_ge(s_pow.sem, s_pow.at(b))
                    if has(b, 1):
                        dve.wait_ge(s_xps.sem, s_xps.at(b - 1))
                    dve.tensor_scalar(xn[:], x_all[:, b, :], mv[:, 0:1], rstd[:, 0:1], ALU.subtract, ALU.mult)\
                        .then_inc(s_xn.sem, 1)

                def middle(b):
                    dve.wait_ge(s_right.sem, s_right.at(b))
                    dve.tensor_scalar(left[:], right[:], -1.0, 1.0, ALU.mult, ALU.add).then_inc(s_tree.sem, 1)
                    for level in range(LEVELS):
                        n = 2 ** level
                        pair = paths[level][:].rearrange("s (n two) -> s n two", two=2)
                        dve.wait_ge(s_tree.sem, s_tree.at(b, 2 * level))
                        if level == LEVELS - 1 and has(b, 1):
                            dve.wait_ge(s_lps.sem, s_lps.at(b - 1))
                        for side, prob in enumerate((left, right)):
                            g = prob[:, n - 1:2 * n - 1]
                            if level == 0:
                                dve.tensor_copy(paths[0][:, side:side + 1], g).then_inc(s_tree.sem, 1)
                            else:
                                dve.tensor_tensor(pair[:, :, side], paths[level - 1][:], g, ALU.mult)\
                                    .then_inc(s_tree.sem, 1)

                def back(b):
                    dve.wait_ge(s_yps.sem, s_yps.at(b))
                    dve.scalar_tensor_tensor(out=x_all[:, b, :], in0=y_ps[:, 0:D], scalar=gate, in1=x_all[:, b, :],
                                             op0=ALU.mult, op1=ALU.add).then_inc(s_y.sem, 1)

                turns(dve, front, middle, back)


class Plan:

    SLOTS = 256
    PAIRS = 2 * B * S

    def __init__(self, core, ctx, layer, E):
        self.E, self.SC = E, self.SLOTS // P
        self.tiles = (self.PAIRS + E * (self.SLOTS - 1)) // self.SLOTS
        sb = lambda n, s, d=F32: ctx.enter_context(core.nc.sbuf_tensor(f"p{layer}_{n}", s, d))
        self.xn = sb("xn", [S, B, D])
        self.slot = sb("slot", [S, 2 * B], mybir.dt.uint32)
        self.share = sb("share", [S, B, 2])
        self.expert = sb("expert", [1, self.tiles], I32)
        dram = lambda n: core.nc.dram_tensor(f"p{layer}_{n}", (self.tiles * self.SLOTS, D), F32, kind="Internal").ap()
        self.rows_in, self.rows_out = dram("rows_in"), dram("rows_out")


def route_stage(core, layer, E, xT_all=None, mix=None, plan=None):
    nc, dram, x_all, ident, ones = core.nc, core.dram, core.x_all, core.ident, core.ones
    tag = f"r{layer}"
    name = lambda n: f"L{layer}f_{n}"
    gate = core.gates[:, 4 + layer:5 + layer]
    dense = plan is None
    RMS_EPS = float(np.finfo(np.float32).eps)
    with ExitStack() as ctx:
        sb, ps = sub_names(ctx, nc, tag)
        sig = core.new_signals(tag)
        wg = sb("wg", [P, DC, E])
        loads = [(wg[:], dram[name("gateT")])]
        if dense:
            cents = sb("cents", [8, D])
            b2 = sb("b2", [E, D])
            loads += [(cents[:], dram[name("centroids")]), (b2[:], dram[name("b2")])]
            sq, norm, cn = sb("sq", [S, D]), sb("norm", [S, 2, 1]), sb("cn", [8, D])
            cnT = sb("cnT", [P, DC, 8])
            pick = sb("pick", [S, B, E])
            mixT = sb("mixT", [E, 2, S])
        else:
            T, LIMITS = plan.tiles, -(-B * S // plan.SLOTS)
            bg = sb("bg", [1, E])
            number, below = sb("number", [S, E]), sb("below", [S, S])
            limits, before, tile_no = sb("limits", [S, LIMITS]), sb("before", [S, E, E]), sb("tile_no", [1, T])
            loads += [(bg[:], dram[name("gate_bias")]), (number[:], dram[f"numbers{E}"].to_broadcast([S, E])),
                      (below[:], dram["below"]), (limits[:], dram["limits"].to_broadcast([S, LIMITS])),
                      (before[:].rearrange("p e f -> p (e f)"), dram[f"before{E}"].to_broadcast([S, E * E])),
                      (tile_no[:], dram[f"tile_no{E}"])]
            if layer == 2:
                ln_w = sb("ln_w", [P, DC])
                loads.append((ln_w[:], dram[name("ln_w")]))
            share = plan.share
            at, place = sb("at", [S, B, 8], mybir.dt.uint32), sb("place", [S, B, 8])
            every_one = sb("every_one", [S, S])
            chosen = sb("chosen", [S, 2, B, E])
            total_a, total_b = sb("total_a", [S, 2 * B, E]), sb("total_b", [S, 2 * B, E])
            over, tiles_of = sb("over", [S, E, LIMITS]), sb("tiles_of", [S, E])
            earlier, first, ends = sb("earlier", [S, E, E]), sb("first", [S, E]), sb("ends", [S, E])
            passed, slot_f = sb("passed", [1, T, E]), sb("slot_f", [S, 2 * B])
            expert_f = sb("expert_f", [1, T])
            count_ps = ps("count_ps", [S, 2, 512])
        stats, mv, rstd = sb("stats", [S, 2, 6]), sb("mv", [S, 2, 2]), sb("rstd", [S, 2, 1])
        rms = sb("rms", [S, 2, 1])
        xn, xT = sb("xn", [S, 2, D]), sb("xT", [P, 2, DC, S])
        logits = sb("logits", [S, B, E])
        best, total = sb("best", [S, B, 8]), sb("total", [S, B])
        x_ps, l_ps = ps("x_ps", [P, 2, 512]), ps("l_ps", [S, 2, 512])
        if dense:
            m_ps, y_ps = ps("m_ps", [P, 2, 512]), ps("y_ps", [S, 2, 512])
        s_w = sig("weights_in", 1)
        twice = layer in (1, 2)
        s_ln, s_pow, s_xn = sig("ln_steps", 5 if twice else 3), sig("rstd_ready", 2 if twice else 1), sig("xn_ready", 1)
        s_rms, s_l1 = sig("scale_ready", 1), sig("route_part", 1)
        s_xps, s_xT, s_all = sig("x_turned", 1), sig("xT_ready", DC), sig("xT_all_ready", 1)
        s_lps, s_l, s_tick = sig("logits_done", 1), sig("logits_copied", 1), sig("tick", 0)
        s_cos = sig("cosine_part", 1)
        s_rt, s_to_act, s_act = sig("route_steps", 1), sig("for_scalar", 1), sig("scalar_done", 1)
        s_mps, s_m, s_yps, s_y = sig("mix_turned", 1), sig("mixT_ready", 1), sig("bias_done", 1), sig("bias_added", 1)
        s_mix = sig("mix_ready", 1)
        s_chosen, s_count, s_zero = sig("chosen_ready", 1), sig("counts_done", 1), sig("slots_zeroed", 1)
        cosine = dense

        with nc.Block() as block:
            @block.sync
            def _(sp):
                for dst, src in loads:
                    sp.dma_start(dst, src).then_inc(s_w.sem, 16)
                if not dense:
                    sp.wait_ge(s_zero.sem, 1)
                    sp.dma_start(plan.rows_in.rearrange("(c p) d -> p c d", p=P),
                                 core.zeros[:].unsqueeze(1).to_broadcast([P, T * plan.SC, D])).then_inc(s_zero.sem, 16)
                    sp.wait_ge(s_zero.sem, 17)

            @block.gpsimd
            def _(pool):
                core.clear_spent(pool)
                if not dense:
                    pool.memset(core.zeros[:], 0.0).then_inc(s_zero.sem, 1)
                if cosine:
                    pool.wait_ge(s_cos.sem, 2)
                    pool.tensor_tensor(norm[0:8, 0, :], norm[0:8, 0, :], core.minus_half[0:8, :], ALU.pow)\
                        .then_inc(s_cos.sem, 1)

                def body(b, par):
                    pool.wait_ge(s_ln.sem, s_ln.at(b, 2))
                    pool.tensor_tensor(rstd[:, par, :], rstd[:, par, :], core.minus_half[:], ALU.pow)\
                        .then_inc(s_pow.sem, 1)
                    if twice:
                        pool.wait_ge(s_ln.sem, s_ln.at(b, 4))
                        pool.tensor_tensor(rms[:, par, :], rms[:, par, :], core.minus_half[:], ALU.pow)\
                            .then_inc(s_pow.sem, 1)
                each(pool, body)

            @block.tensor
            def _(pe):
                pe.wait_ge(s_w.sem, 16 * len(loads))
                if cosine:
                    pe.wait_ge(s_cos.sem, 4)
                    for c in range(DC):
                        mm = pe.transpose(x_ps[:, 0, c * 8:(c + 1) * 8], cn[:, c * P:(c + 1) * P], ident[0:8, 0:8])
                    mm.then_inc(s_cos.sem, 1)
                    pe.wait_ge(s_cos.sem, 6)

                def turn(b, par):
                    pe.wait_ge(s_xn.sem, s_xn.at(b))
                    if has(b, 2):
                        pe.wait_ge(s_xT.sem, s_xT.at(b - 2, DC - 1))
                    for c in range(DC):
                        mm = pe.transpose(x_ps[:, par, c * S:(c + 1) * S], xn[:, par, c * P:(c + 1) * P],
                                          ident[0:S, 0:S])
                    mm.then_inc(s_xps.sem, 1)

                def score(b, par):
                    pe.wait_ge(s_xT.sem, s_xT.at(b, DC - 1))
                    if has(b, 2):
                        pe.wait_ge(s_l.sem, s_l.at(b - 2))
                    for c in range(DC):
                        mm = pe.matmul(l_ps[:, par, 0:E], xT[:, par, c, :], wg[:, c, :], start=(c == 0),
                                       stop=(cosine and c == DC - 1))
                    if cosine:
                        for c in range(DC):
                            mm = pe.matmul(l_ps[:, par, 8:16], xT[:, par, c, :], cnT[:, c, :], start=(c == 0),
                                           stop=(c == DC - 1))
                    else:
                        mm = pe.matmul(l_ps[:, par, 0:E], ones[0:1, 0:S], bg[:], start=False, stop=True)
                    mm.then_inc(s_lps.sem, 1)

                def body(b, par):
                    turn(b, par)
                    if has(b, 1):
                        score(b - 1, 1 - par)
                each(pe, body)
                score(B - 1, 1)
                if dense:
                    pe.wait_ge(s_mix.sem, 1)
                    for b in range(B):
                        if b >= 2:
                            pe.wait_ge(s_m.sem, b - 1)
                        pe.transpose(m_ps[0:E, b % 2, 0:S], mix[:, b, :], ident[0:S, 0:S]).then_inc(s_mps.sem, 1)
                        pe.wait_ge(s_m.sem, b + 1)
                        if b >= 2:
                            pe.wait_ge(s_y.sem, b - 1)
                        pe.matmul(y_ps[:, b % 2, 0:D], mixT[:, b % 2, :], b2[:], start=True, stop=True)\
                            .then_inc(s_yps.sem, 1)
                else:
                    pe.wait_ge(s_chosen.sem, 1)
                    pairs = chosen[:].rearrange("s k b e -> s (k b e)")
                    for i, w in enumerate((below, every_one)):
                        mm = pe.matmul(count_ps[:, i, 0:2 * B * E], w[:], pairs, start=True, stop=True)
                    mm.then_inc(s_count.sem, 1)

            @block.scalar
            def _(act):
                act.wait_ge(s_w.sem, 16 * len(loads))
                if cosine:
                    act.wait_ge(s_cos.sem, 5)
                    act.activation(cnT[:], x_ps[:, 0, 0:DC * 8].rearrange("p (c e) -> p c e", c=DC), ACT.Copy)\
                        .then_inc(s_cos.sem, 1)

                def body(b, par):
                    act.wait_ge(s_xps.sem, s_xps.at(b))
                    if has(b, 2):
                        act.wait_ge(s_lps.sem, s_lps.at(b - 2))
                        act.wait_ge(s_all.sem, s_all.at(b - 2))
                    for c in range(DC):
                        act.activation(xT[:, par, c, :], x_ps[:, par, c * S:(c + 1) * S], ACT.Copy,
                                       scale=ln_w[:, c:c + 1] if layer == 2 else 1.0).then_inc(s_xT.sem, 1)
                    if dense:
                        act.wait_ge(s_xT.sem, s_xT.at(b, DC - 1))
                        act.sem_inc(s_tick.sem, 1)
                        act.activation(xT_all[:, :, b, :], xT[:, par, :, :], ACT.Copy).then_inc(s_all.sem, 1)
                    else:
                        act.activation(plan.xn[:, b, :], xn[:, par, :], ACT.Copy).then_inc(s_all.sem, 1)
                each(act, body)
                what = pick[:] if dense else share[:, :, 1] if layer == 2 else logits[:]
                act.wait_ge(s_to_act.sem, 1)
                act.activation(what, what, ACT.Sigmoid if layer == 3 else ACT.Exp).then_inc(s_act.sem, 1)
                if dense:
                    for b in range(B):
                        act.wait_ge(s_mps.sem, b + 1)
                        if b >= 2:
                            act.wait_ge(s_yps.sem, b - 1)
                        act.activation(mixT[:, b % 2, :], m_ps[0:E, b % 2, 0:S], ACT.Copy).then_inc(s_m.sem, 1)

            @block.vector
            def _(dve):
                if not dense:
                    dve.memset(every_one[:], 1.0)
                dve.wait_ge(s_w.sem, 16 * len(loads))
                if cosine:
                    dve.tensor_tensor_reduce(out=cn[:], in0=cents[:], in1=cents[:], scale=1.0, scalar=0.0,
                                             op0=ALU.mult, op1=ALU.add, accum_out=norm[0:8, 0, :])\
                        .then_inc(s_cos.sem, 1)
                    dve.wait_ge(s_cos.sem, 1)
                    dve.tensor_scalar(norm[0:8, 0, :], norm[0:8, 0, :], 1e-24, None, ALU.max).then_inc(s_cos.sem, 1)
                    dve.wait_ge(s_cos.sem, 3)
                    dve.tensor_scalar(cn[:], cents[:], norm[0:8, 0, :], None, ALU.mult).then_inc(s_cos.sem, 1)

                def hold(sem, value):
                    dve.wait_ge(sem, value)
                    dve.sem_inc(s_tick.sem, 1)

                def front(b, par):
                    dve.bn_stats(stats[:, par, :], x_all[:, b, :]).then_inc(s_ln.sem, 1)
                    hold(s_ln.sem, s_ln.at(b, 0))
                    dve.bn_aggr(mv[:, par, :], stats[:, par, :]).then_inc(s_ln.sem, 1)
                    dve.wait_ge(s_ln.sem, s_ln.at(b, 1))
                    dve.tensor_scalar(rstd[:, par, :], mv[:, par, 1:2], EPS, None, ALU.add).then_inc(s_ln.sem, 1)
                    if twice:
                        dve.wait_ge(s_pow.sem, s_pow.at(b, 0))
                        dve.scalar_tensor_tensor(out=rms[:, par, :], in0=rstd[:, par, :], scalar=mv[:, par, 1:2],
                                                 in1=rstd[:, par, :], op0=ALU.mult, op1=ALU.mult)\
                            .then_inc(s_ln.sem, 1)
                        dve.wait_ge(s_ln.sem, s_ln.at(b, 3))
                        if layer == 2:
                            dve.tensor_scalar(rms[:, par, :], rms[:, par, :], RMS_EPS, None, ALU.add)\
                                .then_inc(s_ln.sem, 1)
                        else:
                            dve.tensor_scalar(rms[:, par, :], rms[:, par, :], float(D), 1e-24, ALU.mult, ALU.max)\
                                .then_inc(s_ln.sem, 1)

                def apply(b, par):
                    dve.wait_ge(s_pow.sem, s_pow.at(b, s_pow.per - 1))
                    by = rstd
                    if layer == 2:
                        dve.tensor_tensor(rms[:, par, :], rms[:, par, :], rstd[:, par, :], ALU.mult)\
                            .then_inc(s_rms.sem, 1)
                        dve.wait_ge(s_rms.sem, s_rms.at(b))
                        by = rms
                    if has(b, 2):
                        dve.wait_ge(s_all.sem, s_all.at(b - 2))
                        dve.wait_ge(s_xps.sem, s_xps.at(b - 2))
                    dve.tensor_scalar(xn[:, par, :], x_all[:, b, :], mv[:, par, 0:1], by[:, par, :],
                                      ALU.subtract, ALU.mult).then_inc(s_xn.sem, 1)

                def take(b, par):
                    dve.wait_ge(s_lps.sem, s_lps.at(b))
                    if cosine:
                        dve.tensor_scalar(logits[:, b, :], l_ps[:, par, 0:E], 1.0, None, ALU.mult)\
                            .then_inc(s_l1.sem, 1)
                        dve.wait_ge(s_l1.sem, s_l1.at(b))
                        dve.scalar_tensor_tensor(out=logits[:, b, :], in0=l_ps[:, par, 8:16],
                                                 scalar=rms[:, par, :], in1=logits[:, b, :],
                                                 op0=ALU.mult, op1=ALU.add).then_inc(s_l.sem, 1)
                    else:
                        dve.tensor_scalar(logits[:, b, :], l_ps[:, par, 0:E], 1.0, None, ALU.mult)\
                            .then_inc(s_l.sem, 1)

                def body(b, par):
                    front(b, par)
                    apply(b, par)
                    if has(b, 1):
                        take(b - 1, 1 - par)
                each(dve, body)
                take(B - 1, 1)

                steps = [0]

                def done(ins):
                    steps[0] += 1
                    ins.then_inc(s_rt.sem, 1)
                    dve.wait_ge(s_rt.sem, steps[0])

                over_experts = lambda t: t.unsqueeze(2).to_broadcast([S, B, E])
                dve.wait_ge(s_l.sem, B)
                if layer == 3:
                    dve.sem_inc(s_to_act.sem, 1)
                    dve.wait_ge(s_act.sem, 1)
                for b in range(B):
                    last = dve.max(best[:, b, :], logits[:, b, :])
                done(last)
                if dense:
                    done(dve.tensor_tensor(pick[:], logits[:], over_experts(best[:, :, 0]), ALU.subtract))
                    dve.sem_inc(s_to_act.sem, 1)
                    done(dve.tensor_tensor(logits[:], logits[:], over_experts(best[:, :, 1]), ALU.is_ge))
                    dve.wait_ge(s_act.sem, 1)
                    done(dve.tensor_tensor(pick[:], pick[:], logits[:], ALU.mult))
                    done(dve.tensor_reduce(total[:], pick[:], AX.X, ALU.add))
                    done(dve.reciprocal(total[:], total[:]))
                    done(dve.tensor_tensor(mix[:], pick[:], over_experts(total[:]), ALU.mult))
                    done(dve.tensor_scalar(mix[:], mix[:], gate, None, ALU.mult))
                    dve.sem_inc(s_mix.sem, 1)
                    for b in range(B):
                        dve.wait_ge(s_yps.sem, b + 1)
                        dve.tensor_tensor(x_all[:, b, :], x_all[:, b, :], y_ps[:, b % 2, 0:D], ALU.add)\
                            .then_inc(s_y.sem, 1)
                else:
                    for b in range(B):
                        last = dve.max_index(at[:, b, :], best[:, b, :], logits[:, b, :])
                    done(last)
                    done(dve.tensor_copy(place[:], at[:]))
                    every = number[:].unsqueeze(1).to_broadcast([S, B, E])
                    for k in range(2):
                        ins = dve.tensor_tensor(chosen[:, k], every, over_experts(place[:, :, k]), ALU.is_equal)
                    done(ins)
                    dve.sem_inc(s_chosen.sem, 1)
                    if layer == 2:
                        done(dve.tensor_tensor(share[:, :, 1], best[:, :, 1], best[:, :, 0], ALU.subtract))
                        dve.sem_inc(s_to_act.sem, 1)
                        dve.wait_ge(s_act.sem, 1)
                        done(dve.tensor_scalar(total[:], share[:, :, 1], 1.0, None, ALU.add))
                        done(dve.reciprocal(share[:, :, 0], total[:]))
                        done(dve.tensor_tensor(share[:, :, 1], share[:, :, 1], share[:, :, 0], ALU.mult))
                    else:
                        done(dve.tensor_tensor(total[:], best[:, :, 0], best[:, :, 1], ALU.add))
                        done(dve.tensor_scalar(total[:], total[:], 1e-20, None, ALU.add))
                        done(dve.reciprocal(total[:], total[:]))
                        for k in range(2):
                            done(dve.tensor_tensor(share[:, :, k], best[:, :, k], total[:], ALU.mult))
                    done(dve.tensor_scalar(share[:], share[:], gate, None, ALU.mult))

                    dve.wait_ge(s_count.sem, 1)
                    in_column = count_ps[:, 1, 0:2 * B * E].rearrange("s (c e) -> s c e", e=E)
                    above = count_ps[:, 0, 0:2 * B * E].rearrange("s (c e) -> s c e", e=E)
                    done(dve.tensor_copy(total_a[:], in_column))
                    now, new, step = total_a, total_b, 1
                    while step < 2 * B:
                        dve.tensor_copy(new[:, 0:step], now[:, 0:step])
                        done(dve.tensor_tensor(new[:, step:], now[:, step:], now[:, 0:2 * B - step], ALU.add))
                        now, new, step = new, now, 2 * step
                    counts = now[:, 2 * B - 1, :].unsqueeze(2).to_broadcast([S, E, LIMITS])
                    done(dve.tensor_tensor(over[:], counts, limits[:].unsqueeze(1).to_broadcast([S, E, LIMITS]),
                                           ALU.is_gt))
                    done(dve.tensor_reduce(tiles_of[:], over[:], AX.X, ALU.add))
                    done(dve.tensor_tensor(earlier[:], before[:], tiles_of[:].unsqueeze(1).to_broadcast([S, E, E]),
                                           ALU.mult))
                    done(dve.tensor_reduce(first[:], earlier[:], AX.X, ALU.add))
                    done(dve.tensor_tensor(ends[:], first[:], tiles_of[:], ALU.add))
                    done(dve.tensor_tensor(passed[:], tile_no[:].unsqueeze(2).to_broadcast([1, T, E]),
                                           ends[0:1].unsqueeze(1).to_broadcast([1, T, E]), ALU.is_ge))
                    done(dve.tensor_reduce(expert_f[:], passed[:], AX.X, ALU.add))
                    done(dve.tensor_scalar(expert_f[:], expert_f[:], float(E - 1), None, ALU.min))
                    done(dve.tensor_copy(plan.expert[:], expert_f[:]))
                    done(dve.tensor_tensor(new[:], now[:], in_column, ALU.subtract))
                    done(dve.tensor_tensor(new[:], new[:], above, ALU.add))
                    done(dve.tensor_scalar(first[:], first[:], float(plan.SLOTS), None, ALU.mult))
                    done(dve.tensor_tensor(new[:], new[:], first[:].unsqueeze(1).to_broadcast([S, 2 * B, E]), ALU.add))
                    done(dve.tensor_tensor(new[:], new[:], chosen[:].rearrange("s k b e -> s (k b) e"), ALU.mult))
                    done(dve.tensor_reduce(slot_f[:], new[:], AX.X, ALU.add))
                    done(dve.tensor_copy(plan.slot[:], slot_f[:]))


G = 4
GB = B // G
GN = GB * S


def small_experts_stage(core, xT_all, mix):
    nc, dram, x_all = core.nc, core.dram, core.x_all
    E = 8
    with ExitStack() as ctx:
        sb, ps = sub_names(ctx, nc, "e1")
        sig = core.new_signals("e1")
        w1, b1, w2 = sb("w1", [P, DC, E * P]), sb("b1", [P, E]), sb("w2", [P, E, D])
        loads = [(w1, "L1f_w1"), (b1, "L1f_b1"), (w2, "L1f_w2")]
        hid = sb("hid", [P, 2, GN])
        u_ps = ps("u_ps", [P, 2, 512])
        y_ps = ps("y_ps", [S, 2, GB, D])
        s_w = sig("weights_in", 1)
        s_up, s_gelu, s_down, s_y = sig("up_done", E), sig("gelu_done", E), sig("down_done", E), sig("added", E * GB)
        s_tick = sig("tick", 0)
        x_of = xT_all[:].rearrange("p c b s -> p c (b s)")
        with nc.Block() as block:
            @block.sync
            def _(sp):
                for dst, what in loads:
                    sp.dma_start(dst[:], dram[what]).then_inc(s_w.sem, 16)

            @block.gpsimd
            def _(pool):
                core.clear_spent(pool)

            def groups(eng, body):
                body(0)
                with eng.Fori(1, G, 1) as g:
                    body(g)

            @block.tensor
            def _(pe):
                pe.wait_ge(s_w.sem, 16 * len(loads))

                def down(g, e):
                    pe.wait_ge(s_gelu.sem, s_gelu.at(g, e))
                    if has(g, 1) or e >= 2:
                        pe.wait_ge(s_y.sem, s_y.at(g, GB * e + GB - 1) - 2 * GB)
                    for t in range(GB):
                        mm = pe.matmul(y_ps[:, e % 2, t, :], hid[:, e % 2, t * S:(t + 1) * S], w2[:, e, :],
                                       start=True, stop=True)
                    mm.then_inc(s_down.sem, 1)

                def body(g):
                    for e in range(E):
                        if has(g, 1) or e >= 2:
                            pe.wait_ge(s_gelu.sem, s_gelu.at(g, e) - 2)
                        for c in range(DC):
                            mm = pe.matmul(u_ps[:, e % 2, 0:GN], w1[:, c, e * P:(e + 1) * P],
                                           x_of[:, c, bass.ds(g * GN, GN)], start=(c == 0), stop=(c == DC - 1))
                        mm.then_inc(s_up.sem, 1)
                        if e > 0:
                            down(g, e - 1)
                    down(g, E - 1)
                groups(pe, body)

            @block.scalar
            def _(act):
                act.wait_ge(s_w.sem, 16 * len(loads))

                def body(g):
                    for e in range(E):
                        act.wait_ge(s_up.sem, s_up.at(g, e))
                        if has(g, 1) or e >= 2:
                            act.wait_ge(s_down.sem, s_down.at(g, e) - 2)
                        act.activation(hid[:, e % 2, :], u_ps[:, e % 2, 0:GN], ACT.Gelu, bias=b1[:, e:e + 1])\
                            .then_inc(s_gelu.sem, 1)
                groups(act, body)

            @block.vector
            def _(dve):
                def body(g):
                    for e in range(E):
                        dve.wait_ge(s_down.sem, s_down.at(g, e))
                        for t in range(GB):
                            b = g * GB + t
                            if e > 0:
                                dve.wait_ge(s_y.sem, s_y.at(g, (e - 1) * GB + t))
                            dve.scalar_tensor_tensor(out=x_all[:, b, :], in0=y_ps[:, e % 2, t, :],
                                                     scalar=mix[:, b, e:e + 1], in1=x_all[:, b, :],
                                                     op0=ALU.mult, op1=ALU.add).then_inc(s_y.sem, 1)
                groups(dve, body)


def experts_stage(core, layer, E, F, plan):
    nc, dram, x_all, ident = core.nc, core.dram, core.x_all, core.ident
    name = lambda n: f"L{layer}f_{n}"
    FC = -(-F // P)
    rows = [min(P, F - f * P) for f in range(FC)]
    T, SLOTS, SC = plan.tiles, plan.SLOTS, plan.SC
    biased = layer == 2
    RING, FETCH = 4, 8
    assert 2 * FC % RING == 0
    with ExitStack() as ctx:
        sb, ps = sub_names(ctx, nc, f"e{layer}")
        sig = core.new_signals(f"e{layer}")
        w1, w3, w2 = sb("w1", [P, 2, DC, F]), sb("w3", [P, 2, DC, F]), sb("w2", [P, 2, FC, D])
        loads = [(w1, "w1"), (w3, "w3"), (w2, "w2")]
        if biased:
            b1, b3, b2 = sb("b1", [P, 2, FC]), sb("b3", [P, 2, FC]), sb("b2", [P, 2, D])
            ln_w = sb("ln_w", [P, DC])
            loads += [(b1, "b1"), (b3, "b3")]
        x_in = sb("x_in", [P, 2, SC, D])
        xT = sb("xT", [P, DC, SLOTS])
        silu = sb("silu", [P, RING, SLOTS])
        hid = sb("hid", [P, FC, SLOTS])
        y_out = sb("y_out", [P, 2, SC, D])
        fetched = sb("fetched", [S, FETCH, D])
        x_ps, ab_ps, y_ps = ps("x_ps", [P, DC, SLOTS]), ps("ab_ps", [P, RING, 2, SLOTS]), ps("y_ps", [P, 2, SC, D])
        s_w = [sig(f"weights_in{i}", 1) for i in range(2)]
        s_ln = sig("ln_w_in", 1)
        s_scattered = sig("rows_scattered", 1)
        s_x = [sig(f"x_in{i}", 1) for i in range(2)]
        s_xps, s_xT = sig("x_turned", 1), sig("xT_ready", DC)
        s_up, s_silu, s_hid = sig("up_done", FC), sig("silu_done", FC), sig("hid_ready", FC)
        s_down, s_y = sig("down_done", 1), sig("y_copied", 1)
        s_stored = [sig(f"y_stored{i}", 1) for i in range(2)]
        s_fetched = [sig(f"fetched{i}", 1) for i in range(FETCH)]
        s_added = sig("added", 1)
        s_tick = [sig(f"tick{i}", 0) for i in range(2)]
        next_tile = lambda t: not isinstance(t, int) or t + 1 < T
        tile_rows = lambda d, t: d[bass.ds(t * SLOTS, SLOTS), :].rearrange("(c p) d -> p c d", p=P)

        def each_tile(eng, body):
            body(0, 0)
            body(1, 1)
            pairs = (T - 1) // 2
            with eng.Fori(1, pairs, 1) as j:
                body(j * 2, 0)
                body(j * 2 + 1, 1)
            for t in range(2 * pairs, T):
                body(t, t % 2)

        def weights_in(eng, t, par):
            eng.wait_ge(s_w[par].sem, half(t, par) * (len(loads) + biased))

        with nc.Block() as block:
            @block.gpsimd
            def _(pool):
                core.clear_spent(pool)
                for i in range(2 * B):
                    pool.indirect_dma_start(plan.rows_in, bass.IndirectOffsetOnAxis(plan.slot[:, i:i + 1], 0),
                                            plan.xn[:, i % B, :], None).then_inc(s_scattered.sem, 16)
                for par in range(2):
                    pool.wait_ge(s_stored[par].sem, 16 * len(range(par, T, 2)))
                for i in range(2 * B):
                    if i >= FETCH:
                        pool.wait_ge(s_added.sem, i - FETCH + 1)
                    pool.indirect_dma_start(fetched[:, i % FETCH, :], None, plan.rows_out,
                                            bass.IndirectOffsetOnAxis(plan.slot[:, i:i + 1], 0))\
                        .then_inc(s_fetched[i % FETCH].sem, 16)

            @block.sync
            def _(sp):
                if biased:
                    sp.dma_start(ln_w[:], dram[name("ln_w")]).then_inc(s_ln.sem, 16)

                def load_weights(t, par):
                    if has(t, 2):
                        sp.wait_ge(s_down.sem, s_down.at(t - 2))
                        sp.sem_inc(s_tick[0].sem, 1)
                    e = sp.value_load(plan.expert[0:1, bass.ds(t, 1)], min_val=0, max_val=E - 1)
                    for dst, what in loads:
                        sp.dma_start(dst[:, par], dram[name(what)][e]).then_inc(s_w[par].sem, 16)
                    if biased:
                        if has(t, 2):
                            sp.wait_ge(s_y.sem, s_y.at(t - 2))
                            sp.sem_inc(s_tick[0].sem, 1)
                        sp.dma_start(b2[:, par], dram[name("b2")][bass.ds(e, 1), :].to_broadcast([P, D]))\
                            .then_inc(s_w[par].sem, 16)

                def load_rows(t, par):
                    sp.dma_start(x_in[:, par], tile_rows(plan.rows_in, t)).then_inc(s_x[par].sem, 16)

                def body(t, par):
                    if has(t, 2):
                        load_weights(t, par)
                        load_rows(t, par)

                load_weights(0, 0)
                load_weights(1, 1)
                sp.wait_ge(s_scattered.sem, 16 * 2 * B)
                load_rows(0, 0)
                load_rows(1, 1)
                each_tile(sp, body)

            @block.tensor
            def _(pe):
                def turn(t, par):
                    pe.wait_ge(s_x[par].sem, half(t, par))
                    if has(t, 1):
                        pe.wait_ge(s_xT.sem, s_xT.at(t - 1, DC - 1))
                    for c in range(DC):
                        for h in range(SC):
                            mm = pe.transpose(x_ps[:, c, h * P:(h + 1) * P], x_in[:, par, h, c * P:(c + 1) * P],
                                              ident[:, :])
                    mm.then_inc(s_xps.sem, 1)

                def up(t, par):
                    weights_in(pe, t, par)
                    pe.wait_ge(s_xT.sem, s_xT.at(t, DC - 1))
                    for f in range(FC):
                        if has(t, 1) or f >= RING:
                            pe.wait_ge(s_hid.sem, s_hid.at(t, f) - RING)
                        for i, w in enumerate((w1, w3)):
                            for c in range(DC):
                                mm = pe.matmul(ab_ps[0:rows[f], (par * FC + f) % RING, i, :],
                                               w[:, par, c, f * P:f * P + rows[f]], xT[:, c, :],
                                               start=(c == 0), stop=(c == DC - 1))
                        mm.then_inc(s_up.sem, 1)

                def down(t, par):
                    if has(t, 2):
                        pe.wait_ge(s_y.sem, s_y.at(t - 2))
                    for h in range(SC):
                        for f in range(FC):
                            if h == 0:
                                pe.wait_ge(s_hid.sem, s_hid.at(t, f))
                            mm = pe.matmul(y_ps[:, par, h, :], hid[0:rows[f], f, h * P:(h + 1) * P],
                                           w2[0:rows[f], par, f, :], start=(f == 0), stop=(f == FC - 1))
                    mm.then_inc(s_down.sem, 1)

                def body(t, par):
                    up(t, par)
                    if next_tile(t):
                        turn(t + 1, 1 - par)
                    down(t, par)

                turn(0, 0)
                each_tile(pe, body)

            @block.scalar
            def _(act):
                def copy_xT(t):
                    act.wait_ge(s_xps.sem, s_xps.at(t))
                    for c in range(DC):
                        act.activation(xT[:, c, :], x_ps[:, c, :], ACT.Copy, scale=ln_w[:, c:c + 1] if biased else 1.0)\
                            .then_inc(s_xT.sem, 1)

                def body(t, par):
                    if biased:
                        weights_in(act, t, par)
                    for f in range(FC):
                        r, i = rows[f], (par * FC + f) % RING
                        act.wait_ge(s_up.sem, s_up.at(t, f))
                        if has(t, 1) or f >= RING:
                            act.wait_ge(s_hid.sem, s_hid.at(t, f) - RING)
                        act.activation(silu[0:r, i, :], ab_ps[0:r, i, 0, :], ACT.Silu,
                                       bias=b1[0:r, par, f:f + 1] if biased else 0.0).then_inc(s_silu.sem, 1)
                    if next_tile(t):
                        copy_xT(t + 1)
                    act.wait_ge(s_y.sem, s_y.at(t))
                    act.dma_start(tile_rows(plan.rows_out, t), y_out[:, par]).then_inc(s_stored[par].sem, 16)

                if biased:
                    act.wait_ge(s_ln.sem, 16)
                copy_xT(0)
                each_tile(act, body)

            @block.vector
            def _(dve):
                def body(t, par):
                    if biased:
                        weights_in(dve, t, par)
                    for f in range(FC):
                        r, i = rows[f], (par * FC + f) % RING
                        dve.wait_ge(s_silu.sem, s_silu.at(t, f))
                        if biased:
                            dve.scalar_tensor_tensor(out=hid[0:r, f, :], in0=ab_ps[0:r, i, 1, :],
                                                     scalar=b3[0:r, par, f:f + 1], in1=silu[0:r, i, :],
                                                     op0=ALU.add, op1=ALU.mult).then_inc(s_hid.sem, 1)
                        else:
                            dve.tensor_tensor(hid[0:r, f, :], ab_ps[0:r, i, 1, :], silu[0:r, i, :], ALU.mult)\
                                .then_inc(s_hid.sem, 1)
                    dve.wait_ge(s_down.sem, s_down.at(t))
                    if has(t, 2):
                        dve.wait_ge(s_stored[par].sem, half(t, par) - 16)
                    if biased:
                        dve.tensor_tensor(y_out[:, par], y_ps[:, par], b2[:, par, :].unsqueeze(1)
                                          .to_broadcast([P, SC, D]), ALU.add).then_inc(s_y.sem, 1)
                    else:
                        dve.tensor_copy(y_out[:, par], y_ps[:, par]).then_inc(s_y.sem, 1)

                each_tile(dve, body)
                for i in range(2 * B):
                    b, k = i % B, i // B
                    dve.wait_ge(s_fetched[i % FETCH].sem, 16 * (i // FETCH + 1))
                    if k == 1:
                        dve.wait_ge(s_added.sem, i - B + 1)
                    dve.scalar_tensor_tensor(out=x_all[:, b, :], in0=fetched[:, i % FETCH, :],
                                             scalar=plan.share[:, b, k:k + 1], in1=x_all[:, b, :],
                                             op0=ALU.mult, op1=ALU.add).then_inc(s_added.sem, 1)


def moe(core, layer, E, F):
    with ExitStack() as ctx:
        if layer == 1:
            xT_all = ctx.enter_context(core.nc.sbuf_tensor("xT_all", [P, DC, B, S], F32))
            mix = ctx.enter_context(core.nc.sbuf_tensor("mix", [S, B, E], F32))
            route_stage(core, layer, E, xT_all=xT_all, mix=mix)
            small_experts_stage(core, xT_all, mix)
        else:
            plan = Plan(core, ctx, layer, E)
            route_stage(core, layer, E, plan=plan)
            experts_stage(core, layer, E, F, plan)


def store_stage(core, out):
    nc = core.nc
    s_out = core.stack.enter_context(nc.semaphore("x_stored"))
    with nc.Block() as block:
        @block.sync
        def _(sp):
            sp.dma_start(out.rearrange("b s d -> s b d"), core.x_all[:]).then_inc(s_out, 16)
            sp.wait_ge(s_out, 16)


def flamingo(nc, dram, out, stages=8):
    with ExitStack() as stack:
        core = Core(nc, dram, stack)
        setup_stage(core)
        todo = [
            lambda: attention_stage(core, 0, heads=8, hd=32, scale=D ** -0.5, kan=True),
            lambda: tree_stage(core),
            lambda: attention_stage(core, 1, heads=16, hd=64, scale=64 ** -0.5, mask="keys"),
            lambda: moe(core, 1, 8, 128),
            lambda: attention_stage(core, 2, heads=16, hd=16, scale=0.25, rope=True),
            lambda: moe(core, 2, 8, 1024),
            lambda: attention_stage(core, 3, heads=16, hd=16, scale=0.25, mask="scores"),
            lambda: moe(core, 3, 9, 704),
        ]
        for stage in todo[:stages]:
            stage()
        store_stage(core, out)


def host_layout(inputs):
    get = lambda n: np.asarray(inputs[n])

    def chunks(a):
        return np.ascontiguousarray(a.reshape(a.shape[0] // P, P, *a.shape[1:]).swapaxes(0, 1))

    turned = lambda a: chunks(np.ascontiguousarray(a.T))
    row = lambda a: np.ascontiguousarray(a.reshape(1, -1))
    col = lambda a: np.ascontiguousarray(a.reshape(-1, P).T)
    o = {
        "x": get("x"),
        "gates": np.concatenate([get("g_xattn"), get("g_ffn")]).reshape(1, 8),
        "ident": np.eye(P, dtype=np.float32),
        "ctxT": np.ascontiguousarray(get("ctx_1024").transpose(0, 2, 1).reshape(B, DC, P, SK).transpose(0, 2, 1, 3)),
        "mask_keys": np.ascontiguousarray(get("mask_BxS2_bf1")).view(np.uint8).reshape(B, 1, SK),
        "mask_scores": get("mask_1x1xSxS2_ik1")[0, 0],
        "below": np.triu(np.ones((S, S), np.float32), 1),
        "limits": np.arange(-(-B * S // Plan.SLOTS), dtype=np.float32).reshape(1, -1) * Plan.SLOTS,
        "numbers8": np.arange(8, dtype=np.float32).reshape(1, 8),
        "numbers9": np.arange(9, dtype=np.float32).reshape(1, 9),
    }
    for e in (8, 9):
        o[f"before{e}"] = np.tril(np.ones((e, e), np.float32), -1).reshape(1, -1)
        o[f"tile_no{e}"] = np.arange((Plan.PAIRS + e * (Plan.SLOTS - 1)) // Plan.SLOTS, dtype=np.float32).reshape(1, -1)
    for n in "qkv":
        o[f"L0x_w{n}T"] = turned(get(f"L0_xattn_w{n}"))
        o[f"L0x_b{n}"] = col(get(f"L0_xattn_b{n}"))
    o["L0x_bqrow"], o["L0x_bvrow"] = row(get("L0_xattn_bq")), row(get("L0_xattn_bv"))
    o["L0x_ln_g"], o["L0x_ln_b"] = col(get("L0_xattn_ln_g")), col(get("L0_xattn_ln_b"))
    o["L0x_base_wT"] = turned(get("L0_xattn_kan_base_w"))
    o["L0x_spline_wT"] = chunks(get("L0_xattn_kan_spline_w").transpose(1, 2, 0))
    o["L0x_scalerT"] = turned(get("L0_xattn_kan_spline_scaler"))
    o["L0x_centers"] = np.ascontiguousarray(np.broadcast_to(np.arange(8, dtype=np.float32) - 3.5, (P, 8)))
    o["L0f_wqT"], o["L0f_routersT"] = turned(get("L0_ffn_Wq")), turned(get("L0_ffn_routers"))
    o["L0f_leaves"], o["L0f_woutT"] = chunks(get("L0_ffn_leaf_values")), turned(get("L0_ffn_Wout_w"))
    o["L0f_bout"] = row(get("L0_ffn_Wout_b"))
    o["L1x_wqT"] = turned(get("L1_xattn_Wq"))
    o["L1x_wkT"], o["L1x_wvT"] = turned(get("L1_xattn_Wkv")[:1024]), turned(get("L1_xattn_Wkv")[1024:])
    o["L1x_woT"], o["L1x_bo"] = turned(get("L1_xattn_Wout")), row(get("L1_xattn_b_out"))
    o["L1f_gateT"], o["L1f_centroids"] = turned(get("L1_ffn_w_route")), get("L1_ffn_centroids")
    o["L1f_b2"] = get("L1_ffn_b2")
    o["L1f_w1"] = chunks(get("L1_ffn_w1").transpose(1, 0, 2).reshape(D, 8 * P))
    o["L1f_b1"] = np.ascontiguousarray(get("L1_ffn_b1").T)
    o["L1f_w2"] = np.ascontiguousarray(get("L1_ffn_w2").transpose(1, 0, 2))
    for layer in (2, 3):
        for n in "qkvo":
            o[f"L{layer}x_w{n}T"] = turned(get(f"L{layer}_xattn_W{n}"))
            o[f"L{layer}x_b{n}"] = (row if n == "o" else col)(get(f"L{layer}_xattn_b{n}"))
        spread = np.zeros((16, 32, D), np.float32)
        spread[:, :16] = get(f"L{layer}_xattn_Wo").T.reshape(16, 16, D)
        o[f"L{layer}x_woT"] = chunks(spread.reshape(512, D))
        spread = np.zeros((16, 32), np.float32)
        spread[:, :16] = get(f"L{layer}_xattn_bv").reshape(16, 16)
        o[f"L{layer}x_bv"] = col(spread)
        odd = np.arange(P) // 16 % 2
        o[f"L{layer}x_halves"] = np.stack([(1 - odd) * 0.25, odd * 0.25], axis=1).astype(np.float32)
    swap = np.arange(D) // 16 * 16 + (np.arange(D) % 16 + 8) % 16
    for n in "qk":
        o[f"L2x_w{n}rT"] = turned(get(f"L2_xattn_W{n}")[swap])
        o[f"L2x_b{n}r"] = col(get(f"L2_xattn_b{n}")[swap])
    inv_freq = np.float32(1.0) / np.float32(10000.0) ** (np.arange(0, 16, 2, dtype=np.float32) / np.float32(16))
    freqs = np.arange(SK, dtype=np.float32)[None, :] * inv_freq[np.arange(P) % 8][:, None]
    sign = np.where(np.arange(P) % 16 < 8, -1.0, 1.0).astype(np.float32)
    o["L2x_cos"] = np.cos(freqs)
    o["L2x_sin"] = np.sin(freqs) * sign[:, None]
    o["L2f_gateT"], o["L2f_gate_bias"] = chunks(get("L2_ffn_Wg")), row(get("L2_ffn_bg"))
    o["L2f_ln_w"], o["L2f_b2"] = col(get("L2_ffn_ln_w")), get("L2_ffn_b2")
    per_expert = lambda a: np.ascontiguousarray(a.reshape(a.shape[0], a.shape[1] // P, P, a.shape[2]).transpose(0, 2, 1, 3))
    o["L2f_w1"], o["L2f_w3"] = per_expert(get("L2_ffn_W1a")), per_expert(get("L2_ffn_W1b"))
    o["L2f_w2"] = per_expert(get("L2_ffn_W2"))
    for n, what in (("b1", "b1a"), ("b3", "b1b")):
        o[f"L2f_{n}"] = np.ascontiguousarray(get(f"L2_ffn_{what}").reshape(8, 8, P).transpose(0, 2, 1))
    both = lambda a, b: np.concatenate([get(a), get(b)], axis=0)
    o["L3f_gateT"] = turned(both("L3_ffn_gate_weight", "L3_ffn_new_gate_weight"))
    o["L3f_gate_bias"] = row(np.concatenate([np.zeros(8, np.float32), get("L3_ffn_gate_bias")]))
    for n in ("w1", "w3"):
        o[f"L3f_{n}"] = per_expert(both(f"L3_ffn_{n}", f"L3_ffn_new_{n}").transpose(0, 2, 1))
    w2 = both("L3_ffn_w2", "L3_ffn_new_w2").transpose(0, 2, 1)
    padded = np.zeros((w2.shape[0], 6 * P, D), np.float32)
    padded[:, :w2.shape[1]] = w2
    o["L3f_w2"] = per_expert(padded)
    return {k: np.ascontiguousarray(a) for k, a in o.items()}


def kernel(**inputs):
    import concourse.bacc as bacc
    from concourse.bass_utils import run_bass_kernel_spmd

    nc = bacc.Bacc("TRN2", target_bir_lowering=False, num_devices=1)
    arrays = {f"in_{k}": a for k, a in host_layout(inputs).items()}
    dram = {k[3:]: nc.dram_tensor(k, a.shape, mybir.dt.from_np(a.dtype), kind="ExternalInput").ap()
            for k, a in arrays.items()}
    out = nc.dram_tensor("out_0", (B, S, D), F32, kind="ExternalOutput").ap()
    flamingo(nc, dram, out)
    result = run_bass_kernel_spmd(nc, [arrays], core_ids=[0])
    return result.results[0]["out_0"]
```

```python
from contextlib import ExitStack

import numpy as np

import concourse.bass as bass
from concourse import mybir

F32 = mybir.dt.float32
U8 = mybir.dt.uint8
I32 = mybir.dt.int32
ALU = mybir.AluOpType
ACT = mybir.ActivationFunctionType
AX = mybir.AxisListType

P = 128
B, S, D, SK = 16, 112, 256, 375
DC = D // P
KC = 3
KT = SK // KC
EPS = 1e-5
FLT_MAX = float(np.finfo(np.float32).max)


class Signal:

    def __init__(self, new, name, per):
        self.sem, self.per = new(name), per

    def at(self, b, k=0):
        return b * self.per + (k + 1)


def has(b, lag):
    return not isinstance(b, int) or b - lag >= 0


def more(b):
    return not isinstance(b, int) or b < B - 1


def exists(b):
    return not isinstance(b, int) or 0 <= b < B


def half(b, par):
    return (b - par) * 8 + 16


def each(eng, body):
    body(0, 0)
    body(1, 1)
    with eng.Fori(1, B // 2 - 1, 1) as j:
        body(j * 2, 0)
        body(j * 2 + 1, 1)
    body(B - 2, 0)
    body(B - 1, 1)


LEAD = 3
KAN_RES, KAN_VAR, KAN_RESN, KAN_LNT, KAN_DIST, KAN_SILU, KAN_BASES, KAN_STEPS = 0, 3, 4, 6, 7, 12, 16, 17
KAN_EXP, KAN_ABS, KAN_NEAR2, KAN_NEAR1, KAN_SQ1, KAN_ACTS = 0, (1, 4), (2, 6), (3, 7), (5, 8), 9


class Core:

    def __init__(self, nc, dram, stack):
        self.nc, self.dram, self.stack = nc, dram, stack
        sb = lambda n, s: stack.enter_context(nc.sbuf_tensor(n, s, F32))
        self.x_all = sb("x_all", [S, B, D])
        self.row_stats = sb("row_stats", [S, B, 6])
        self.ident = sb("ident", [P, P])
        self.ones = sb("ones", [1, P])
        self.minus_half = sb("minus_half", [S, 1])
        self.zeros = sb("zeros", [P, D])
        self.gates = sb("gates", [S, 8])
        self.spent, self.current = ExitStack(), ExitStack()
        self.spent_sems, self.current_sems = [], []

    def new_signals(self, tag):
        self.spent.close()
        self.spent, self.spent_sems = self.current, self.current_sems
        self.current, self.current_sems = ExitStack(), []

        def new(name):
            sem = self.current.enter_context(self.nc.semaphore(f"{tag}_{name}"))
            self.current_sems.append(sem)
            return sem

        return lambda name, per: Signal(new, name, per)

    def inverse_root(self, pool, t):
        return pool.tensor_tensor(t[:], t[:], self.minus_half[:].unsqueeze(1).to_broadcast([S, B, 1]), ALU.pow)

    def clear_spent(self, pool):
        for sem in self.spent_sems:
            pool.sem_clear(sem)


class Norm:

    def __init__(self, core, sb, sig):
        self.core = core
        self.mv, self.rstd = sb("mv", [S, B, 2]), sb("rstd", [S, B, 1])
        self.s_mv, self.s_var = sig("ln_mv", 1), sig("ln_var", 1)
        self.ready = sig("rstd_ready", 1).sem

    def on_vector(self, dve):
        for b in range(B):
            dve.bn_aggr(self.mv[:, b, :], self.core.row_stats[:, b, :]).then_inc(self.s_mv.sem, 1)
        dve.wait_ge(self.s_mv.sem, B)
        dve.tensor_scalar(self.rstd[:], self.mv[:, :, 1:2], EPS, None, ALU.add).then_inc(self.s_var.sem, 1)

    def on_gpsimd(self, pool):
        pool.wait_ge(self.s_var.sem, 1)
        self.core.inverse_root(pool, self.rstd).then_inc(self.ready, 1)


def sub_names(ctx, nc, stage):
    sb = lambda n, s, d=F32: ctx.enter_context(nc.sbuf_tensor(f"{stage}_{n}", s, d))
    ps = lambda n, s, d=F32: ctx.enter_context(nc.psum_tensor(f"{stage}_{n}", s, d))
    return sb, ps


def attention_stage(core, layer, heads, hd, scale, rope=False, mask=None, kan=False):
    nc, dram = core.nc, core.dram
    x_all, ident, gate, ones = core.x_all, core.ident, core.gates[:, layer:layer + 1], core.ones
    tag = f"a{layer}"
    DQ = heads * hd
    QC = DQ // P
    name = lambda n: f"L{layer}x_{n}"

    k_jobs = [("k", c) for c in range(QC)]
    if rope:
        k_jobs = [(kind, c) for c in range(QC) for kind in ("k", "kr")]
    v_width = min(DQ, 512)
    v_jobs = [("v", t, part) for t in range(KC) for part in range(DQ // v_width)]
    q_jobs = [("q", c) for c in range(0, QC, min(QC, 4))] + ([("qr", 0)] if rope else [])
    if kan:
        q_jobs.append(("qtok", 0))
    qn = min(QC, 4)
    jobs = k_jobs + v_jobs + [("xT", 0)] + q_jobs
    kv = k_jobs + v_jobs
    job_slot = {j: i * (heads - LEAD) // len(jobs) for i, j in enumerate(jobs)}
    index_of = {j: i for i, j in enumerate(jobs)}
    jobs_at = lambda n: [j for j in jobs if job_slot[j] == n]
    pool_heads = (1,) if kan else ()
    scaled_by = [tuple(n for n in range(heads) if n not in pool_heads), pool_heads]
    norm_slot = min(1 if kan else 2, job_slot[("xT", 0)] - 1)
    on_scalar = lambda j: j[0] == "xT" or (j[0] == "v" and layer != 1) or (j[0] in ("k", "q") and not rope)

    VW = max(hd, 32)
    OC = heads * VW // P
    o_groups = -(-OC // 4)
    og_heads = heads // o_groups
    og_blocks = OC // o_groups

    with ExitStack() as ctx:
        sb, ps = sub_names(ctx, nc, tag)
        sig = core.new_signals(tag)

        wq = sb("wq", [P, DC, DQ])
        wk = sb("wk", [P, DC, DQ])
        wv = sb("wv", [P, DC, DQ])
        weights = [(wq, "wqT"), (wk, "wkT"), (wv, "wvT")]
        if rope:
            wqr, wkr = sb("wqr", [P, DC, DQ]), sb("wkr", [P, DC, DQ])
            weights += [(wqr, "wqrT"), (wkr, "wkrT")]
        small = []
        if layer != 1:
            bq, bk, bv = sb("bq", [P, QC]), sb("bk", [P, QC]), sb("bv", [P, OC])
            small += [(bq, "bq"), (bk, "bk"), (bv, "bv")]
        if rope:
            bqr, bkr = sb("bqr", [P, QC]), sb("bkr", [P, QC])
            cos, sin = sb("cos", [P, SK]), sb("sin", [P, SK])
            small += [(bqr, "bqr"), (bkr, "bkr"), (cos, "cos"), (sin, "sin")]
        if hd == 16:
            halves = sb("halves", [P, 2])
            small += [(halves, "halves")]
        if kan:
            lng, lnb = sb("lng", [P, DC]), sb("lnb", [P, DC])
            base_w = sb("base_w", [P, DC, D])
            spline_w = sb("spline_w", [P, DC, 8, D])
            scaler = sb("scaler", [P, DC, D])
            centers = sb("centers", [P, 8])
            bqrow, bvrow = sb("bqrow", [S, D]), sb("bvrow", [S, D])
            bqs = sb("bqs", [P, QC])
            small += [(lng, "ln_g"), (lnb, "ln_b"), (centers, "centers"), (bqrow, "bqrow"), (bvrow, "bvrow")]
            weights += [(base_w, "base_wT"), (spline_w, "spline_wT"), (scaler, "scalerT")]
        else:
            wo = sb("wo", [P, OC, D])
            borow = sb("borow", [S, D])
            weights += [(wo, "woT")]
            small += [(borow, "bo")]

        ctxT = sb("ctxT", [P, 2, DC, SK])
        stats, mv = sb("stats", [S, 6]), sb("mv", [S, 2])
        rstd = sb("rstd", [S, 1])
        xn = sb("xn", [S, D])
        xT = sb("xT", [P, DC, S])
        qT = sb("qT", [P, 2, 2 if hd == 16 else 1, QC, S])
        kT = sb("kT", [P, 2, QC, SK])
        v = sb("v", [KT, 2, KC, heads, VW])
        probs = sb("probs", [S, 4, SK])
        pT = sb("pT", [KT, 2, KC, S])
        negmax = sb("negmax", [S, heads])
        rowsum = sb("rowsum", [S, heads])
        rinv = sb("rinv", [S, heads])
        oT = sb("oT", [P, OC, S])
        if rope:
            rot_a, rot_b = sb("rot_a", [P, 2, SK]), sb("rot_b", [P, 2, SK])
            qrot_a, qrot_b = sb("qrot_a", [P, DC, S]), sb("qrot_b", [P, DC, S])
        if hd == 16:
            qfull = sb("qfull", [P, DC, S])
        if mask:
            masked = sb("masked", [S, 2, SK])
            if mask == "keys":
                mask_in = sb("mask_in", [S, 2, SK], U8)
                mask_add = sb("mask_add", [S, 2, SK])
            else:
                mask_in = sb("mask_in", [S, 1, SK], I32)
                mask_add = sb("mask_add", [S, 1, SK])
        if kan:
            qtok = sb("qtok", [S, 2, D])
            res = sb("res", [S, D])
            stats2, mv2, rstd2 = sb("stats2", [S, 6]), sb("mv2", [S, 2]), sb("rstd2", [S, 1])
            resn = sb("resn", [S, D])
            lnT = sb("lnT", [P, DC, S])
            silu = sb("silu", [P, DC, S])
            sexp = sb("sexp", [P, DC, S])
            dist = sb("dist", [P, DC, 8, S])
            near2, near1 = sb("near2", [P, DC, 8, S]), sb("near1", [P, DC, 8, S])
            sq2, sq1 = sb("sq2", [P, DC, 8, S]), sb("sq1", [P, DC, 8, S])
            bases = sb("bases", [P, DC, 8, S])

        sc_ps = ps("sc_ps", [S, 2, 512])
        pT_ps = ps("pT_ps", [P, 2, 512])
        o_ps = ps("o_ps", [P, 512])
        job_banks = [ps(f"job_ps{i}", [P, 512]) for i in range(2)]
        fin_ps = ps("fin_ps", [P, 512])

        s_w = sig("weights_in", 1)
        s_small = sig("small_in", 1)
        s_ctx = [sig(f"ctx_in{i}", 1) for i in range(2)]
        s_job = sig("job_ready", len(jobs))
        s_jobfree = [sig(f"job_free{i}", len(jobs[i::2])) for i in range(2)]
        s_ln = sig("ln_steps", 3)
        s_pow = sig("rstd_ready", 1)
        s_xn = sig("xn_ready", 1)
        s_scores = sig("scores_ready", heads)
        s_max = sig("max_ready", heads)
        s_probs = sig("probs_ready", heads)
        s_pT = sig("pT_in_psum", heads)
        s_pTc = [sig(f"pT_copied{i}", heads // 2) for i in range(2)]
        s_pv = sig("pv_done", heads)
        s_rinv = sig("rinv_ready", heads)
        s_scaled = [sig(f"probs_scaled{i}", len(scaled_by[i])) for i in range(2)]
        s_o = sig("o_copied", o_groups)
        s_out = sig("output_done", 1)
        s_x = sig("x_updated", 1)
        s_bo, s_biased, s_stats = sig("bias_scaled", 1), sig("x_biased", 1), sig("stats_ready", 1)
        s_zero = sig("v_zeroed", 1)
        s_tick = [sig(f"tick{i}", 0) for i in range(4)]
        if rope:
            s_ropek = sig("rope_k_ready", QC)
            s_rope_q = sig("rope_q_parts", 2 * DC)
            s_qsum = sig("q_summed", 1)
        s_qf = sig("q_chunks", QC)
        if hd == 16:
            s_q2 = sig("q_halves_ready", 2)
        if mask:
            s_mask = sig("mask_ready", 1)
            s_maskin = [sig(f"mask_in{i}", 1) for i in range(2)]
        if kan:
            s_setup = sig("setup", 1)
            s_k = sig("kan_dve", KAN_STEPS)
            s_ka = sig("kan_act", KAN_ACTS)
            s_kp = sig("kan_pool", 2 * DC)
            s_pow2 = sig("rstd2_ready", 1)
            s_oback = sig("o_turned", 1)
            s_lnt = sig("ln_turned", 1)

        def job(j, b):
            return s_job.at(b, index_of[j])

        def freed(j, b):
            i = index_of[j]
            return s_jobfree[i % 2].sem, s_jobfree[i % 2].at(b, i // 2)

        def ahead(b, par, n, lead):
            if n + lead < heads:
                return [(b, par, n + lead)]
            return [(b + 1, 1 - par, n + lead - heads)] if more(b) else []

        def tails(t, n, step):
            for lag in (2, 1):
                if kan and exists(t - lag):
                    step(t - lag, n + heads * (lag - 1))

        def v_of(par, t, part):
            h = v_width // hd
            return v[:, par, t, part * h:(part + 1) * h, 0:hd]

        def q_of(par, n):
            if hd == 16:
                r = 32 * ((n % 8) // 2)
                return qT[r:r + 32, par, n % 2, n // 8, :], r, 32, n // 8
            at = n * hd
            return qT[at % P:at % P + hd, par, 0, at // P, :], at % P, hd, at // P

        with nc.Block() as block:

            @block.sync
            def _(sp):
                for dst, what in small:
                    src = dram[name(what)]
                    if what in ("bqrow", "bvrow", "bo"):
                        src = src.to_broadcast([S, D])
                    sp.dma_start(dst[:], src).then_inc(s_small.sem, 16)
                if mask == "scores":
                    sp.dma_start(mask_in[:, 0, :], dram["mask_scores"]).then_inc(s_maskin[0].sem, 16)
                for dst, what in weights:
                    src = dram[name(what)]
                    sp.dma_start(dst[:], src).then_inc(s_w.sem, 16)

                def load(b, par, known):
                    if known:
                        sp.wait_ge(s_job.sem, job(kv[-1], b - 2))
                        sp.sem_inc(s_tick[2].sem, 1)
                    sp.dma_start(ctxT[:, par], dram["ctxT"][b]).then_inc(s_ctx[par].sem, 16)
                    if mask == "keys":
                        if known:
                            sp.wait_ge(s_mask.sem, s_mask.at(b - 2))
                            sp.sem_inc(s_tick[2].sem, 1)
                        sp.dma_start(mask_in[:, par, :], dram["mask_keys"][b].to_broadcast([S, SK])).then_inc(s_maskin[par].sem, 16)

                load(0, 0, False)
                load(1, 1, False)
                with sp.Fori(1, B // 2, 1) as j:
                    load(j * 2, 0, True)
                    load(j * 2 + 1, 1, True)

            def in_ctx(eng, b, par, sem=s_ctx):
                eng.wait_ge(sem[par].sem, half(b, par))

            @block.gpsimd
            def _(pool):
                core.clear_spent(pool)

                def power(b):
                    pool.wait_ge(s_ln.sem, s_ln.at(b, 2))
                    pool.tensor_tensor(rstd[:], rstd[:], core.minus_half[:], ALU.pow).then_inc(s_pow.sem, 1)

                def scale_probs(b, par, n):
                    if n not in pool_heads:
                        return
                    pool.wait_ge(s_rinv.sem, s_rinv.at(b, n))
                    pool.sem_inc(s_tick[3].sem, 1)
                    pool.tensor_scalar(probs[:, n % 4, :], probs[:, n % 4, :], rinv[:, n:n + 1], None, ALU.mult)\
                        .then_inc(s_scaled[1].sem, 1)

                def kan_step(b, slot):
                    if slot == 1:
                        pool.wait_ge(s_k.sem, s_k.at(b, KAN_VAR))
                        pool.tensor_tensor(rstd2[:], rstd2[:], core.minus_half[:], ALU.pow).then_inc(s_pow2.sem, 1)
                    for c in range(DC):
                        if slot == 6 + 2 * c:
                            pool.wait_ge(s_ka.sem, s_ka.at(b, KAN_NEAR2[c]))
                            pool.sem_inc(s_tick[3].sem, 1)
                            pool.tensor_tensor(sq2[:, c], near2[:, c], near2[:, c], ALU.mult).then_inc(s_kp.sem, 1)
                        if slot == 7 + c:
                            pool.wait_ge(s_kp.sem, s_kp.at(b, 2 * c))
                            pool.sem_inc(s_tick[3].sem, 1)
                            pool.tensor_tensor(near2[:, c], sq2[:, c], near2[:, c], ALU.mult).then_inc(s_kp.sem, 1)

                def body(b, par):
                    for n in range(heads):
                        for at in ahead(b, par, n, 1):
                            scale_probs(*at)
                        if n == 0 and more(b):
                            power(b + 1)
                        tails(b, n, kan_step)
                        add_bias(b, n)
                        for c in range(QC):
                            if rope and more(b) and job_slot[("kr", c)] == n:
                                rope_add(b + 1, 1 - par, c)

                def add_bias(t, n):
                    if not kan and n == heads - 4 and exists(t - 1):
                        if isinstance(t, int) and t == 1:
                            pool.wait_ge(s_bo.sem, 1)
                        pool.wait_ge(s_x.sem, s_x.at(t - 1))
                        pool.sem_inc(s_tick[3].sem, 1)
                        pool.tensor_tensor(x_all[:, t - 1, :], x_all[:, t - 1, :], borow[:], ALU.add)\
                            .then_inc(s_biased.sem, 1)

                def rope_add(b, par, c):
                    if has(b, 2):
                        pool.wait_ge(s_pv.sem, s_pv.at(b - 2, heads - 1))
                    for kind in ("k", "kr"):
                        pool.wait_ge(*freed((kind, c), b))
                    pool.tensor_tensor(kT[:, par, c, :], rot_a[:, c, :], rot_b[:, c, :], ALU.add)\
                        .then_inc(s_ropek.sem, 1)

                power(0)
                if rope:
                    for c in range(QC):
                        rope_add(0, 0, c)
                scale_probs(0, 0, 0)
                each(pool, body)
                for t in range(B, B + 2):
                    for n in range(heads):
                        tails(t, n, kan_step)
                        add_bias(t, n)

            @block.tensor
            def _(pe):
                pe.wait_ge(s_w.sem, 16 * len(weights))
                pe.wait_ge(s_small.sem, 16 * len(small))
                if kan:
                    pe.wait_ge(s_setup.sem, 3 + DC)

                def run_job(j, b, par):
                    kind = j[0]
                    free, value = freed(j, b)
                    if has(b, 1) or index_of[j] >= 2:
                        pe.wait_ge(free, value - 1)
                    if j in q_jobs[:1]:
                        pe.wait_ge(*freed(("xT", 0), b))
                    job_ps = job_banks[index_of[j] % 2]
                    if j == jobs[0]:
                        in_ctx(pe, b, par)
                    if kind in ("k", "kr"):
                        w = wk if kind == "k" else wkr
                        for c in range(DC):
                            mm = pe.matmul(job_ps[:, 0:SK], w[:, c, j[1] * P:(j[1] + 1) * P],
                                           ctxT[:, par, c, :], start=(c == 0), stop=(c == DC - 1))
                    elif kind == "v":
                        _, t, part = j
                        for c in range(DC):
                            mm = pe.matmul(job_ps[0:KT, 0:v_width], ctxT[:, par, c, t * KT:(t + 1) * KT],
                                           wv[:, c, part * v_width:(part + 1) * v_width],
                                           start=(c == 0), stop=(c == DC - 1))
                    elif kind == "xT":
                        pe.wait_ge(s_xn.sem, s_xn.at(b))
                        for c in range(DC):
                            mm = pe.transpose(job_ps[:, c * S:(c + 1) * S], xn[:, c * P:(c + 1) * P],
                                              ident[0:S, 0:S])
                    elif kind in ("q", "qr"):
                        w = wq if kind == "q" else wqr
                        for i in range(qn):
                            f = j[1] + i
                            for c in range(DC):
                                mm = pe.matmul(job_ps[:, i * S:(i + 1) * S], w[:, c, f * P:(f + 1) * P],
                                               xT[:, c, :], start=(c == 0), stop=(c == DC - 1))
                    else:
                        for c in range(DC):
                            mm = pe.matmul(job_ps[0:S, 0:D], xT[:, c, :], wq[:, c, :], start=(c == 0),
                                           stop=(c == DC - 1))
                    mm.then_inc(s_job.sem, 1)

                def scores(b, par, n):
                    if n == 0:
                        for j in jobs[-2:]:
                            pe.wait_ge(*freed(j, b))
                        if rope:
                            pe.wait_ge(s_ropek.sem, s_ropek.at(b, QC - 1))
                        if hd == 16:
                            pe.wait_ge(s_q2.sem, s_q2.at(b, 1))
                    free = s_max if mask else s_probs
                    if has(b, 1) or n >= 2:
                        pe.wait_ge(free.sem, free.at(b, n) - 2)
                    lhs, r, k, c = q_of(par, n)
                    pe.matmul(sc_ps[:, n % 2, 0:SK], lhs, kT[r:r + k, par, c, :], start=True, stop=True)\
                        .then_inc(s_scores.sem, 1)

                def transposes(b, n):
                    who = int(n in pool_heads)
                    pe.wait_ge(s_scaled[who].sem, s_scaled[who].at(b, scaled_by[who].index(n)))
                    copied = s_pTc[n % 2]
                    if has(b, 1) or n >= 2:
                        pe.wait_ge(copied.sem, copied.at(b, n // 2) - 1)
                    for t in range(KC):
                        mm = pe.transpose(pT_ps[0:KT, n % 2, t * S:(t + 1) * S],
                                          probs[:, n % 4, t * KT:(t + 1) * KT], ident[0:S, 0:S])
                    mm.then_inc(s_pT.sem, 1)

                def pv(b, par, n):
                    pe.wait_ge(s_pTc[n % 2].sem, s_pTc[n % 2].at(b, n // 2))
                    if n % og_heads == 0 and (has(b, 1) or n > 0):
                        pe.wait_ge(s_o.sem, s_o.at(b, n // og_heads) - 1)
                    r, w = n * VW % P, n * VW // P % 4 * S
                    for t in range(KC):
                        mm = pe.matmul(o_ps[r:r + VW, w:w + S], v[:, par, t, n, :], pT[:, n % 2, t, :],
                                       start=(t == 0), stop=(t == KC - 1))
                    mm.then_inc(s_pv.sem, 1)

                def output(b):
                    pe.wait_ge(s_o.sem, s_o.at(b, o_groups - 1))
                    if has(b, 1):
                        pe.wait_ge(s_x.sem, s_x.at(b - 1))
                    for c in range(OC):
                        mm = pe.matmul(fin_ps[0:S, 0:D], oT[:, c, :], wo[:, c, :], start=(c == 0), stop=(c == OC - 1))
                    mm.then_inc(s_out.sem, 1)

                def turn(src, b, signal):
                    for c in range(DC):
                        if signal is s_oback:
                            mm = pe.transpose(fin_ps[0:S, c * P:(c + 1) * P], src[:, c, :], ident[:, :])
                        else:
                            mm = pe.transpose(fin_ps[:, c * S:(c + 1) * S], src[:, c * P:(c + 1) * P], ident[0:S, 0:S])
                    mm.then_inc(signal.sem, 1)

                def kan_output(b):
                    pe.wait_ge(s_k.sem, s_k.at(b, KAN_BASES))
                    if more(b):
                        pe.wait_ge(s_k.sem, s_k.at(b + 1, KAN_LNT))
                    for c in range(DC):
                        pe.matmul(fin_ps[0:S, 0:D], silu[:, c, :], base_w[:, c, :], start=(c == 0), stop=False)
                    for c in range(DC):
                        for i in range(8):
                            mm = pe.matmul(fin_ps[0:S, 0:D], bases[:, c, i, :], spline_w[:, c, i, :],
                                           start=False, stop=(c == DC - 1 and i == 7))
                    mm.then_inc(s_out.sem, 1)

                def finish(t, n):
                    if not kan:
                        if n == 1 and exists(t - 1):
                            output(t - 1)
                        return
                    if n == 1 and exists(t - 1):
                        pe.wait_ge(s_o.sem, s_o.at(t - 1))
                        if has(t, 3):
                            pe.wait_ge(s_x.sem, s_x.at(t - 3))
                        turn(oT, t - 1, s_oback)
                    if n == 3 and exists(t - 1):
                        pe.wait_ge(s_k.sem, s_k.at(t - 1, KAN_RESN))
                        turn(resn, t - 1, s_lnt)
                    if n == 4 and exists(t - 2):
                        kan_output(t - 2)

                def body(b, par):
                    for n in range(heads):
                        for at in ahead(b, par, n, LEAD):
                            scores(*at)
                        todo = jobs_at(n) if more(b) else []
                        for j in todo[:1]:
                            run_job(j, b + 1, 1 - par)
                        transposes(b, n)
                        if n > 0:
                            pv(b, par, n - 1)
                        elif has(b, 1):
                            pv(b - 1, 1 - par, heads - 1)
                        for j in todo[1:]:
                            run_job(j, b + 1, 1 - par)
                        finish(b, n)

                if hd == 16:
                    pe.wait_ge(s_zero.sem, 1)
                for j in jobs:
                    run_job(j, 0, 0)
                for n in range(LEAD):
                    scores(0, 0, n)
                each(pe, body)
                pv(B - 1, 1, heads - 1)
                for t in range(B, B + 2):
                    for n in range(heads):
                        finish(t, n)

            @block.scalar
            def _(act):
                act.wait_ge(s_small.sem, 16 * len(small))

                def copy_job(j, b, par):
                    kind = j[0]
                    if not on_scalar(j):
                        return
                    if kind in ("v", "k", "q") and has(b, 2):
                        act.wait_ge(s_pv.sem, s_pv.at(b - 2, heads - 1))
                    act.wait_ge(s_job.sem, job(j, b))
                    free, job_ps = freed(j, b)[0], job_banks[index_of[j] % 2]
                    if kind == "k":
                        f = j[1]
                        act.activation(kT[:, par, f, :], job_ps[:, 0:SK], ACT.Identity,
                                       bias=bk[:, f:f + 1] if layer != 1 else 0.0).then_inc(free, 1)
                    elif kind == "v":
                        _, t, part = j
                        if hd == 16 and isinstance(b, int) and b < 2:
                            act.wait_ge(s_zero.sem, 1)
                        act.activation(v_of(par, t, part), job_ps[0:KT, 0:v_width].rearrange("p (h d) -> p h d", d=hd),
                                       ACT.Copy).then_inc(free, 1)
                    elif kind == "xT":
                        act.activation(xT[:, :, :], job_ps[:, 0:DC * S].rearrange("p (c s) -> p c s", c=DC),
                                       ACT.Copy).then_inc(free, 1)
                    elif kind == "q" and layer == 1:
                        act.activation(qT[:, par, 0, j[1]:j[1] + qn, :],
                                       job_ps[:, 0:qn * S].rearrange("p (c s) -> p c s", c=qn),
                                       ACT.Copy, scale=scale).then_inc(free, 1)
                    elif kind == "q" and hd == 16:
                        if has(b, 1):
                            act.wait_ge(s_q2.sem, s_q2.at(b - 1, 1))
                        for c in range(QC):
                            ins = act.activation(qfull[:, c, :], job_ps[:, c * S:(c + 1) * S], ACT.Identity,
                                                 bias=bq[:, c:c + 1])
                            ins.then_inc(s_qf.sem, 1)
                        act.wait_ge(s_qf.sem, s_qf.at(b, QC - 1))
                        act.sem_inc(free, 1)
                    elif kind == "q":
                        for c in range(QC):
                            act.activation(qT[:, par, 0, c, :], job_ps[:, c * S:(c + 1) * S], ACT.Identity,
                                           scale=scale, bias=bqs[:, c:c + 1]).then_inc(s_qf.sem, 1)
                        act.wait_ge(s_qf.sem, s_qf.at(b, QC - 1))
                        act.sem_inc(free, 1)

                def exps(b, par, n):
                    act.wait_ge(s_max.sem, s_max.at(b, n))
                    if has(b, 1) or n >= 4:
                        act.wait_ge(s_pT.sem, s_pT.at(b, n) - 4)
                    src = masked[:, n % 2, :] if mask else sc_ps[:, n % 2, 0:SK]
                    act.activation(probs[:, n % 4, :], src, ACT.Exp, bias=negmax[:, n:n + 1],
                                   scale=-1.0 if mask else 1.0,
                                   accum_out=rowsum[:, n:n + 1]).then_inc(s_probs.sem, 1)

                def copy_pT(b, n):
                    act.wait_ge(s_pT.sem, s_pT.at(b, n))
                    if has(b, 1) or n >= 2:
                        act.wait_ge(s_pv.sem, s_pv.at(b, n) - 2)
                    act.activation(pT[:, n % 2, :, :], pT_ps[0:KT, n % 2, 0:KC * S].rearrange("p (c s) -> p c s", c=KC),
                                   ACT.Copy).then_inc(s_pTc[n % 2].sem, 1)

                def copy_oT(b, g):
                    act.wait_ge(s_pv.sem, s_pv.at(b, (g + 1) * og_heads - 1))
                    if has(b, 1):
                        used = s_oback if kan else s_out
                        act.wait_ge(used.sem, used.at(b - 1))
                    act.activation(oT[:, g * og_blocks:(g + 1) * og_blocks, :],
                                   o_ps[:, 0:og_blocks * S].rearrange("p (c s) -> p c s", c=og_blocks),
                                   ACT.Copy).then_inc(s_o.sem, 1)

                def kan_step(b, slot):
                    def done(ins):
                        ins.then_inc(s_ka.sem, 1)

                    def bend(c, dst, src, func, after, **scaling):
                        act.wait_ge(s_ka.sem, s_ka.at(b, after))
                        done(act.activation(dst[:, c], src[:, c], func, **scaling))

                    def distance(c):
                        act.wait_ge(s_k.sem, s_k.at(b, KAN_DIST + c))
                        done(act.activation(dist[:, c], dist[:, c], ACT.Abs))

                    near = lambda c, dst, reach: bend(c, dst, dist, ACT.Relu, KAN_ABS[c], scale=-1.0, bias=reach)
                    if slot == 4:
                        act.wait_ge(s_k.sem, s_k.at(b, KAN_LNT))
                        done(act.activation(sexp[:], lnT[:], ACT.Exp, scale=-1.0))
                        distance(0)
                    if slot == 5:
                        near(0, near2, 2.0)
                        near(0, near1, 1.0)
                    if slot == 6:
                        distance(1)
                        bend(0, sq1, near1, ACT.Square, KAN_NEAR1[0])
                    if slot == 7:
                        near(1, near2, 2.0)
                        near(1, near1, 1.0)
                    if slot == 8:
                        bend(1, sq1, near1, ACT.Square, KAN_NEAR1[1])

                def body(b, par):
                    for n in range(heads):
                        for at in ahead(b, par, n, 2):
                            exps(*at)
                        todo = jobs_at(n) if more(b) else []
                        for j in todo[:1]:
                            copy_job(j, b + 1, 1 - par)
                        if n % 2 == 0:
                            copy_pT(b, n)
                        if n == 0 and has(b, 1) and hd != 16:
                            copy_oT(b - 1, o_groups - 1)
                        tails(b, n, kan_step)
                        if o_groups == 2 and n == og_heads:
                            copy_oT(b, 0)
                        for j in todo[1:]:
                            copy_job(j, b + 1, 1 - par)

                if kan:
                    act.wait_ge(s_setup.sem, 3 + DC)
                for j in jobs:
                    copy_job(j, 0, 0)
                exps(0, 0, 0)
                exps(0, 0, 1)
                each(act, body)
                if hd != 16:
                    copy_oT(B - 1, o_groups - 1)
                for t in range(B, B + 2):
                    for n in range(heads):
                        tails(t, n, kan_step)

            @block.vector
            def _(dve):
                dve.wait_ge(s_small.sem, 16 * len(small))

                def hold(sem, value):
                    dve.wait_ge(sem, value)
                    dve.sem_inc(s_tick[1].sem, 1)

                if hd == 16:
                    dve.memset(v[:], 0.0).then_inc(s_zero.sem, 1)
                if mask == "scores":
                    dve.wait_ge(s_maskin[0].sem, 16)
                    dve.tensor_scalar(mask_add[:, 0, :], mask_in[:, 0, :], -1e15, None, ALU.mult)\
                        .then_inc(s_mask.sem, 1)
                    dve.wait_ge(s_mask.sem, 1)
                if kan:
                    dve.wait_ge(s_w.sem, 16 * len(weights))
                    dve.tensor_tensor(bqrow[:], bqrow[:], bvrow[:], ALU.add).then_inc(s_setup.sem, 1)
                    dve.tensor_scalar(bqs[:], bq[:], scale, None, ALU.mult).then_inc(s_setup.sem, 1)
                    dve.tensor_scalar(scaler[:], scaler[:], 1.0 / 6.0, None, ALU.mult).then_inc(s_setup.sem, 1)
                    dve.wait_ge(s_setup.sem, 3)
                    for c in range(DC):
                        dve.tensor_tensor(spline_w[:, c], spline_w[:, c],
                                          scaler[:, c, :].unsqueeze(1).to_broadcast([P, 8, D]),
                                          ALU.mult).then_inc(s_setup.sem, 1)

                if not kan:
                    dve.tensor_scalar(borow[:], borow[:], gate, None, ALU.mult).then_inc(s_bo.sem, 1)

                def norm_stats(b):
                    dve.bn_stats(stats[:], x_all[:, b, :]).then_inc(s_ln.sem, 1)
                    hold(s_ln.sem, s_ln.at(b, 0))
                    dve.bn_aggr(mv[:], stats[:]).then_inc(s_ln.sem, 1)
                    dve.wait_ge(s_ln.sem, s_ln.at(b, 1))
                    dve.tensor_scalar(rstd[:], mv[:, 1:2], EPS, None, ALU.add).then_inc(s_ln.sem, 1)

                def norm_apply(b):
                    dve.wait_ge(s_pow.sem, s_pow.at(b))
                    if has(b, 1):
                        dve.wait_ge(s_job.sem, job(("xT", 0), b - 1))
                    dve.tensor_scalar(xn[:], x_all[:, b, :], mv[:, 0:1], rstd[:, 0:1], ALU.subtract, ALU.mult)\
                        .then_inc(s_xn.sem, 1)

                def make_mask(b, par):
                    in_ctx(dve, b, par, s_maskin)
                    if has(b, 2):
                        dve.wait_ge(s_max.sem, s_max.at(b - 2, heads - 1))
                    dve.tensor_scalar(mask_add[:, par, :], mask_in[:, par, :], 1.0, FLT_MAX, ALU.subtract, ALU.mult)\
                        .then_inc(s_mask.sem, 1)

                def copy_job(j, b, par):
                    kind = j[0]
                    if on_scalar(j):
                        return
                    dve.wait_ge(s_job.sem, job(j, b))
                    free, job_ps = freed(j, b)[0], job_banks[index_of[j] % 2]
                    if kind in ("k", "kr"):
                        f = j[1]
                        if has(b, 1):
                            dve.wait_ge(s_ropek.sem, s_ropek.at(b - 1, f))
                        dst, bias, table = (rot_a, bk, cos) if kind == "k" else (rot_b, bkr, sin)
                        dve.scalar_tensor_tensor(out=dst[:, f, :], in0=job_ps[:, 0:SK], scalar=bias[:, f:f + 1],
                                                 in1=table[:], op0=ALU.add, op1=ALU.mult).then_inc(free, 1)
                    elif kind in ("q", "qr"):
                        if has(b, 1):
                            dve.wait_ge(s_qsum.sem, s_qsum.at(b - 1))
                        dst, bias, table = (qrot_a, bq, cos) if kind == "q" else (qrot_b, bqr, sin)
                        for c in range(DC):
                            dve.scalar_tensor_tensor(out=dst[:, c, :], in0=job_ps[:, c * S:(c + 1) * S],
                                                     scalar=bias[:, c:c + 1], in1=table[:, 0:S], op0=ALU.add,
                                                     op1=ALU.mult).then_inc(s_rope_q.sem, 1)
                        dve.wait_ge(s_rope_q.sem, s_rope_q.at(b, (kind == "qr") * DC + DC - 1))
                        dve.sem_inc(free, 1)
                    elif kind == "v":
                        if has(b, 2):
                            dve.wait_ge(s_pv.sem, s_pv.at(b - 2, heads - 1))
                        _, t, part = j
                        dve.tensor_copy(v_of(par, t, part), job_ps[0:KT, 0:v_width].rearrange("p (h d) -> p h d", d=hd))\
                            .then_inc(free, 1)
                    elif kind == "qtok":
                        if has(b, 2):
                            dve.wait_ge(s_k.sem, s_k.at(b - 2, KAN_RES))
                        dve.tensor_tensor(qtok[:, par, :], job_ps[0:S, 0:D], bqrow[:], ALU.add).then_inc(free, 1)

                def halve_q(b, par):
                    if rope:
                        dve.wait_ge(s_rope_q.sem, s_rope_q.at(b, 2 * DC - 1))
                        if has(b, 1):
                            dve.wait_ge(s_q2.sem, s_q2.at(b - 1, 1))
                        dve.tensor_tensor(qfull[:], qrot_a[:], qrot_b[:], ALU.add).then_inc(s_qsum.sem, 1)
                        dve.wait_ge(s_qsum.sem, s_qsum.at(b))
                    else:
                        dve.wait_ge(s_qf.sem, s_qf.at(b, QC - 1))
                    if has(b, 2):
                        dve.wait_ge(s_pv.sem, s_pv.at(b - 2, heads - 1))
                    for i in range(2):
                        dve.tensor_scalar(qT[:, par, i], qfull[:], halves[:, i:i + 1], None, ALU.mult)\
                            .then_inc(s_q2.sem, 1)

                def row_max(b, par, n):
                    dve.wait_ge(s_scores.sem, s_scores.at(b, n))
                    if has(b, 1) and not mask:
                        dve.wait_ge(s_probs.sem, s_probs.at(b - 1, n))
                    if mask:
                        if n == 0 and mask == "keys":
                            dve.wait_ge(s_mask.sem, s_mask.at(b))
                        if has(b, 1) or n >= 2:
                            dve.wait_ge(s_probs.sem, s_probs.at(b, n) - 2)
                        dve.sem_inc(s_tick[1].sem, 1)
                        m = mask_add[:, par if mask == "keys" else 0, :]
                        dve.tensor_tensor_reduce(out=masked[:, n % 2, :], in0=sc_ps[:, n % 2, 0:SK], in1=m,
                                                 scale=-1.0, scalar=FLT_MAX, op0=ALU.add, op1=ALU.min,
                                                 accum_out=negmax[:, n:n + 1]).then_inc(s_max.sem, 1)
                    else:
                        dve.tensor_reduce(negmax[:, n:n + 1], sc_ps[:, n % 2, 0:SK], AX.X, ALU.max, negate=True)\
                            .then_inc(s_max.sem, 1)

                def copy_pT(b, n):
                    dve.wait_ge(s_pT.sem, s_pT.at(b, n))
                    if has(b, 1) or n >= 2:
                        dve.wait_ge(s_pv.sem, s_pv.at(b, n) - 2)
                    dve.tensor_copy(pT[:, n % 2, :, :], pT_ps[0:KT, n % 2, 0:KC * S].rearrange("p (c s) -> p c s", c=KC))\
                        .then_inc(s_pTc[n % 2].sem, 1)

                def invert(b, par, n):
                    dve.wait_ge(s_probs.sem, s_probs.at(b, n))
                    dve.reciprocal(rinv[:, n:n + 1], rowsum[:, n:n + 1]).then_inc(s_rinv.sem, 1)

                def scale_probs(b, par, n):
                    if n in pool_heads:
                        return
                    hold(s_rinv.sem, s_rinv.at(b, n))
                    dve.tensor_scalar(probs[:, n % 4, :], probs[:, n % 4, :], rinv[:, n:n + 1], None, ALU.mult)\
                        .then_inc(s_scaled[0].sem, 1)

                def copy_oT(b):
                    dve.wait_ge(s_pv.sem, s_pv.at(b, heads - 1))
                    if has(b, 1):
                        dve.wait_ge(s_out.sem, s_out.at(b - 1))
                    dve.tensor_tensor(oT[:], o_ps[:, 0:OC * S].rearrange("p (c s) -> p c s", c=OC),
                                      bv[:].unsqueeze(2).to_broadcast([P, OC, S]), ALU.add).then_inc(s_o.sem, 1)

                def update(b):
                    dve.wait_ge(s_out.sem, s_out.at(b))
                    dve.scalar_tensor_tensor(out=x_all[:, b, :], in0=fin_ps[0:S, 0:D], scalar=gate,
                                             in1=x_all[:, b, :], op0=ALU.mult, op1=ALU.add).then_inc(s_x.sem, 1)

                def kan_step(b, par, slot):
                    def done(ins, k):
                        ins.then_inc(s_k.sem, 1)
                        hold(s_k.sem, s_k.at(b, k))
                    if slot == 1:
                        dve.wait_ge(s_oback.sem, s_oback.at(b))
                        done(dve.tensor_tensor(res[:], fin_ps[0:S, 0:D], qtok[:, par, :], ALU.add), KAN_RES)
                        done(dve.bn_stats(stats2[:], res[:]), KAN_RES + 1)
                        done(dve.bn_aggr(mv2[:], stats2[:]), KAN_RES + 2)
                        done(dve.tensor_scalar(rstd2[:], mv2[:, 1:2], EPS, None, ALU.add), KAN_VAR)
                    if slot == 2:
                        dve.wait_ge(s_pow2.sem, s_pow2.at(b))
                        done(dve.tensor_scalar(resn[:], res[:], mv2[:, 0:1], rstd2[:, 0:1], ALU.subtract, ALU.mult),
                             KAN_RESN)
                    if slot == 3:
                        dve.wait_ge(s_lnt.sem, s_lnt.at(b))
                        for c in range(DC):
                            done(dve.tensor_scalar(lnT[:, c, :], fin_ps[:, c * S:(c + 1) * S], lng[:, c:c + 1],
                                                   lnb[:, c:c + 1], ALU.mult, ALU.add), KAN_RESN + 1 + c)
                    for c in range(DC):
                        if slot == 3 + c:
                            done(dve.scalar_tensor_tensor(
                                out=dist[:, c], in0=lnT[:, c, :].unsqueeze(1).to_broadcast([P, 8, S]), scalar=2.5,
                                in1=centers[:].unsqueeze(2).to_broadcast([P, 8, S]),
                                op0=ALU.mult, op1=ALU.subtract), KAN_DIST + c)
                        if slot == 8 + c:
                            dve.wait_ge(s_ka.sem, s_ka.at(b, KAN_SQ1[c]))
                            done(dve.scalar_tensor_tensor(out=near1[:, c], in0=sq1[:, c], scalar=-4.0,
                                                          in1=near1[:, c], op0=ALU.mult, op1=ALU.mult),
                                 KAN_SILU + 1 + 2 * c)
                            dve.wait_ge(s_kp.sem, s_kp.at(b, 2 * c + 1))
                            done(dve.tensor_tensor(bases[:, c], near2[:, c], near1[:, c], ALU.add),
                                 KAN_SILU + 2 + 2 * c)
                    if slot == 5:
                        dve.wait_ge(s_ka.sem, s_ka.at(b, KAN_EXP))
                        done(dve.tensor_scalar(sexp[:], sexp[:], 1.0, None, ALU.add), KAN_DIST + 2)
                        done(dve.reciprocal(sexp[:, 0], sexp[:, 0]), KAN_DIST + 3)
                    if slot == 6:
                        done(dve.reciprocal(sexp[:, 1], sexp[:, 1]), KAN_DIST + 4)
                        if has(b, 1):
                            hold(s_out.sem, s_out.at(b - 1))
                        done(dve.tensor_tensor(silu[:], lnT[:], sexp[:], ALU.mult), KAN_SILU)

                def finish(t, n, par):
                    if hd == 16 and n == 0 and exists(t - 1):
                        copy_oT(t - 1)
                    if not kan and n == 2 and exists(t - 1):
                        update(t - 1)
                    if kan and n == 5 and exists(t - 2):
                        update(t - 2)
                    lag, slot, done = (2, 6, s_x) if kan else (1, heads - 2, s_biased)
                    if n == slot and exists(t - lag):
                        hold(done.sem, done.at(t - lag))
                        dve.bn_stats(core.row_stats[:, t - lag, :], x_all[:, t - lag, :]).then_inc(s_stats.sem, 1)
                    tails(t, n, lambda b, slot: kan_step(b, (par + slot // heads + 1) % 2, slot))

                def body(b, par):
                    for n in range(heads):
                        for at in ahead(b, par, n, 1):
                            invert(*at)
                        for at in ahead(b, par, n, LEAD):
                            row_max(*at)
                        for at in ahead(b, par, n, 1):
                            scale_probs(*at)
                        todo = jobs_at(n) if more(b) else []
                        for j in todo[:1]:
                            copy_job(j, b + 1, 1 - par)
                        if n % 2 == 1:
                            copy_pT(b, n)
                        if more(b):
                            if n == 0:
                                norm_stats(b + 1)
                            if n == norm_slot:
                                norm_apply(b + 1)
                        finish(b, n, par)
                        if more(b):
                            if n == norm_slot:
                                if mask == "keys":
                                    make_mask(b + 1, 1 - par)
                            for j in todo[1:]:
                                copy_job(j, b + 1, 1 - par)
                            if n == job_slot[jobs[-1]] and hd == 16:
                                halve_q(b + 1, 1 - par)

                norm_stats(0)
                norm_apply(0)
                if mask == "keys":
                    make_mask(0, 0)
                for j in jobs:
                    copy_job(j, 0, 0)
                if hd == 16:
                    halve_q(0, 0)
                for n in range(LEAD):
                    row_max(0, 0, n)
                    if n == 0:
                        invert(0, 0, 0)
                        scale_probs(0, 0, 0)
                each(dve, body)
                for t in range(B, B + 2):
                    for n in range(heads):
                        finish(t, n, t % 2)


def setup_stage(core):
    nc = core.nc
    s_in = core.stack.enter_context(nc.semaphore("x_in"))
    s_g = core.stack.enter_context(nc.semaphore("gates_in"))
    s_one = core.stack.enter_context(nc.semaphore("ones_ready"))
    with nc.Block() as block:
        @block.sync
        def _(sp):
            sp.dma_start(core.gates[:], core.dram["gates"].to_broadcast([S, 8])).then_inc(s_g, 16)
            sp.dma_start(core.ident[:], core.dram["ident"]).then_inc(s_in, 16)
            sp.dma_start(core.x_all[:], core.dram["x"].rearrange("b s d -> s b d")).then_inc(s_in, 16)
            sp.wait_ge(s_in, 32)

        @block.scalar
        def _(act):
            act.wait_ge(s_g, 16)
            act.activation(core.gates[:], core.gates[:], ACT.Tanh).then_inc(s_g, 1)
            act.wait_ge(s_g, 17)

        @block.vector
        def _(dve):
            dve.memset(core.ones[:], 1.0).then_inc(s_one, 1)
            dve.memset(core.minus_half[:], -0.5).then_inc(s_one, 1)
            dve.wait_ge(s_one, 2)


def tree_stage(core):
    nc, dram, x_all, ident, ones = core.nc, core.dram, core.x_all, core.ident, core.ones
    gate = core.gates[:, 4:5]
    LEVELS = 8
    M = 2 ** LEVELS
    PAIRS = B // 2
    with ExitStack() as ctx:
        sb, ps = sub_names(ctx, nc, "f0")
        sig = core.new_signals("f0")
        wq, routers = sb("wq", [P, DC, D]), sb("routers", [P, DC, M - 1])
        leaves, wout, bout = sb("leaves", [P, DC, D]), sb("wout", [P, DC, D]), sb("bout", [1, D])
        loads = [(wq, "L0f_wqT"), (routers, "L0f_routersT"), (leaves, "L0f_leaves"), (wout, "L0f_woutT"),
                 (bout, "L0f_bout")]
        norm_x = Norm(core, sb, sig)
        xn = sb("xn", [S, 2, D])
        feature_major = lambda n: sb(n, [P, DC, 2, S])
        xT, qT, leafT, retT = [feature_major(n) for n in ("xT", "qT", "leafT", "retT")]
        sides = sb("sides", [S, 2, M, 2])
        paths = [sb(f"paths{l}", [S, 2, 2 ** (l + 1)]) for l in range(LEVELS)]
        x_ps, q_ps, l_ps, v_ps = [ps(n, [P, DC, 2, P]) for n in ("x_ps", "q_ps", "l_ps", "v_ps")]
        r_ps, y_ps = ps("r_ps", [S, 2, D]), ps("y_ps", [S, 2, D])
        s_w, s_xn = sig("weights_in", 1), sig("xn_ready", 2)
        s_xps, s_xT, s_qps, s_qT = sig("x_turned", 1), sig("xT_ready", 1), sig("q_ready", 1), sig("qT_ready", 1)
        s_rps, s_right, s_tree = sig("routers_done", 1), sig("right_ready", 1), sig("tree_steps", 1 + LEVELS)
        s_lps, s_leafT = sig("leaves_turned", 1), sig("leafT_ready", 1)
        s_vps, s_retT, s_yps, s_y = sig("values_done", 1), sig("retT_ready", 1), sig("out_done", 1), sig("x_updated", 2)
        is_pair = lambda g: not isinstance(g, int) or 0 <= g < PAIRS

        def turns(eng, turn):
            for t in range(3):
                turn(t)
            with eng.Fori(3, PAIRS, 1) as t:
                turn(t)
            for t in range(PAIRS, PAIRS + 3):
                turn(t)

        with nc.Block() as block:
            @block.sync
            def _(sp):
                for dst, what in loads:
                    sp.dma_start(dst[:], dram[what]).then_inc(s_w.sem, 16)

            @block.gpsimd
            def _(pool):
                core.clear_spent(pool)
                norm_x.on_gpsimd(pool)

            @block.tensor
            def _(pe):
                pe.wait_ge(s_w.sem, 16 * len(loads))

                def turn_rows(dst, src):
                    for i in range(2):
                        for c in range(DC):
                            mm = pe.transpose(dst[:, c, i, 0:S], src[:, i, c * P:(c + 1) * P], ident[0:S, 0:S])
                    return mm

                def product(dst, w, src):
                    for f in range(DC):
                        for c in range(DC):
                            mm = pe.matmul(dst[:, f, :, 0:S], w[:, c, f * P:(f + 1) * P], src[:, c],
                                           start=(c == 0), stop=(c == DC - 1))
                    return mm

                def turn(t):
                    if is_pair(t):
                        pe.wait_ge(s_xn.sem, s_xn.at(t, 1))
                        if has(t, 1):
                            pe.wait_ge(s_xT.sem, s_xT.at(t - 1))
                        turn_rows(x_ps, xn).then_inc(s_xps.sem, 1)
                    if is_pair(t - 3):
                        pe.wait_ge(s_retT.sem, s_retT.at(t - 3))
                        if has(t, 4):
                            pe.wait_ge(s_y.sem, s_y.at(t - 4, 1))
                        for i in range(2):
                            for c in range(DC):
                                pe.matmul(y_ps[:, i, :], retT[:, c, i, :], wout[:, c, :], start=(c == 0), stop=False)
                            mm = pe.matmul(y_ps[:, i, :], ones[0:1, 0:S], bout[:], start=False, stop=True)
                        mm.then_inc(s_yps.sem, 1)
                    if is_pair(t - 1):
                        pe.wait_ge(s_qT.sem, s_qT.at(t - 1))
                        if has(t, 2):
                            pe.wait_ge(s_right.sem, s_right.at(t - 2))
                        for i in range(2):
                            for c in range(DC):
                                mm = pe.matmul(r_ps[:, i, 0:M - 1], qT[:, c, i, :], routers[:, c, :],
                                               start=(c == 0), stop=(c == DC - 1))
                        mm.then_inc(s_rps.sem, 1)
                    if is_pair(t - 2):
                        pe.wait_ge(s_tree.sem, s_tree.at(t - 2, LEVELS))
                        if has(t, 3):
                            pe.wait_ge(s_leafT.sem, s_leafT.at(t - 3))
                        turn_rows(l_ps, paths[-1]).then_inc(s_lps.sem, 1)
                    if is_pair(t):
                        pe.wait_ge(s_xT.sem, s_xT.at(t))
                        if has(t, 1):
                            pe.wait_ge(s_qT.sem, s_qT.at(t - 1))
                        product(q_ps, wq, xT).then_inc(s_qps.sem, 1)
                    if is_pair(t - 2):
                        pe.wait_ge(s_leafT.sem, s_leafT.at(t - 2))
                        if has(t, 3):
                            pe.wait_ge(s_retT.sem, s_retT.at(t - 3))
                        product(v_ps, leaves, leafT).then_inc(s_vps.sem, 1)

                turns(pe, turn)

            @block.scalar
            def _(act):
                def copy(dst, src):
                    return act.activation(dst[:], src[:, :, :, 0:S], ACT.Copy)

                def turn(t):
                    if is_pair(t):
                        act.wait_ge(s_xps.sem, s_xps.at(t))
                        copy(xT, x_ps).then_inc(s_xT.sem, 1)
                    if is_pair(t - 1):
                        act.wait_ge(s_rps.sem, s_rps.at(t - 1))
                        if has(t, 2):
                            act.wait_ge(s_tree.sem, s_tree.at(t - 2, LEVELS))
                        act.activation(sides[:, :, 0:M - 1, 1], r_ps[:, :, 0:M - 1], ACT.Sigmoid)\
                            .then_inc(s_right.sem, 1)
                    if is_pair(t - 2):
                        act.wait_ge(s_lps.sem, s_lps.at(t - 2))
                        copy(leafT, l_ps).then_inc(s_leafT.sem, 1)
                    if is_pair(t):
                        act.wait_ge(s_qps.sem, s_qps.at(t))
                        copy(qT, q_ps).then_inc(s_qT.sem, 1)
                    if is_pair(t - 2):
                        act.wait_ge(s_vps.sem, s_vps.at(t - 2))
                        copy(retT, v_ps).then_inc(s_retT.sem, 1)

                turns(act, turn)

            @block.vector
            def _(dve):
                def normed(g):
                    if has(g, 1):
                        dve.wait_ge(s_xps.sem, s_xps.at(g - 1))
                    for i in range(2):
                        b = g * 2 + i
                        dve.tensor_scalar(xn[:, i, :], x_all[:, b, :], norm_x.mv[:, b, 0:1], norm_x.rstd[:, b, :],
                                          ALU.subtract, ALU.mult).then_inc(s_xn.sem, 1)

                def tree(g):
                    dve.wait_ge(s_right.sem, s_right.at(g))
                    dve.tensor_scalar(sides[:, :, 0:M - 1, 0], sides[:, :, 0:M - 1, 1], -1.0, 1.0,
                                      ALU.mult, ALU.add).then_inc(s_tree.sem, 1)
                    for level in range(LEVELS):
                        n = 2 ** level
                        dve.wait_ge(s_tree.sem, s_tree.at(g, level))
                        if level == LEVELS - 1 and has(g, 1):
                            dve.wait_ge(s_lps.sem, s_lps.at(g - 1))
                        here = sides[:, :, n - 1:2 * n - 1, :]
                        below = paths[level][:].rearrange("s i (n two) -> s i n two", two=2)
                        if level == 0:
                            ins = dve.tensor_copy(below, here)
                        else:
                            ins = dve.tensor_tensor(below, paths[level - 1][:].unsqueeze(3)
                                                    .to_broadcast([S, 2, n, 2]), here, ALU.mult)
                        ins.then_inc(s_tree.sem, 1)

                def turn(t):
                    if is_pair(t - 3):
                        dve.wait_ge(s_yps.sem, s_yps.at(t - 3))
                        for i in range(2):
                            b = (t - 3) * 2 + i
                            dve.scalar_tensor_tensor(out=x_all[:, b, :], in0=y_ps[:, i, :], scalar=gate,
                                                     in1=x_all[:, b, :], op0=ALU.mult, op1=ALU.add)\
                                .then_inc(s_y.sem, 1)
                    if is_pair(t - 1):
                        tree(t - 1)
                    if is_pair(t + 1) and (not isinstance(t, int) or t + 1 < PAIRS):
                        normed(t + 1)

                norm_x.on_vector(dve)
                dve.wait_ge(norm_x.ready, 1)
                normed(0)
                for t in range(3):
                    turn(t)
                with dve.Fori(3, PAIRS - 1, 1) as t:
                    turn(t)
                for t in range(PAIRS - 1, PAIRS + 3):
                    turn(t)


class Plan:

    SLOTS = 256
    PAIRS = 2 * B * S

    def __init__(self, core, ctx, layer, E):
        self.E, self.SC = E, self.SLOTS // P
        self.tiles = (self.PAIRS + E * (self.SLOTS - 1)) // self.SLOTS
        sb = lambda n, s, d=F32: ctx.enter_context(core.nc.sbuf_tensor(f"p{layer}_{n}", s, d))
        self.xn = sb("xn", [S, B, D])
        self.slot = sb("slot", [S, 2 * B], mybir.dt.uint32)
        self.share = sb("share", [S, B, 2])
        self.expert = sb("expert", [1, self.tiles], I32)
        dram = lambda n: core.nc.dram_tensor(f"p{layer}_{n}", (self.tiles * self.SLOTS, D), F32, kind="Internal").ap()
        self.rows_in, self.rows_out = dram("rows_in"), dram("rows_out")


def route_stage(core, layer, E, xT_all=None, mix=None, plan=None):
    nc, dram, x_all, ident, ones = core.nc, core.dram, core.x_all, core.ident, core.ones
    tag = f"r{layer}"
    name = lambda n: f"L{layer}f_{n}"
    gate = core.gates[:, 4 + layer:5 + layer]
    dense = plan is None
    RMS_EPS = float(np.finfo(np.float32).eps)
    with ExitStack() as ctx:
        sb, ps = sub_names(ctx, nc, tag)
        sig = core.new_signals(tag)
        wg = sb("wg", [P, DC, E])
        loads = [(wg[:], dram[name("gateT")])]
        if dense:
            cents = sb("cents", [8, D])
            b2 = sb("b2", [E, D])
            loads += [(cents[:], dram[name("centroids")]), (b2[:], dram[name("b2")])]
            sq, norm, cn = sb("sq", [S, D]), sb("norm", [S, 2, 1]), sb("cn", [8, D])
            cnT = sb("cnT", [P, DC, 8])
            pick = sb("pick", [S, B, E])
            mixT = sb("mixT", [E, 2, S])
        else:
            T, LIMITS = plan.tiles, -(-B * S // plan.SLOTS)
            bg = sb("bg", [1, E])
            number, below = sb("number", [S, E]), sb("below", [S, S])
            limits, before, tile_no = sb("limits", [S, LIMITS]), sb("before", [S, E, E]), sb("tile_no", [1, T])
            loads += [(bg[:], dram[name("gate_bias")]), (number[:], dram[f"numbers{E}"].to_broadcast([S, E])),
                      (below[:], dram["below"]), (limits[:], dram["limits"].to_broadcast([S, LIMITS])),
                      (before[:].rearrange("p e f -> p (e f)"), dram[f"before{E}"].to_broadcast([S, E * E])),
                      (tile_no[:], dram[f"tile_no{E}"])]
            if layer == 2:
                ln_w = sb("ln_w", [P, DC])
                loads.append((ln_w[:], dram[name("ln_w")]))
            share = plan.share
            at, place = sb("at", [S, B, 8], mybir.dt.uint32), sb("place", [S, B, 8])
            every_one = sb("every_one", [S, S])
            chosen = sb("chosen", [S, 2, B, E])
            total_a, total_b = sb("total_a", [S, 2 * B, E]), sb("total_b", [S, 2 * B, E])
            over, tiles_of = sb("over", [S, E, LIMITS]), sb("tiles_of", [S, E])
            earlier, first, ends = sb("earlier", [S, E, E]), sb("first", [S, E]), sb("ends", [S, E])
            passed, slot_f = sb("passed", [1, T, E]), sb("slot_f", [S, 2 * B])
            expert_f = sb("expert_f", [1, T])
            count_ps = ps("count_ps", [S, 2, 512])
        norm_x = Norm(core, sb, sig)
        mv, rstd, rms = norm_x.mv, norm_x.rstd, sb("rms", [S, B, 1])
        xn, xT = sb("xn", [S, 2, D]), sb("xT", [P, 2, DC, S])
        logits = sb("logits", [S, B, E])
        best, total = sb("best", [S, B, 8]), sb("total", [S, B])
        x_ps, l_ps = ps("x_ps", [P, 2, 512]), ps("l_ps", [S, 2, 512])
        if dense:
            m_ps, y_ps = ps("m_ps", [P, 2, 512]), ps("y_ps", [S, 2, 512])
        s_w = sig("weights_in", 1)
        twice = layer in (1, 2)
        s_xn = sig("xn_ready", 1)
        s_rms, s_rms_root, s_l1 = sig("rms_steps", 1), sig("rms_root", 1), sig("route_part", 1)
        x_copies = DC if layer == 2 else 1
        s_xps, s_xT, s_all = sig("x_turned", 1), sig("xT_ready", x_copies), sig("x_kept", 1)
        s_lps, s_l, s_tick = sig("logits_done", 1), sig("logits_copied", 1), sig("tick", 0)
        s_cos = sig("cosine_part", 1)
        s_rt, s_to_act, s_act = sig("route_steps", 1), sig("for_scalar", 1), sig("scalar_done", 1)
        s_mps, s_m, s_yps, s_y = sig("mix_turned", 1), sig("mixT_ready", 1), sig("bias_done", 1), sig("bias_added", 1)
        s_mix = sig("mix_ready", 1)
        s_chosen, s_count, s_zero = sig("chosen_ready", 1), sig("counts_done", 1), sig("slots_zeroed", 1)
        cosine = dense

        with nc.Block() as block:
            @block.sync
            def _(sp):
                for dst, src in loads:
                    sp.dma_start(dst, src).then_inc(s_w.sem, 16)
                if not dense:
                    sp.wait_ge(s_zero.sem, 1)
                    sp.dma_start(plan.rows_in.rearrange("(c p) d -> p c d", p=P),
                                 core.zeros[:].unsqueeze(1).to_broadcast([P, T * plan.SC, D])).then_inc(s_zero.sem, 16)
                    sp.wait_ge(s_zero.sem, 17)

            @block.gpsimd
            def _(pool):
                core.clear_spent(pool)
                if not dense:
                    pool.memset(core.zeros[:], 0.0).then_inc(s_zero.sem, 1)
                if cosine:
                    pool.wait_ge(s_cos.sem, 2)
                    pool.tensor_tensor(norm[0:8, 0, :], norm[0:8, 0, :], core.minus_half[0:8, :], ALU.pow)\
                        .then_inc(s_cos.sem, 1)

                norm_x.on_gpsimd(pool)
                if twice:
                    pool.wait_ge(s_rms.sem, 3)
                    core.inverse_root(pool, rms).then_inc(s_rms_root.sem, 1)

            @block.tensor
            def _(pe):
                pe.wait_ge(s_w.sem, 16 * len(loads))
                if cosine:
                    pe.wait_ge(s_cos.sem, 4)
                    for c in range(DC):
                        mm = pe.transpose(x_ps[:, 0, c * 8:(c + 1) * 8], cn[:, c * P:(c + 1) * P], ident[0:8, 0:8])
                    mm.then_inc(s_cos.sem, 1)
                    pe.wait_ge(s_cos.sem, 6)

                def turn(b, par):
                    pe.wait_ge(s_xn.sem, s_xn.at(b))
                    if has(b, 2):
                        pe.wait_ge(s_xT.sem, s_xT.at(b - 2, x_copies - 1))
                    for c in range(DC):
                        mm = pe.transpose(x_ps[:, par, c * S:(c + 1) * S], xn[:, par, c * P:(c + 1) * P],
                                          ident[0:S, 0:S])
                    mm.then_inc(s_xps.sem, 1)

                def score(b, par):
                    pe.wait_ge(s_xT.sem, s_xT.at(b, x_copies - 1))
                    if has(b, 2):
                        pe.wait_ge(s_l.sem, s_l.at(b - 2))
                    for c in range(DC):
                        mm = pe.matmul(l_ps[:, par, 0:E], xT[:, par, c, :], wg[:, c, :], start=(c == 0),
                                       stop=(cosine and c == DC - 1))
                    if cosine:
                        for c in range(DC):
                            mm = pe.matmul(l_ps[:, par, 8:16], xT[:, par, c, :], cnT[:, c, :], start=(c == 0),
                                           stop=(c == DC - 1))
                    else:
                        mm = pe.matmul(l_ps[:, par, 0:E], ones[0:1, 0:S], bg[:], start=False, stop=True)
                    mm.then_inc(s_lps.sem, 1)

                def body(b, par):
                    turn(b, par)
                    if has(b, 1):
                        score(b - 1, 1 - par)
                each(pe, body)
                score(B - 1, 1)
                if dense:
                    pe.wait_ge(s_mix.sem, 1)
                    for b in range(B):
                        if b >= 2:
                            pe.wait_ge(s_m.sem, b - 1)
                        pe.transpose(m_ps[0:E, b % 2, 0:S], mix[:, b, :], ident[0:S, 0:S]).then_inc(s_mps.sem, 1)
                        pe.wait_ge(s_m.sem, b + 1)
                        if b >= 2:
                            pe.wait_ge(s_y.sem, b - 1)
                        pe.matmul(y_ps[:, b % 2, 0:D], mixT[:, b % 2, :], b2[:], start=True, stop=True)\
                            .then_inc(s_yps.sem, 1)
                else:
                    pe.wait_ge(s_chosen.sem, 1)
                    pairs = chosen[:].rearrange("s k b e -> s (k b e)")
                    for i, w in enumerate((below, every_one)):
                        mm = pe.matmul(count_ps[:, i, 0:2 * B * E], w[:], pairs, start=True, stop=True)
                    mm.then_inc(s_count.sem, 1)

            @block.scalar
            def _(act):
                act.wait_ge(s_w.sem, 16 * len(loads))
                if cosine:
                    act.wait_ge(s_cos.sem, 5)
                    act.activation(cnT[:], x_ps[:, 0, 0:DC * 8].rearrange("p (c e) -> p c e", c=DC), ACT.Copy)\
                        .then_inc(s_cos.sem, 1)

                def body(b, par):
                    act.wait_ge(s_xps.sem, s_xps.at(b))
                    if has(b, 2):
                        act.wait_ge(s_lps.sem, s_lps.at(b - 2))
                        act.wait_ge(s_all.sem, s_all.at(b - 2))
                    if layer == 2:
                        for c in range(DC):
                            act.activation(xT[:, par, c, :], x_ps[:, par, c * S:(c + 1) * S], ACT.Copy,
                                           scale=ln_w[:, c:c + 1]).then_inc(s_xT.sem, 1)
                    else:
                        act.activation(xT[:, par], x_ps[:, par, 0:DC * S].rearrange("p (c s) -> p c s", c=DC),
                                       ACT.Copy).then_inc(s_xT.sem, 1)
                    if dense:
                        act.wait_ge(s_xT.sem, s_xT.at(b, x_copies - 1))
                        act.sem_inc(s_tick.sem, 1)
                        act.activation(xT_all[:, :, b, :], xT[:, par, :, :], ACT.Copy).then_inc(s_all.sem, 1)
                    else:
                        act.activation(plan.xn[:, b, :], xn[:, par, :], ACT.Copy).then_inc(s_all.sem, 1)
                each(act, body)
                what = pick[:] if dense else share[:, :, 1] if layer == 2 else logits[:]
                act.wait_ge(s_to_act.sem, 1)
                act.activation(what, what, ACT.Sigmoid if layer == 3 else ACT.Exp).then_inc(s_act.sem, 1)
                if dense:
                    for b in range(B):
                        act.wait_ge(s_mps.sem, b + 1)
                        if b >= 2:
                            act.wait_ge(s_yps.sem, b - 1)
                        act.activation(mixT[:, b % 2, :], m_ps[0:E, b % 2, 0:S], ACT.Copy).then_inc(s_m.sem, 1)

            @block.vector
            def _(dve):
                if not dense:
                    dve.memset(every_one[:], 1.0)
                dve.wait_ge(s_w.sem, 16 * len(loads))
                if cosine:
                    dve.tensor_tensor_reduce(out=cn[:], in0=cents[:], in1=cents[:], scale=1.0, scalar=0.0,
                                             op0=ALU.mult, op1=ALU.add, accum_out=norm[0:8, 0, :])\
                        .then_inc(s_cos.sem, 1)
                    dve.wait_ge(s_cos.sem, 1)
                    dve.tensor_scalar(norm[0:8, 0, :], norm[0:8, 0, :], 1e-24, None, ALU.max).then_inc(s_cos.sem, 1)
                    dve.wait_ge(s_cos.sem, 3)
                    dve.tensor_scalar(cn[:], cents[:], norm[0:8, 0, :], None, ALU.mult).then_inc(s_cos.sem, 1)

                norm_x.on_vector(dve)
                dve.wait_ge(norm_x.ready, 1)
                by = rstd
                if twice:
                    dve.tensor_tensor(rms[:], rstd[:], rstd[:], ALU.mult).then_inc(s_rms.sem, 1)
                    dve.wait_ge(s_rms.sem, 1)
                    dve.tensor_tensor(rms[:], rms[:], mv[:, :, 1:2], ALU.mult).then_inc(s_rms.sem, 1)
                    dve.wait_ge(s_rms.sem, 2)
                    if layer == 2:
                        dve.tensor_scalar(rms[:], rms[:], RMS_EPS, None, ALU.add).then_inc(s_rms.sem, 1)
                    else:
                        dve.tensor_scalar(rms[:], rms[:], float(D), 1e-24, ALU.mult, ALU.max).then_inc(s_rms.sem, 1)
                    dve.wait_ge(s_rms_root.sem, 1)
                if layer == 2:
                    dve.tensor_tensor(rms[:], rms[:], rstd[:], ALU.mult).then_inc(s_rms.sem, 1)
                    dve.wait_ge(s_rms.sem, 4)
                    by = rms

                def apply(b, par):
                    if has(b, 2):
                        if not dense:
                            dve.wait_ge(s_all.sem, s_all.at(b - 2))
                        dve.wait_ge(s_xps.sem, s_xps.at(b - 2))
                    dve.tensor_scalar(xn[:, par, :], x_all[:, b, :], mv[:, b, 0:1], by[:, b, :],
                                      ALU.subtract, ALU.mult).then_inc(s_xn.sem, 1)

                def take(b, par):
                    dve.wait_ge(s_lps.sem, s_lps.at(b))
                    if cosine:
                        dve.tensor_scalar(logits[:, b, :], l_ps[:, par, 0:E], 1.0, None, ALU.mult)\
                            .then_inc(s_l1.sem, 1)
                        dve.wait_ge(s_l1.sem, s_l1.at(b))
                        dve.scalar_tensor_tensor(out=logits[:, b, :], in0=l_ps[:, par, 8:16],
                                                 scalar=rms[:, b, :], in1=logits[:, b, :],
                                                 op0=ALU.mult, op1=ALU.add).then_inc(s_l.sem, 1)
                    else:
                        dve.tensor_scalar(logits[:, b, :], l_ps[:, par, 0:E], 1.0, None, ALU.mult)\
                            .then_inc(s_l.sem, 1)

                def body(b, par):
                    if more(b):
                        apply(b + 1, 1 - par)
                    if has(b, 1):
                        take(b - 1, 1 - par)
                apply(0, 0)
                each(dve, body)
                take(B - 1, 1)

                steps = [0]

                def done(ins):
                    steps[0] += 1
                    ins.then_inc(s_rt.sem, 1)
                    dve.wait_ge(s_rt.sem, steps[0])

                over_experts = lambda t: t.unsqueeze(2).to_broadcast([S, B, E])
                dve.wait_ge(s_l.sem, B)
                if layer == 3:
                    dve.sem_inc(s_to_act.sem, 1)
                    dve.wait_ge(s_act.sem, 1)
                for b in range(B):
                    last = dve.max(best[:, b, :], logits[:, b, :])
                done(last)
                if dense:
                    done(dve.tensor_tensor(pick[:], logits[:], over_experts(best[:, :, 0]), ALU.subtract))
                    dve.sem_inc(s_to_act.sem, 1)
                    done(dve.tensor_tensor(logits[:], logits[:], over_experts(best[:, :, 1]), ALU.is_ge))
                    dve.wait_ge(s_act.sem, 1)
                    done(dve.tensor_tensor(pick[:], pick[:], logits[:], ALU.mult))
                    done(dve.tensor_reduce(total[:], pick[:], AX.X, ALU.add))
                    done(dve.reciprocal(total[:], total[:]))
                    done(dve.tensor_tensor(mix[:], pick[:], over_experts(total[:]), ALU.mult))
                    done(dve.tensor_scalar(mix[:], mix[:], gate, None, ALU.mult))
                    dve.sem_inc(s_mix.sem, 1)
                    for b in range(B):
                        dve.wait_ge(s_yps.sem, b + 1)
                        dve.tensor_tensor(x_all[:, b, :], x_all[:, b, :], y_ps[:, b % 2, 0:D], ALU.add)\
                            .then_inc(s_y.sem, 1)
                else:
                    for b in range(B):
                        last = dve.max_index(at[:, b, :], best[:, b, :], logits[:, b, :])
                    done(last)
                    done(dve.tensor_copy(place[:], at[:]))
                    every = number[:].unsqueeze(1).to_broadcast([S, B, E])
                    for k in range(2):
                        ins = dve.tensor_tensor(chosen[:, k], every, over_experts(place[:, :, k]), ALU.is_equal)
                    done(ins)
                    dve.sem_inc(s_chosen.sem, 1)
                    if layer == 2:
                        done(dve.tensor_tensor(share[:, :, 1], best[:, :, 1], best[:, :, 0], ALU.subtract))
                        dve.sem_inc(s_to_act.sem, 1)
                        dve.wait_ge(s_act.sem, 1)
                        done(dve.tensor_scalar(total[:], share[:, :, 1], 1.0, None, ALU.add))
                        done(dve.reciprocal(share[:, :, 0], total[:]))
                        done(dve.tensor_tensor(share[:, :, 1], share[:, :, 1], share[:, :, 0], ALU.mult))
                    else:
                        done(dve.tensor_tensor(total[:], best[:, :, 0], best[:, :, 1], ALU.add))
                        done(dve.tensor_scalar(total[:], total[:], 1e-20, None, ALU.add))
                        done(dve.reciprocal(total[:], total[:]))
                        for k in range(2):
                            done(dve.tensor_tensor(share[:, :, k], best[:, :, k], total[:], ALU.mult))
                    done(dve.tensor_scalar(share[:], share[:], gate, None, ALU.mult))

                    dve.wait_ge(s_count.sem, 1)
                    in_column = count_ps[:, 1, 0:2 * B * E].rearrange("s (c e) -> s c e", e=E)
                    above = count_ps[:, 0, 0:2 * B * E].rearrange("s (c e) -> s c e", e=E)
                    done(dve.tensor_copy(total_a[:], in_column))
                    now, new, step = total_a, total_b, 1
                    while step < 2 * B:
                        dve.tensor_copy(new[:, 0:step], now[:, 0:step])
                        done(dve.tensor_tensor(new[:, step:], now[:, step:], now[:, 0:2 * B - step], ALU.add))
                        now, new, step = new, now, 2 * step
                    counts = now[:, 2 * B - 1, :].unsqueeze(2).to_broadcast([S, E, LIMITS])
                    done(dve.tensor_tensor(over[:], counts, limits[:].unsqueeze(1).to_broadcast([S, E, LIMITS]),
                                           ALU.is_gt))
                    done(dve.tensor_reduce(tiles_of[:], over[:], AX.X, ALU.add))
                    done(dve.tensor_tensor(earlier[:], before[:], tiles_of[:].unsqueeze(1).to_broadcast([S, E, E]),
                                           ALU.mult))
                    done(dve.tensor_reduce(first[:], earlier[:], AX.X, ALU.add))
                    done(dve.tensor_tensor(ends[:], first[:], tiles_of[:], ALU.add))
                    done(dve.tensor_tensor(passed[:], tile_no[:].unsqueeze(2).to_broadcast([1, T, E]),
                                           ends[0:1].unsqueeze(1).to_broadcast([1, T, E]), ALU.is_ge))
                    done(dve.tensor_reduce(expert_f[:], passed[:], AX.X, ALU.add))
                    done(dve.tensor_scalar(expert_f[:], expert_f[:], float(E - 1), None, ALU.min))
                    done(dve.tensor_copy(plan.expert[:], expert_f[:]))
                    done(dve.tensor_tensor(new[:], now[:], in_column, ALU.subtract))
                    done(dve.tensor_tensor(new[:], new[:], above, ALU.add))
                    done(dve.tensor_scalar(first[:], first[:], float(plan.SLOTS), None, ALU.mult))
                    done(dve.tensor_tensor(new[:], new[:], first[:].unsqueeze(1).to_broadcast([S, 2 * B, E]), ALU.add))
                    done(dve.tensor_tensor(new[:], new[:], chosen[:].rearrange("s k b e -> s (k b) e"), ALU.mult))
                    done(dve.tensor_reduce(slot_f[:], new[:], AX.X, ALU.add))
                    done(dve.tensor_copy(plan.slot[:], slot_f[:]))


G = 4
GB = B // G
GN = GB * S


def small_experts_stage(core, xT_all, mix):
    nc, dram, x_all = core.nc, core.dram, core.x_all
    E = 8
    with ExitStack() as ctx:
        sb, ps = sub_names(ctx, nc, "e1")
        sig = core.new_signals("e1")
        w1, b1, w2 = sb("w1", [P, DC, E * P]), sb("b1", [P, E]), sb("w2", [P, E, D])
        loads = [(w1, "L1f_w1"), (b1, "L1f_b1"), (w2, "L1f_w2")]
        hid = sb("hid", [P, 2, GN])
        u_ps = ps("u_ps", [P, 2, 512])
        y_ps = ps("y_ps", [S, 2, GB, D])
        s_w = sig("weights_in", 1)
        s_up, s_gelu, s_down, s_y = sig("up_done", E), sig("gelu_done", E), sig("down_done", E), sig("added", E * GB)
        s_tick = sig("tick", 0)
        x_of = xT_all[:].rearrange("p c b s -> p c (b s)")
        with nc.Block() as block:
            @block.sync
            def _(sp):
                for dst, what in loads:
                    sp.dma_start(dst[:], dram[what]).then_inc(s_w.sem, 16)

            @block.gpsimd
            def _(pool):
                core.clear_spent(pool)

            def groups(eng, body):
                body(0)
                with eng.Fori(1, G, 1) as g:
                    body(g)

            @block.tensor
            def _(pe):
                pe.wait_ge(s_w.sem, 16 * len(loads))

                def down(g, e):
                    pe.wait_ge(s_gelu.sem, s_gelu.at(g, e))
                    if has(g, 1) or e >= 2:
                        pe.wait_ge(s_y.sem, s_y.at(g, GB * e + GB - 1) - 2 * GB)
                    for t in range(GB):
                        mm = pe.matmul(y_ps[:, e % 2, t, :], hid[:, e % 2, t * S:(t + 1) * S], w2[:, e, :],
                                       start=True, stop=True)
                    mm.then_inc(s_down.sem, 1)

                def body(g):
                    for e in range(E):
                        if has(g, 1) or e >= 2:
                            pe.wait_ge(s_gelu.sem, s_gelu.at(g, e) - 2)
                        for c in range(DC):
                            mm = pe.matmul(u_ps[:, e % 2, 0:GN], w1[:, c, e * P:(e + 1) * P],
                                           x_of[:, c, bass.ds(g * GN, GN)], start=(c == 0), stop=(c == DC - 1))
                        mm.then_inc(s_up.sem, 1)
                        if e > 0:
                            down(g, e - 1)
                    down(g, E - 1)
                groups(pe, body)

            @block.scalar
            def _(act):
                act.wait_ge(s_w.sem, 16 * len(loads))

                def body(g):
                    for e in range(E):
                        act.wait_ge(s_up.sem, s_up.at(g, e))
                        if has(g, 1) or e >= 2:
                            act.wait_ge(s_down.sem, s_down.at(g, e) - 2)
                        act.activation(hid[:, e % 2, :], u_ps[:, e % 2, 0:GN], ACT.Gelu, bias=b1[:, e:e + 1])\
                            .then_inc(s_gelu.sem, 1)
                groups(act, body)

            @block.vector
            def _(dve):
                def body(g):
                    for e in range(E):
                        dve.wait_ge(s_down.sem, s_down.at(g, e))
                        for t in range(GB):
                            b = g * GB + t
                            if e > 0:
                                dve.wait_ge(s_y.sem, s_y.at(g, (e - 1) * GB + t))
                            dve.scalar_tensor_tensor(out=x_all[:, b, :], in0=y_ps[:, e % 2, t, :],
                                                     scalar=mix[:, b, e:e + 1], in1=x_all[:, b, :],
                                                     op0=ALU.mult, op1=ALU.add).then_inc(s_y.sem, 1)
                groups(dve, body)


def experts_stage(core, layer, E, F, plan):
    nc, dram, x_all, ident = core.nc, core.dram, core.x_all, core.ident
    name = lambda n: f"L{layer}f_{n}"
    FC = -(-F // P)
    rows = [min(P, F - f * P) for f in range(FC)]
    T, SLOTS, SC = plan.tiles, plan.SLOTS, plan.SC
    biased = layer == 2
    RING, FETCH = 4, 8
    assert 2 * FC % RING == 0
    with ExitStack() as ctx:
        sb, ps = sub_names(ctx, nc, f"e{layer}")
        sig = core.new_signals(f"e{layer}")
        w1, w3, w2 = sb("w1", [P, 2, DC, F]), sb("w3", [P, 2, DC, F]), sb("w2", [P, 2, FC, D])
        loads = [(w1, "w1"), (w3, "w3"), (w2, "w2")]
        if biased:
            b1, b3, b2 = sb("b1", [P, 2, FC]), sb("b3", [P, 2, FC]), sb("b2", [P, 2, D])
            ln_w = sb("ln_w", [P, DC])
            loads += [(b1, "b1"), (b3, "b3")]
        x_in = sb("x_in", [P, 2, SC, D])
        xT = sb("xT", [P, DC, SLOTS])
        silu = sb("silu", [P, RING, SLOTS])
        hid = sb("hid", [P, FC, SLOTS])
        y_out = sb("y_out", [P, 2, SC, D])
        fetched = sb("fetched", [S, FETCH, D])
        x_ps, ab_ps, y_ps = ps("x_ps", [P, DC, SLOTS]), ps("ab_ps", [P, RING, 2, SLOTS]), ps("y_ps", [P, 2, SC, D])
        s_w = [sig(f"weights_in{i}", 1) for i in range(2)]
        s_ln = sig("ln_w_in", 1)
        s_scattered = sig("rows_scattered", 1)
        s_x = [sig(f"x_in{i}", 1) for i in range(2)]
        s_xps, s_xT = sig("x_turned", 1), sig("xT_ready", DC)
        s_up, s_silu, s_hid = sig("up_done", FC), sig("silu_done", FC), sig("hid_ready", FC)
        s_down, s_y = sig("down_done", 1), sig("y_copied", 1)
        s_stored = [sig(f"y_stored{i}", 1) for i in range(2)]
        s_fetched = [sig(f"fetched{i}", 1) for i in range(FETCH)]
        s_added = sig("added", 1)
        s_tick = [sig(f"tick{i}", 0) for i in range(2)]
        next_tile = lambda t: not isinstance(t, int) or t + 1 < T
        tile_rows = lambda d, t: d[bass.ds(t * SLOTS, SLOTS), :].rearrange("(c p) d -> p c d", p=P)

        def each_tile(eng, body):
            body(0, 0)
            body(1, 1)
            pairs = (T - 1) // 2
            with eng.Fori(1, pairs, 1) as j:
                body(j * 2, 0)
                body(j * 2 + 1, 1)
            for t in range(2 * pairs, T):
                body(t, t % 2)

        def weights_in(eng, t, par):
            eng.wait_ge(s_w[par].sem, half(t, par) * (len(loads) + biased))

        with nc.Block() as block:
            @block.gpsimd
            def _(pool):
                core.clear_spent(pool)
                for i in range(2 * B):
                    pool.indirect_dma_start(plan.rows_in, bass.IndirectOffsetOnAxis(plan.slot[:, i:i + 1], 0),
                                            plan.xn[:, i % B, :], None).then_inc(s_scattered.sem, 16)
                for par in range(2):
                    pool.wait_ge(s_stored[par].sem, 16 * len(range(par, T, 2)))
                for i in range(2 * B):
                    if i >= FETCH:
                        pool.wait_ge(s_added.sem, i - FETCH + 1)
                    pool.indirect_dma_start(fetched[:, i % FETCH, :], None, plan.rows_out,
                                            bass.IndirectOffsetOnAxis(plan.slot[:, i:i + 1], 0))\
                        .then_inc(s_fetched[i % FETCH].sem, 16)

            @block.sync
            def _(sp):
                if biased:
                    sp.dma_start(ln_w[:], dram[name("ln_w")]).then_inc(s_ln.sem, 16)

                def load_weights(t, par):
                    if has(t, 2):
                        sp.wait_ge(s_down.sem, s_down.at(t - 2))
                        sp.sem_inc(s_tick[0].sem, 1)
                    e = sp.value_load(plan.expert[0:1, bass.ds(t, 1)], min_val=0, max_val=E - 1)
                    for dst, what in loads:
                        sp.dma_start(dst[:, par], dram[name(what)][e]).then_inc(s_w[par].sem, 16)
                    if biased:
                        if has(t, 2):
                            sp.wait_ge(s_y.sem, s_y.at(t - 2))
                            sp.sem_inc(s_tick[0].sem, 1)
                        sp.dma_start(b2[:, par], dram[name("b2")][bass.ds(e, 1), :].to_broadcast([P, D]))\
                            .then_inc(s_w[par].sem, 16)

                def load_rows(t, par):
                    sp.dma_start(x_in[:, par], tile_rows(plan.rows_in, t)).then_inc(s_x[par].sem, 16)

                def body(t, par):
                    if has(t, 2):
                        load_weights(t, par)
                        load_rows(t, par)

                load_weights(0, 0)
                load_weights(1, 1)
                sp.wait_ge(s_scattered.sem, 16 * 2 * B)
                load_rows(0, 0)
                load_rows(1, 1)
                each_tile(sp, body)

            @block.tensor
            def _(pe):
                def turn(t, par):
                    pe.wait_ge(s_x[par].sem, half(t, par))
                    if has(t, 1):
                        pe.wait_ge(s_xT.sem, s_xT.at(t - 1, DC - 1))
                    for c in range(DC):
                        for h in range(SC):
                            mm = pe.transpose(x_ps[:, c, h * P:(h + 1) * P], x_in[:, par, h, c * P:(c + 1) * P],
                                              ident[:, :])
                    mm.then_inc(s_xps.sem, 1)

                def up(t, par):
                    weights_in(pe, t, par)
                    pe.wait_ge(s_xT.sem, s_xT.at(t, DC - 1))
                    for f in range(FC):
                        if has(t, 1) or f >= RING:
                            pe.wait_ge(s_hid.sem, s_hid.at(t, f) - RING)
                        for i, w in enumerate((w1, w3)):
                            for c in range(DC):
                                mm = pe.matmul(ab_ps[0:rows[f], (par * FC + f) % RING, i, :],
                                               w[:, par, c, f * P:f * P + rows[f]], xT[:, c, :],
                                               start=(c == 0), stop=(c == DC - 1))
                        mm.then_inc(s_up.sem, 1)

                def down(t, par):
                    if has(t, 2):
                        pe.wait_ge(s_y.sem, s_y.at(t - 2))
                    for h in range(SC):
                        for f in range(FC):
                            if h == 0:
                                pe.wait_ge(s_hid.sem, s_hid.at(t, f))
                            mm = pe.matmul(y_ps[:, par, h, :], hid[0:rows[f], f, h * P:(h + 1) * P],
                                           w2[0:rows[f], par, f, :], start=(f == 0), stop=(f == FC - 1))
                    mm.then_inc(s_down.sem, 1)

                def body(t, par):
                    up(t, par)
                    if next_tile(t):
                        turn(t + 1, 1 - par)
                    down(t, par)

                turn(0, 0)
                each_tile(pe, body)

            @block.scalar
            def _(act):
                def copy_xT(t):
                    act.wait_ge(s_xps.sem, s_xps.at(t))
                    for c in range(DC):
                        act.activation(xT[:, c, :], x_ps[:, c, :], ACT.Copy, scale=ln_w[:, c:c + 1] if biased else 1.0)\
                            .then_inc(s_xT.sem, 1)

                def body(t, par):
                    if biased:
                        weights_in(act, t, par)
                    for f in range(FC):
                        r, i = rows[f], (par * FC + f) % RING
                        act.wait_ge(s_up.sem, s_up.at(t, f))
                        if has(t, 1) or f >= RING:
                            act.wait_ge(s_hid.sem, s_hid.at(t, f) - RING)
                        act.activation(silu[0:r, i, :], ab_ps[0:r, i, 0, :], ACT.Silu,
                                       bias=b1[0:r, par, f:f + 1] if biased else 0.0).then_inc(s_silu.sem, 1)
                    if next_tile(t):
                        copy_xT(t + 1)
                    act.wait_ge(s_y.sem, s_y.at(t))
                    act.dma_start(tile_rows(plan.rows_out, t), y_out[:, par]).then_inc(s_stored[par].sem, 16)

                if biased:
                    act.wait_ge(s_ln.sem, 16)
                copy_xT(0)
                each_tile(act, body)

            @block.vector
            def _(dve):
                def body(t, par):
                    if biased:
                        weights_in(dve, t, par)
                    for f in range(FC):
                        r, i = rows[f], (par * FC + f) % RING
                        dve.wait_ge(s_silu.sem, s_silu.at(t, f))
                        if biased:
                            dve.scalar_tensor_tensor(out=hid[0:r, f, :], in0=ab_ps[0:r, i, 1, :],
                                                     scalar=b3[0:r, par, f:f + 1], in1=silu[0:r, i, :],
                                                     op0=ALU.add, op1=ALU.mult).then_inc(s_hid.sem, 1)
                        else:
                            dve.tensor_tensor(hid[0:r, f, :], ab_ps[0:r, i, 1, :], silu[0:r, i, :], ALU.mult)\
                                .then_inc(s_hid.sem, 1)
                    dve.wait_ge(s_down.sem, s_down.at(t))
                    if has(t, 2):
                        dve.wait_ge(s_stored[par].sem, half(t, par) - 16)
                    if biased:
                        dve.tensor_tensor(y_out[:, par], y_ps[:, par], b2[:, par, :].unsqueeze(1)
                                          .to_broadcast([P, SC, D]), ALU.add).then_inc(s_y.sem, 1)
                    else:
                        dve.tensor_copy(y_out[:, par], y_ps[:, par]).then_inc(s_y.sem, 1)

                each_tile(dve, body)
                for i in range(2 * B):
                    b, k = i % B, i // B
                    dve.wait_ge(s_fetched[i % FETCH].sem, 16 * (i // FETCH + 1))
                    if k == 1:
                        dve.wait_ge(s_added.sem, i - B + 1)
                    dve.scalar_tensor_tensor(out=x_all[:, b, :], in0=fetched[:, i % FETCH, :],
                                             scalar=plan.share[:, b, k:k + 1], in1=x_all[:, b, :],
                                             op0=ALU.mult, op1=ALU.add).then_inc(s_added.sem, 1)


def moe(core, layer, E, F):
    with ExitStack() as ctx:
        if layer == 1:
            xT_all = ctx.enter_context(core.nc.sbuf_tensor("xT_all", [P, DC, B, S], F32))
            mix = ctx.enter_context(core.nc.sbuf_tensor("mix", [S, B, E], F32))
            route_stage(core, layer, E, xT_all=xT_all, mix=mix)
            small_experts_stage(core, xT_all, mix)
        else:
            plan = Plan(core, ctx, layer, E)
            route_stage(core, layer, E, plan=plan)
            experts_stage(core, layer, E, F, plan)


def store_stage(core, out):
    nc = core.nc
    s_out = core.stack.enter_context(nc.semaphore("x_stored"))
    with nc.Block() as block:
        @block.sync
        def _(sp):
            sp.dma_start(out.rearrange("b s d -> s b d"), core.x_all[:]).then_inc(s_out, 16)
            sp.wait_ge(s_out, 16)


def flamingo(nc, dram, out, stages=8):
    with ExitStack() as stack:
        core = Core(nc, dram, stack)
        setup_stage(core)
        todo = [
            lambda: attention_stage(core, 0, heads=8, hd=32, scale=D ** -0.5, kan=True),
            lambda: tree_stage(core),
            lambda: attention_stage(core, 1, heads=16, hd=64, scale=64 ** -0.5, mask="keys"),
            lambda: moe(core, 1, 8, 128),
            lambda: attention_stage(core, 2, heads=16, hd=16, scale=0.25, rope=True),
            lambda: moe(core, 2, 8, 1024),
            lambda: attention_stage(core, 3, heads=16, hd=16, scale=0.25, mask="scores"),
            lambda: moe(core, 3, 9, 704),
        ]
        for stage in todo[:stages]:
            stage()
        store_stage(core, out)


def host_layout(inputs):
    get = lambda n: np.asarray(inputs[n])

    def chunks(a):
        return np.ascontiguousarray(a.reshape(a.shape[0] // P, P, *a.shape[1:]).swapaxes(0, 1))

    turned = lambda a: chunks(np.ascontiguousarray(a.T))
    row = lambda a: np.ascontiguousarray(a.reshape(1, -1))
    col = lambda a: np.ascontiguousarray(a.reshape(-1, P).T)
    o = {
        "x": get("x"),
        "gates": np.concatenate([get("g_xattn"), get("g_ffn")]).reshape(1, 8),
        "ident": np.eye(P, dtype=np.float32),
        "ctxT": np.ascontiguousarray(get("ctx_1024").transpose(0, 2, 1).reshape(B, DC, P, SK).transpose(0, 2, 1, 3)),
        "mask_keys": np.ascontiguousarray(get("mask_BxS2_bf1")).view(np.uint8).reshape(B, 1, SK),
        "mask_scores": get("mask_1x1xSxS2_ik1")[0, 0],
        "below": np.triu(np.ones((S, S), np.float32), 1),
        "limits": np.arange(-(-B * S // Plan.SLOTS), dtype=np.float32).reshape(1, -1) * Plan.SLOTS,
        "numbers8": np.arange(8, dtype=np.float32).reshape(1, 8),
        "numbers9": np.arange(9, dtype=np.float32).reshape(1, 9),
    }
    for e in (8, 9):
        o[f"before{e}"] = np.tril(np.ones((e, e), np.float32), -1).reshape(1, -1)
        o[f"tile_no{e}"] = np.arange((Plan.PAIRS + e * (Plan.SLOTS - 1)) // Plan.SLOTS, dtype=np.float32).reshape(1, -1)
    for n in "qkv":
        o[f"L0x_w{n}T"] = turned(get(f"L0_xattn_w{n}"))
        o[f"L0x_b{n}"] = col(get(f"L0_xattn_b{n}"))
    o["L0x_bqrow"], o["L0x_bvrow"] = row(get("L0_xattn_bq")), row(get("L0_xattn_bv"))
    o["L0x_ln_g"], o["L0x_ln_b"] = col(get("L0_xattn_ln_g")), col(get("L0_xattn_ln_b"))
    o["L0x_base_wT"] = turned(get("L0_xattn_kan_base_w"))
    o["L0x_spline_wT"] = chunks(get("L0_xattn_kan_spline_w").transpose(1, 2, 0))
    o["L0x_scalerT"] = turned(get("L0_xattn_kan_spline_scaler"))
    o["L0x_centers"] = np.ascontiguousarray(np.broadcast_to(np.arange(8, dtype=np.float32) - 3.5, (P, 8)))
    o["L0f_wqT"], o["L0f_routersT"] = turned(get("L0_ffn_Wq")), turned(get("L0_ffn_routers"))
    o["L0f_leaves"], o["L0f_woutT"] = chunks(get("L0_ffn_leaf_values")), turned(get("L0_ffn_Wout_w"))
    o["L0f_bout"] = row(get("L0_ffn_Wout_b"))
    o["L1x_wqT"] = turned(get("L1_xattn_Wq"))
    o["L1x_wkT"], o["L1x_wvT"] = turned(get("L1_xattn_Wkv")[:1024]), turned(get("L1_xattn_Wkv")[1024:])
    o["L1x_woT"], o["L1x_bo"] = turned(get("L1_xattn_Wout")), row(get("L1_xattn_b_out"))
    o["L1f_gateT"], o["L1f_centroids"] = turned(get("L1_ffn_w_route")), get("L1_ffn_centroids")
    o["L1f_b2"] = get("L1_ffn_b2")
    o["L1f_w1"] = chunks(get("L1_ffn_w1").transpose(1, 0, 2).reshape(D, 8 * P))
    o["L1f_b1"] = np.ascontiguousarray(get("L1_ffn_b1").T)
    o["L1f_w2"] = np.ascontiguousarray(get("L1_ffn_w2").transpose(1, 0, 2))
    for layer in (2, 3):
        for n in "qkvo":
            o[f"L{layer}x_w{n}T"] = turned(get(f"L{layer}_xattn_W{n}"))
            o[f"L{layer}x_b{n}"] = (row if n == "o" else col)(get(f"L{layer}_xattn_b{n}"))
        spread = np.zeros((16, 32, D), np.float32)
        spread[:, :16] = get(f"L{layer}_xattn_Wo").T.reshape(16, 16, D)
        o[f"L{layer}x_woT"] = chunks(spread.reshape(512, D))
        spread = np.zeros((16, 32), np.float32)
        spread[:, :16] = get(f"L{layer}_xattn_bv").reshape(16, 16)
        o[f"L{layer}x_bv"] = col(spread)
        odd = np.arange(P) // 16 % 2
        o[f"L{layer}x_halves"] = np.stack([(1 - odd) * 0.25, odd * 0.25], axis=1).astype(np.float32)
    swap = np.arange(D) // 16 * 16 + (np.arange(D) % 16 + 8) % 16
    for n in "qk":
        o[f"L2x_w{n}rT"] = turned(get(f"L2_xattn_W{n}")[swap])
        o[f"L2x_b{n}r"] = col(get(f"L2_xattn_b{n}")[swap])
    inv_freq = np.float32(1.0) / np.float32(10000.0) ** (np.arange(0, 16, 2, dtype=np.float32) / np.float32(16))
    freqs = np.arange(SK, dtype=np.float32)[None, :] * inv_freq[np.arange(P) % 8][:, None]
    sign = np.where(np.arange(P) % 16 < 8, -1.0, 1.0).astype(np.float32)
    o["L2x_cos"] = np.cos(freqs)
    o["L2x_sin"] = np.sin(freqs) * sign[:, None]
    o["L2f_gateT"], o["L2f_gate_bias"] = chunks(get("L2_ffn_Wg")), row(get("L2_ffn_bg"))
    o["L2f_ln_w"], o["L2f_b2"] = col(get("L2_ffn_ln_w")), get("L2_ffn_b2")
    per_expert = lambda a: np.ascontiguousarray(a.reshape(a.shape[0], a.shape[1] // P, P, a.shape[2]).transpose(0, 2, 1, 3))
    o["L2f_w1"], o["L2f_w3"] = per_expert(get("L2_ffn_W1a")), per_expert(get("L2_ffn_W1b"))
    o["L2f_w2"] = per_expert(get("L2_ffn_W2"))
    for n, what in (("b1", "b1a"), ("b3", "b1b")):
        o[f"L2f_{n}"] = np.ascontiguousarray(get(f"L2_ffn_{what}").reshape(8, 8, P).transpose(0, 2, 1))
    both = lambda a, b: np.concatenate([get(a), get(b)], axis=0)
    o["L3f_gateT"] = turned(both("L3_ffn_gate_weight", "L3_ffn_new_gate_weight"))
    o["L3f_gate_bias"] = row(np.concatenate([np.zeros(8, np.float32), get("L3_ffn_gate_bias")]))
    for n in ("w1", "w3"):
        o[f"L3f_{n}"] = per_expert(both(f"L3_ffn_{n}", f"L3_ffn_new_{n}").transpose(0, 2, 1))
    w2 = both("L3_ffn_w2", "L3_ffn_new_w2").transpose(0, 2, 1)
    padded = np.zeros((w2.shape[0], 6 * P, D), np.float32)
    padded[:, :w2.shape[1]] = w2
    o["L3f_w2"] = per_expert(padded)
    return {k: np.ascontiguousarray(a) for k, a in o.items()}


def kernel(**inputs):
    import concourse.bacc as bacc
    from concourse.bass_utils import run_bass_kernel_spmd

    nc = bacc.Bacc("TRN2", target_bir_lowering=False, num_devices=1)
    arrays = {f"in_{k}": a for k, a in host_layout(inputs).items()}
    dram = {k[3:]: nc.dram_tensor(k, a.shape, mybir.dt.from_np(a.dtype), kind="ExternalInput").ap()
            for k, a in arrays.items()}
    out = nc.dram_tensor("out_0", (B, S, D), F32, kind="ExternalOutput").ap()
    flamingo(nc, dram, out)
    result = run_bass_kernel_spmd(nc, [arrays], core_ids=[0])
    return result.results[0]["out_0"]
```
